# Optimizing a Trainium2 kernel written in Bass

```python
import numpy as np
import jax
import jax.numpy as jnp

def _softmax(x, axis=-1):
    return jax.nn.softmax(x, axis=axis)

def _gelu(x):
    return jax.nn.gelu(x, approximate=True)

def _silu(x):
    return jax.nn.silu(x)

def _sigmoid(x):
    return jax.nn.sigmoid(x)

def _layernorm(x, axis=-1, eps=1e-05):
    m = jnp.mean(x, axis=axis, keepdims=True)
    v = jnp.var(x, axis=axis, keepdims=True)
    return (x - m) / jnp.sqrt(v + eps)

def _scatter_add(tgt, idx, src, axis=0):
    return tgt.at[idx].add(src)

def _segment_sum(src, seg, n):
    return jax.ops.segment_sum(src, seg, n)
kernel_name = 'mk_early_fusion_d2_tok_img768_r4_cfbe97'

def setup_inputs(seed: int=0):
    np.random.seed(seed)
    _w = jnp.asarray

    def _rec_inputs():
        import jax
        import jax.numpy as jnp
        _rk = jax.random.key(seed)
        x = -0.000596345 + 1.00056 * jax.random.normal(jax.random.fold_in(_rk, 1), (4, 3, 64, 64), jnp.float32)
        txt = -0.000190561 + 0.886117 * jax.random.normal(jax.random.fold_in(_rk, 2), (4, 128, 192), jnp.float32)
        return (x, txt)
    x, txt = _rec_inputs()

    def _L0_tok_setup():
        import jax, jax.numpy as jnp
        import numpy as np
        B = 16
        IMG = 64
        CH = 3
        EMBED = 64
        GP = 16
        PRE = [1, 2, 4]
        N_LEVELS = 3
        FUSED = EMBED * N_LEVELS

        def hilbert_flat_indices(n):
            t = np.arange(n * n, dtype=np.int64)
            x = np.zeros(n * n, dtype=np.int64)
            y = np.zeros(n * n, dtype=np.int64)
            s = 1
            while s < n:
                rx = 1 & t // 2
                ry = 1 & (t ^ rx)
                swap = ry == 0
                flip = swap & (rx == 1)
                x = np.where(flip, s - 1 - x, x)
                y = np.where(flip, s - 1 - y, y)
                x2 = np.where(swap, y, x)
                y2 = np.where(swap, x, y)
                x, y = (x2, y2)
                x = x + s * rx
                y = y + s * ry
                t = t // 4
                s *= 2
            return y * n + x

        def _level(x, idx, W, b, p, gp):
            Bsz, C, H, _ = x.shape
            h = H // p
            t = x.reshape(Bsz, C, h, p, h, p).transpose(0, 2, 4, 3, 5, 1).reshape(Bsz, h * h, p * p * C)
            t = t[:, idx]
            t = t.reshape(Bsz, h * h // gp, gp * p * p * C)
            return t @ W.T + b

        def _interp_linear(x, n_out):
            L = x.shape[1]
            pos = (jnp.arange(n_out, dtype=jnp.float32) + 0.5) * (L / n_out) - 0.5
            pos = jnp.clip(pos, 0.0, L - 1)
            i0 = jnp.floor(pos).astype(jnp.int32)
            i1 = jnp.minimum(i0 + 1, L - 1)
            w = (pos - i0).astype(x.dtype)
            return x[:, i0] * (1.0 - w)[None, :, None] + x[:, i1] * w[None, :, None]
        key = jax.random.key(seed)
        ks = jax.random.split(key, 9)
        inp = {'x': jax.random.normal(ks[0], (B, CH, IMG, IMG), jnp.float32)}
        for i, p in enumerate(PRE):
            din = CH * p * p * GP
            inp[f'W{i}'] = jax.random.normal(ks[1 + 2 * i], (EMBED, din), jnp.float32) * din ** (-0.5)
            inp[f'b{i}'] = jax.random.normal(ks[2 + 2 * i], (EMBED,), jnp.float32) * 0.02
        inp['Wf'] = jax.random.normal(ks[7], (FUSED, FUSED), jnp.float32) * FUSED ** (-0.5)
        inp['bf'] = jax.random.normal(ks[8], (FUSED,), jnp.float32) * 0.02
        for i, p in enumerate(PRE):
            inp[f'idx{i}'] = jnp.asarray(hilbert_flat_indices(IMG // p), jnp.int32)
        return inp
    _L0_tok_all = _L0_tok_setup()
    _L0_tok_in = {k: v for k, v in _L0_tok_all.items() if k in ('W0', 'b0', 'W1', 'b1', 'W2', 'b2', 'Wf', 'bf', 'idx0', 'idx1', 'idx2')}
    del _L0_tok_all

    def _L0_attn_setup():
        import jax, jax.numpy as jnp
        import numpy as np
        N_HEAD = 12
        key = jax.random.key(seed)
        k1, k2, k3 = jax.random.split(key, 3)
        B, T, C = (8, 256, 192)
        x = jax.random.normal(k1, (B, T, C), dtype=jnp.float32)
        W_attn = jax.random.normal(k2, (C, 3 * C), dtype=jnp.float32) * 0.02
        b_attn = jax.random.normal(k3, (3 * C,), dtype=jnp.float32) * 0.02
        return {'x': x, 'W_attn': W_attn, 'b_attn': b_attn}
    _L0_attn_all = _L0_attn_setup()
    _L0_attn_in = {k: v for k, v in _L0_attn_all.items() if k in ('W_attn', 'b_attn')}
    del _L0_attn_all

    def _L0_ffn_setup():
        import jax, jax.numpy as jnp
        import numpy as np
        B, L, D = (4, 256, 192)
        E, S, H = (32, 32, 768)
        EPS = 1e-12

        def _l2norm(v, axis):
            n = jnp.sqrt(jnp.sum(v * v, axis=axis, keepdims=True))
            return v / jnp.maximum(n, EPS)
        key = jax.random.key(seed)
        ks = jax.random.split(key, 6)
        x = jax.random.normal(ks[0], (B, L, D), dtype=jnp.float32)
        phi = jax.random.normal(ks[1], (D, E, S), dtype=jnp.float32) / np.sqrt(D)
        scale = jnp.ones((1,), dtype=jnp.float32)
        w1 = jax.random.normal(ks[2], (E, D, H), dtype=jnp.float32) / np.sqrt(D)
        b1 = jax.random.normal(ks[3], (E, H), dtype=jnp.float32) * 0.01
        w2 = jax.random.normal(ks[4], (E, H, D), dtype=jnp.float32) / np.sqrt(H)
        b2 = jax.random.normal(ks[5], (E, D), dtype=jnp.float32) * 0.01
        return {'x': x, 'phi': phi, 'scale': scale, 'w1': w1, 'b1': b1, 'w2': w2, 'b2': b2}
    _L0_ffn_all = _L0_ffn_setup()
    _L0_ffn_in = {k: v for k, v in _L0_ffn_all.items() if k in ('phi', 'scale', 'w1', 'b1', 'w2', 'b2')}
    del _L0_ffn_all

    def _L1_attn_setup():
        import jax, jax.numpy as jnp
        import numpy as np
        EMBED_DIM = 192
        SEQ_LEN = 256
        BATCH = 32
        ALPHA = 0.99

        def _decay_mask(sl: int, alpha: float) -> jnp.ndarray:
            i = jnp.arange(sl, dtype=jnp.float32)
            diff = i[:, None] - i[None, :]
            return jnp.where(diff >= 0, jnp.float32(alpha) ** diff, 0.0)
        key = jax.random.key(seed)
        k1, k2 = jax.random.split(key)
        x = jax.random.normal(k1, (BATCH, SEQ_LEN, EMBED_DIM), dtype=jnp.float32)
        W_qkv = jax.random.normal(k2, (EMBED_DIM, 3 * EMBED_DIM), dtype=jnp.float32) * EMBED_DIM ** (-0.5)
        b_qkv = jnp.zeros((3 * EMBED_DIM,), dtype=jnp.float32)
        return {'x': x, 'W_qkv': W_qkv, 'b_qkv': b_qkv}
    _L1_attn_all = _L1_attn_setup()
    _L1_attn_in = {k: v for k, v in _L1_attn_all.items() if k in ('W_qkv', 'b_qkv')}
    del _L1_attn_all

    def _L1_ffn_setup():
        import jax, jax.numpy as jnp
        import numpy as np
        EPS = 1e-05

        def ter_quant(w):
            gamma = jnp.mean(jnp.abs(w)) + EPS
            wq = jnp.clip(jnp.round(w / gamma), -1.0, 1.0) * gamma
            return wq
        key = jax.random.key(seed)
        k_x, k_w1, k_w2 = jax.random.split(key, 3)
        B, S, D, H = (64, 197, 192, 768)
        x = jax.random.normal(k_x, (B, S, D), dtype=jnp.float32)
        w1 = jax.random.normal(k_w1, (H, D), dtype=jnp.float32) * (1.0 / np.sqrt(D))
        b1 = jnp.zeros((H,), dtype=jnp.float32)
        w2 = jax.random.normal(k_w2, (D, H), dtype=jnp.float32) * (1.0 / np.sqrt(H))
        b2 = jnp.zeros((D,), dtype=jnp.float32)
        return {'x': x, 'w1': w1, 'b1': b1, 'w2': w2, 'b2': b2}
    _L1_ffn_all = _L1_ffn_setup()
    _L1_ffn_in = {k: v for k, v in _L1_ffn_all.items() if k in ('w1', 'b1', 'w2', 'b2')}
    del _L1_ffn_all
    return {'x': x, 'txt': txt, 'L0_tok_W0': _L0_tok_in['W0'], 'L0_tok_b0': _L0_tok_in['b0'], 'L0_tok_W1': _L0_tok_in['W1'], 'L0_tok_b1': _L0_tok_in['b1'], 'L0_tok_W2': _L0_tok_in['W2'], 'L0_tok_b2': _L0_tok_in['b2'], 'L0_tok_Wf': _L0_tok_in['Wf'], 'L0_tok_bf': _L0_tok_in['bf'], 'L0_tok_idx0': _L0_tok_in['idx0'], 'L0_tok_idx1': _L0_tok_in['idx1'], 'L0_tok_idx2': _L0_tok_in['idx2'], 'L0_attn_W_attn': _L0_attn_in['W_attn'], 'L0_attn_b_attn': _L0_attn_in['b_attn'], 'L0_ffn_phi': _L0_ffn_in['phi'], 'L0_ffn_scale': _L0_ffn_in['scale'], 'L0_ffn_w1': _L0_ffn_in['w1'], 'L0_ffn_b1': _L0_ffn_in['b1'], 'L0_ffn_w2': _L0_ffn_in['w2'], 'L0_ffn_b2': _L0_ffn_in['b2'], 'L1_attn_W_qkv': _L1_attn_in['W_qkv'], 'L1_attn_b_qkv': _L1_attn_in['b_qkv'], 'L1_ffn_w1': _L1_ffn_in['w1'], 'L1_ffn_b1': _L1_ffn_in['b1'], 'L1_ffn_w2': _L1_ffn_in['w2'], 'L1_ffn_b2': _L1_ffn_in['b2']}

def reference(x, txt, L0_tok_W0, L0_tok_b0, L0_tok_W1, L0_tok_b1, L0_tok_W2, L0_tok_b2, L0_tok_Wf, L0_tok_bf, L0_tok_idx0, L0_tok_idx1, L0_tok_idx2, L0_attn_W_attn, L0_attn_b_attn, L0_ffn_phi, L0_ffn_scale, L0_ffn_w1, L0_ffn_b1, L0_ffn_w2, L0_ffn_b2, L1_attn_W_qkv, L1_attn_b_qkv, L1_ffn_w1, L1_ffn_b1, L1_ffn_w2, L1_ffn_b2):
    import jax
    import jax.numpy as jnp

    def _L0_tok_ref(x, W0, b0, W1, b1, W2, b2, Wf, bf, idx0, idx1, idx2):
        import jax, jax.numpy as jnp
        import numpy as np
        B = 16
        IMG = 64
        CH = 3
        EMBED = 64
        GP = 16
        PRE = [1, 2, 4]
        N_LEVELS = 3
        FUSED = EMBED * N_LEVELS

        def hilbert_flat_indices(n):
            t = np.arange(n * n, dtype=np.int64)
            x = np.zeros(n * n, dtype=np.int64)
            y = np.zeros(n * n, dtype=np.int64)
            s = 1
            while s < n:
                rx = 1 & t // 2
                ry = 1 & (t ^ rx)
                swap = ry == 0
                flip = swap & (rx == 1)
                x = np.where(flip, s - 1 - x, x)
                y = np.where(flip, s - 1 - y, y)
                x2 = np.where(swap, y, x)
                y2 = np.where(swap, x, y)
                x, y = (x2, y2)
                x = x + s * rx
                y = y + s * ry
                t = t // 4
                s *= 2
            return y * n + x

        def _level(x, idx, W, b, p, gp):
            Bsz, C, H, _ = x.shape
            h = H // p
            t = x.reshape(Bsz, C, h, p, h, p).transpose(0, 2, 4, 3, 5, 1).reshape(Bsz, h * h, p * p * C)
            t = t[:, idx]
            t = t.reshape(Bsz, h * h // gp, gp * p * p * C)
            return t @ W.T + b

        def _interp_linear(x, n_out):
            L = x.shape[1]
            pos = (jnp.arange(n_out, dtype=jnp.float32) + 0.5) * (L / n_out) - 0.5
            pos = jnp.clip(pos, 0.0, L - 1)
            i0 = jnp.floor(pos).astype(jnp.int32)
            i1 = jnp.minimum(i0 + 1, L - 1)
            w = (pos - i0).astype(x.dtype)
            return x[:, i0] * (1.0 - w)[None, :, None] + x[:, i1] * w[None, :, None]
        Ws = [(idx0, W0, b0, PRE[0]), (idx1, W1, b1, PRE[1]), (idx2, W2, b2, PRE[2])]
        outs = [_level(x, idx, W, b, p, GP) for idx, W, b, p in Ws]
        n_tokens = outs[0].shape[1]
        outs = [outs[0]] + [_interp_linear(o, n_tokens) for o in outs[1:]]
        y = jnp.concatenate(outs, axis=-1)
        return y @ Wf.T + bf

    def _L0_attn_ref(x, W_attn, b_attn):
        import jax, jax.numpy as jnp
        import numpy as np
        N_HEAD = 12
        B, T, C = x.shape
        H = N_HEAD
        hs = C // H
        scale = 1.0 / jnp.sqrt(jnp.asarray(hs, dtype=x.dtype))
        qkv = x @ W_attn + b_attn
        q, k, v = jnp.split(qkv, 3, axis=-1)
        q = q.reshape(B, T, H, hs).transpose(0, 2, 1, 3)
        k = k.reshape(B, T, H, hs).transpose(0, 2, 1, 3)
        v = v.reshape(B, T, H, hs).transpose(0, 2, 1, 3)
        scores = jnp.einsum('bhqd,bhkd->bhqk', q, k) * scale
        causal = jnp.tril(jnp.ones((T, T), dtype=bool))
        att = jnp.where(causal[None, None], jax.nn.relu(scores), jnp.zeros((), dtype=scores.dtype))
        out = jnp.einsum('bhqk,bhkd->bhqd', att, v)
        out = out.transpose(0, 2, 1, 3).reshape(B, T, C)
        return out

    def _L0_ffn_ref(x, phi, scale, w1, b1, w2, b2):
        import jax, jax.numpy as jnp
        import numpy as np
        B, L, D = (4, 256, 192)
        E, S, H = (32, 32, 768)
        EPS = 1e-12

        def _l2norm(v, axis):
            n = jnp.sqrt(jnp.sum(v * v, axis=axis, keepdims=True))
            return v / jnp.maximum(n, EPS)
        b, l, d = x.shape
        xn = _l2norm(x, axis=2)
        phin = scale * _l2norm(phi, axis=0)
        logits = jnp.einsum('bld,des->bles', xn, phin)
        d_w = jax.nn.softmax(logits, axis=-1)
        c_w = jax.nn.softmax(logits.reshape(b, l, E * S), axis=-1)
        slots = jnp.einsum('bld,bles->besd', xn, d_w)
        h = jax.nn.gelu(jnp.einsum('besd,edh->besh', slots, w1) + b1[:, None, :], approximate=False)
        eo = jnp.einsum('besh,ehd->besd', h, w2) + b2[:, None, :]
        eo = eo.reshape(b, E * S, d)
        return jnp.einsum('bkd,blk->bld', eo, c_w)

    def _L1_attn_ref(x, W_qkv, b_qkv):
        import jax, jax.numpy as jnp
        import numpy as np
        EMBED_DIM = 192
        SEQ_LEN = 256
        BATCH = 32
        ALPHA = 0.99

        def _decay_mask(sl: int, alpha: float) -> jnp.ndarray:
            i = jnp.arange(sl, dtype=jnp.float32)
            diff = i[:, None] - i[None, :]
            return jnp.where(diff >= 0, jnp.float32(alpha) ** diff, 0.0)
        bs, sl, d = x.shape
        qkv = x @ W_qkv + b_qkv
        q, k, v = jnp.split(qkv, 3, axis=-1)
        M = _decay_mask(sl, ALPHA)
        dim_sqrt = jnp.sqrt(jnp.float32(d))
        scores = jnp.einsum('bsd,btd->bst', q, k) / dim_sqrt * M
        return jnp.einsum('bst,btd->bsd', scores, v)

    def _L1_ffn_ref(x, w1, b1, w2, b2):
        import jax, jax.numpy as jnp
        import numpy as np
        EPS = 1e-05

        def ter_quant(w):
            gamma = jnp.mean(jnp.abs(w)) + EPS
            wq = jnp.clip(jnp.round(w / gamma), -1.0, 1.0) * gamma
            return wq
        h = jnp.einsum('bsd,hd->bsh', x, ter_quant(w1)) + b1
        h = jax.nn.gelu(h, approximate=False)
        y = jnp.einsum('bsh,dh->bsd', h, ter_quant(w2)) + b2
        return y
    h = _L0_tok_ref(x, L0_tok_W0, L0_tok_b0, L0_tok_W1, L0_tok_b1, L0_tok_W2, L0_tok_b2, L0_tok_Wf, L0_tok_bf, L0_tok_idx0, L0_tok_idx1, L0_tok_idx2)
    h = jnp.concatenate([h, txt], axis=1)
    h = h + _L0_attn_ref(_layernorm(h, axis=-1), L0_attn_W_attn, L0_attn_b_attn)
    h = h + _L0_ffn_ref(_layernorm(h, axis=-1), L0_ffn_phi, L0_ffn_scale, L0_ffn_w1, L0_ffn_b1, L0_ffn_w2, L0_ffn_b2)
    h = h + _L1_attn_ref(_layernorm(h, axis=-1), L1_attn_W_qkv, L1_attn_b_qkv)
    h = h + _L1_ffn_ref(_layernorm(h, axis=-1), L1_ffn_w1, L1_ffn_b1, L1_ffn_w2, L1_ffn_b2)
    return h

_drawn_inputs = setup_inputs


def setup_inputs(seed=0):
    import zlib

    import numpy as np

    out = dict(_drawn_inputs(seed))
    spreads = {'L1_attn_b_qkv': (0.0, 0.1), 'L1_ffn_b1': (0.0, 0.8), 'L1_ffn_b2': (0.0, 0.8)}
    factors = {'L0_ffn_phi': 64.0,
     'L0_ffn_b1': 25.055,
     'L0_ffn_b2': 8.0,
     'L1_ffn_w1': 4.268,
     'L1_ffn_w2': 3.655}
    for name, (base, spread) in spreads.items():
        noise = np.random.default_rng([zlib.crc32(name.encode()), seed]).standard_normal(out[name].shape)
        drawn = base * np.exp(spread * noise) if base else spread * noise
        out[name] = jnp.asarray(drawn.astype(out[name].dtype))
    for name, factor in factors.items():
        out[name] = (out[name] * factor).astype(out[name].dtype)
    return out
```

```python
from contextlib import ExitStack

import numpy as np

import concourse.bass as bass
from concourse import mybir

ALU = mybir.AluOpType
ACT = mybir.ActivationFunctionType
AX = mybir.AxisListType
F32 = mybir.dt.float32
BF16 = mybir.dt.bfloat16
I32 = mybir.dt.int32

P = 128
NB = 4
NT = 3
T = NT * P
D = 192
DC = 96
GP = 16
HEADS, HS = 12, 16
HG = 4
NG = HEADS // HG
NE, NS, HID = 32, 32, 768
NC = HID // P
KC = NE * NS // P
EPC = P // NS
RING = 4
LN_EPS, L2_EPS, TQ_EPS = 1e-5, 1e-12, 1e-5
ALPHA = 0.99
PRODUCTS = ((0, 0, 1, 3), (3, 0, 2, 3), (6, 0, 0, 2))


def steps():
    tok = [("phi",), ("ternary",), ("embed",)]
    a = []
    for b in range(2):
        a += [("stats", 0, b)]
    for b in range(2):
        a += [("norm", 0, b), ("turn", 0, b), ("qkv", b)]
    for b in range(NB):
        if b + 2 < NB:
            a += [("stats", 0, b + 2), ("norm", 0, b + 2)]
        a += [("attend", b)]
        if b + 2 < NB:
            a += [("turn", 0, b + 2), ("qkv", b + 2)]
        a += [("join", b)]
    m = [("stats", 1, 0), ("stats", 1, 1), ("norm", 1, 0), ("turn", 1, 0), ("logits", 0),
         ("norm", 1, 1), ("peak", 0), ("weigh", 0)]
    for u in range(NB * NT):
        b, t = divmod(u, NT)
        if u + 1 < NB * NT:
            if t == NT - 1:
                m += [("turn", 1, b + 1)]
            m += [("logits", u + 1)]
        m += [("slots", u)]
        if u + 1 < NB * NT:
            m += [("peak", u + 1), ("weigh", u + 1)]
        m += [("slots_out", u)]
        if t == 0 and 1 <= b <= NB - 2:
            m += [("stats", 1, b + 1), ("norm", 1, b + 1)]
    c = [("combine", 0), ("combine", 1), ("stats", 2, 0), ("combine", 2), ("norm", 2, 0), ("turn", 2, 0),
         ("qkv3", 0), ("stats", 2, 1), ("combine", 3), ("norm", 2, 1), ("turn", 2, 1), ("qkv3", 1),
         ("stats", 2, 2), ("norm", 2, 2), ("decay", 0), ("turn", 2, 2), ("qkv3", 2),
         ("stats", 2, 3), ("norm", 2, 3), ("stats", 3, 0), ("decay", 1), ("norm", 3, 0),
         ("turn", 2, 3), ("qkv3", 3), ("stats", 3, 1), ("decay", 2), ("turn", 3, 0), ("norm", 3, 1), ("ffn", 0),
         ("stats", 3, 2), ("decay", 3), ("turn", 3, 1), ("norm", 3, 2), ("ffn", 1),
         ("stats", 3, 3), ("turn", 3, 2), ("norm", 3, 3), ("ffn", 2), ("turn", 3, 3), ("ffn", 3)]
    return tok + a + m, c


def jobs_of(step):
    kind, *n = step
    n = tuple(n)
    if kind == "phi":
        return [("phi", 0), ("phi", 1)]
    if kind == "ternary":
        return [("gamma",)]
    if kind == "embed":
        return ([("f2",), ("o2",), ("z2", 0), ("z2", 1), ("f1",), ("o1",), ("z1", 0), ("z1", 1)]
                + [j for v in range(2) for j in (("f0", v), ("o0", v))]
                + [("y", b, v) for b in range(NB) for v in range(2)])
    if kind == "turn":
        return [("xT", *n, c) for c in range(2)]
    if kind in ("qkv", "qkv3"):
        return [(kind, *n, m) for m in range(4)] + [(kind + "_v", *n, t) for t in range(NT)]
    if kind == "attend":
        out = []
        for g in range(NG + 1):
            if g < NG:
                out += [(s, *n, h) for h in range(HG * g, HG * g + HG) for s in ("near", "far")]
            if g:
                out += [("mix", *n, g - 1)]
        return out
    if kind == "join":
        return [("join", *n, t) for t in range(NT)]
    if kind == "logits":
        return [("logits", *n, v) for v in range(2)]
    if kind == "slots":
        u, = n
        first = [("slots", u // NT, c, v) for c in range(2) for v in range(2)] if u % NT == 0 else []
        return first + [("cwT", u, v) for v in range(2)]
    if kind == "combine":
        return [("combine", *n, t) for t in range(NT)]
    if kind == "decay":
        return [("score", *n, 0), ("score", *n, 1)] + [("read", *n, t) for t in range(NT)]
    if kind == "ffn":
        return [("hidden", *n, m) for m in range(NC)] + [("down", *n, t) for t in range(NT)]
    return []


def plan_banks(before, after):
    fixed = {"logits": (0, 1), "cwT": (2, 3)}
    use, count, turn = {}, [0] * 8, 0
    for s in before + after:
        for j in jobs_of(s):
            if j[0] in fixed:
                bank = fixed[j[0]][j[-1]]
            elif j[0] == "slots":
                bank = 4 + 2 * j[2] + j[3]
            elif j[0] == "xT" and j[1] == 1:
                bank = 2 + j[3]
            else:
                bank, turn = turn % 8, turn + 1
            count[bank] += 1
            use[j] = (bank, count[bank])
    return use


def build(nc, x0, x1, x2, idx, txt, w0, w1t, w2t, wf, tok_b, bf, interp1, interp2, ident_in, causal_in,
          decay_in, wa, ba_qk, ba_v, phi_in, scale_in, ew1, eb1, ew2, eb2, wq, bq_qk, bq_v, fw1, fb1, fw2,
          fb2, out):
    before, after = steps()
    use = plan_banks(before, after)
    q_dram = nc.dram_tensor("q_parts", [NB, 2, 3, DC, T], BF16).ap()
    k_dram = nc.dram_tensor("k_parts", [NB, 2, 5, DC, T], BF16).ap()

    with ExitStack() as ctx:
        def sb(name, shape, dt=F32):
            return ctx.enter_context(nc.sbuf_tensor(name, shape, dt))

        def sem(name):
            return ctx.enter_context(nc.semaphore(name))

        h = sb("h", [P, NB, NT, D])
        ident = sb("ident", [P, P])
        causal = sb("causal", [P, NT, P])
        decay = sb("decay", [P, T])
        ones = sb("ones", [P, P])
        bias_row = sb("bias_row", [P, 4, D])
        bias_col = sb("bias_col", [P, 24])
        tokb_c, baqk_c, bqqk_c, fb1_c = (bias_col[:, 0:3], bias_col[:, 3:7], bias_col[:, 7:11],
                                         bias_col[:, 11:17])
        scale_c = bias_col[:, 17:18]
        xn = sb("xn", [P, 2, NT, D])
        xT = sb("xT", [DC, 2, 2, T])
        st6 = sb("st6", [P, NT, 6])
        mv = sb("mv", [P, 2, NT, 2])
        rstd = sb("rstd", [P, 2, NT])
        veps = sb("veps", [P, NT])
        ssq = sb("ssq", [P, 2, NT])
        rl2 = sb("rl2", [P, 2, NT])
        mhalf = sb("mhalf", [P, NT])
        sm = sb("sm", [P, 2, 6, NE])
        tot = sb("tot", [P, 2, 3])
        tern1 = sb("tern1", [DC, 2, HID])
        tern2 = sb("tern2", [P, NC, D])
        gsum = sb("gsum", [P, 2])
        gamma = sb("gamma", [P, 2])
        half = sb("half", [P, 2])
        nhalf = sb("nhalf", [P, 2])
        wq_s = sb("wq_s", [DC, 2, 3 * D])

        A_WORDS = 26624
        arena = sb("arena", [P, A_WORDS])

        def cut(region, at, shape, dt=F32, parts=P):
            n = int(np.prod(shape))
            words = n if dt == F32 else n // 2
            v = region[0:parts, at:at + words]
            if dt != F32:
                v = v.bitcast(dt)
            names = "abcde"[:len(shape)]
            if len(shape) > 1:
                v = v.rearrange(f"p ({' '.join(names)}) -> p {' '.join(names)}",
                                **{k: s for k, s in zip(names, shape)})
            return v, at + words

        at = 0
        qs, at = cut(arena, at, [2, HEADS, T], BF16)
        ks, at = cut(arena, at, [2, HEADS, T], BF16)
        att, at = cut(arena, at, [2 * HG, 2, T])
        parts, at = cut(arena, at, [2, 4, 3, T], BF16, DC)
        resid, at = cut(arena, at, [2, T], F32, DC)
        vpad, at = cut(arena, at, [2, NT, HEADS, 2 * HS])
        oT, at = cut(arena, at, [NG, T])
        wa_s, at = cut(arena, at, [2, 3 * D], F32, DC)
        at = 0
        slotsT, at = cut(arena, at, [2, NE, NB, NS], F32, DC + 1)
        cwT, at = cut(arena, at, [NB, KC, T])
        e_at = at
        ex, at = cut(arena, at, [2, NE, NS])
        dw, at = cut(arena, at, [2, NE, NS])
        cw, at = cut(arena, at, [2, NE, NS])
        assert at <= A_WORDS
        eok, at = cut(arena, e_at, [KC, NB, D])
        phi = sb("phi", [DC, 2, NE * NS])

        R_WORDS = RING * (2 * HID + NC * D + D)
        ring = sb("ring", [P, R_WORDS])
        at = 0
        ew1_s, at = cut(ring, at, [RING, 2, HID], F32, DC + 1)
        ew2_s, at = cut(ring, at, [RING, NC, D])
        eb2_s, at = cut(ring, at, [RING, D])
        at = 0
        g0, at = cut(ring, at, [2, GP, NB, 3])
        g1, at = cut(ring, at, [8, NB, 12])
        g2, at = cut(ring, at, [2, NB, 48])
        r0, at = cut(ring, at, [2, NB, GP, 3])
        r1, at = cut(ring, at, [NB, 8, 12])
        r2, at = cut(ring, at, [NB, 2, 48])
        f0, at = cut(ring, at, [2, NB * P], F32, 48)
        f1, at = cut(ring, at, [NB, 2, 64], F32, DC)
        f2, at = cut(ring, at, [NB, 8, 16], F32, DC)
        o0, at = cut(ring, at, [2, NB, P], F32, 64)
        o1, at = cut(ring, at, [NB, 64], F32, 64)
        o2, at = cut(ring, at, [NB, 16], F32, 64)
        z1, at = cut(ring, at, [NB, D], F32, 64)
        z2, at = cut(ring, at, [NB, D], F32, 16)
        w0_s, at = cut(ring, at, [64], F32, 48)
        w1_s, at = cut(ring, at, [2, 64], F32, DC)
        w2_s, at = cut(ring, at, [8, 64], F32, DC)
        wf_s, at = cut(ring, at, [3, D], F32, 64)
        i1_s, at = cut(ring, at, [256], F32, 64)
        i2_s, at = cut(ring, at, [256], F32, 16)
        idx_s = sb("idx_s", [P, 42], I32)
        assert at <= R_WORDS
        at = 0
        sq, at = cut(arena, at, [2, NE * NS], F32, DC)
        ss, at = cut(arena, at, [NE * NS], F32, DC)
        rt, at = cut(arena, at, [NE * NS], F32, DC)
        nw, at = cut(arena, at, [NE * NS], F32, DC)
        fw1_s, at = cut(arena, at, [2, HID], F32, DC)
        fw2_s, at = cut(arena, at, [NC, D])
        neg1, at = cut(arena, at, [2, HID], F32, DC)
        neg2, at = cut(arena, at, [NC, D])
        assert at <= 18432
        at = 0
        qk3, at = cut(ring, at, [2, 4, T], F32, DC)
        v3, at = cut(ring, at, [2, NT, D])
        sc3, at = cut(ring, at, [2, 2, T])
        hid, at = cut(ring, at, [2, NC, T])
        assert at <= R_WORDS
        hT = sb("hT", [P, 2, NC * P])
        squares = hT[:, 0, 0:NT * D].rearrange("p (t d) -> p t d", t=NT)
        y_out, at = cut(arena, 0, [NB, NT, D])

        ps = [ctx.enter_context(nc.psum_tensor(f"ps{k}", [P, 512], F32)) for k in range(8)]

        bank_full = [sem(f"bank_full{k}") for k in range(8)]
        bank_drained = [sem(f"bank_drained{k}") for k in range(8)]
        idx_in, tok_in, txt_in, phi_in_s, tern_in, attn_in, layer1_in = (
            sem(n) for n in ("idx_in", "tok_in", "txt_in", "phi_in", "tern_in", "attn_in", "layer1_in"))
        gathered = [sem(f"gathered{n}") for n in range(3)]
        regrouped = sem("regrouped")
        cleared = sem("cleared")
        phi_sq, phi_ss, phi_root, phi_ready = (sem(n) for n in ("phi_sq", "phi_ss", "phi_root", "phi_ready"))
        abs_sums = sem("abs_sums")
        dve_chain, pool_chain = sem("dve_chain"), sem("pool_chain")
        stats_ready, rstd_ready, xn_ready, l2_sums, rl2_ready = (
            sem(n) for n in ("stats_ready", "rstd_ready", "xn_ready", "l2_sums", "rl2_ready"))
        part1_ready, resid_ready, part2_ready, parts_ready = (
            sem(n) for n in ("part1_ready", "resid_ready", "part2_ready", "parts_ready"))
        parts_out = sem("parts_out")
        stacks_in = [sem("stacks_in0"), sem("stacks_in1")]
        shifted, exps_ready, rsum_ready, share_ready, dw_ready, cw_ready = (
            sem(n) for n in ("shifted", "exps_ready", "rsum_ready", "share_ready", "dw_ready", "cw_ready"))
        ones_row = sem("ones_row")
        landed = [sem(f"weights_landed{j}") for j in range(RING)]
        slot_free = [sem(f"weights_free{j}") for j in range(RING)]
        hid_full, hid_done, eo_full, eo_drained = (sem(n) for n in ("hid_full", "hid_done", "eo_full", "eo_drained"))
        out_ready, stored = sem("out_ready"), sem("stored")

        def refill(pe, job):
            bank, n = use[job]
            if n > 1:
                pe.wait_ge(bank_drained[bank], n - 1)
            return ps[bank]

        def filled(inst, job):
            inst.then_inc(bank_full[use[job][0]], 1)

        def await_fill(eng, job):
            bank, n = use[job]
            eng.wait_ge(bank_full[bank], n)
            return ps[bank]

        def drained(inst, job):
            inst.then_inc(bank_drained[use[job][0]], 1)

        def await_drain(eng, job):
            bank, n = use[job]
            eng.wait_ge(bank_drained[bank], n)

        def chunked(w, rows=DC):
            return w.rearrange("(c p) n -> p c n", p=rows)

        block = ctx.enter_context(nc.Block())

        @block.sync
        def _(sp):
            sp.dma_start(idx_s[:, :], idx).then_inc(idx_in, 16)
            sp.dma_start(phi[:, :, :], chunked(phi_in)).then_inc(phi_in_s, 16)
            sp.dma_start(scale_c[:, :], scale_in.partition_broadcast(P)).then_inc(phi_in_s, 16)
            sp.dma_start(fw1_s, chunked(fw1)).then_inc(tern_in, 16)
            sp.dma_start(fw2_s, fw2.rearrange("(c p) n -> p c n", p=P)).then_inc(tern_in, 16)
            sp.dma_start(ident[:, :], ident_in).then_inc(tok_in, 16)
            sp.dma_start(w0_s, w0).then_inc(tok_in, 16)
            sp.dma_start(w1_s, chunked(w1t)).then_inc(tok_in, 16)
            sp.dma_start(w2_s, chunked(w2t)).then_inc(tok_in, 16)
            sp.dma_start(wf_s, chunked(wf, 64)).then_inc(tok_in, 16)
            sp.dma_start(i1_s, interp1).then_inc(tok_in, 16)
            sp.dma_start(i2_s, interp2).then_inc(tok_in, 16)
            sp.dma_start(tokb_c[0:64, :], tok_b).then_inc(tok_in, 16)
            sp.dma_start(bias_row[:, 1, :], bf.partition_broadcast(P)).then_inc(tok_in, 16)
            sp.dma_start(h[:, :, NT - 1, :], txt.rearrange("b t d -> t b d")).then_inc(txt_in, 16)
            sp.dma_start(wa_s, chunked(wa)).then_inc(attn_in, 16)
            sp.dma_start(baqk_c[0:DC, :], ba_qk).then_inc(attn_in, 16)
            sp.dma_start(bias_row[:, 0, :], ba_v.partition_broadcast(P)).then_inc(attn_in, 16)
            sp.dma_start(causal[:, :, :], causal_in).then_inc(attn_in, 16)
            sp.dma_start(wq_s[:, :, :], chunked(wq)).then_inc(layer1_in, 16)
            sp.dma_start(bqqk_c[0:DC, :], bq_qk).then_inc(layer1_in, 16)
            sp.dma_start(bias_row[:, 2, :], bq_v.partition_broadcast(P)).then_inc(layer1_in, 16)
            sp.dma_start(bias_row[:, 3, :], fb2.partition_broadcast(P)).then_inc(layer1_in, 16)
            sp.dma_start(fb1_c[:, :], fb1).then_inc(layer1_in, 16)
            sp.dma_start(decay[:, :], decay_in).then_inc(layer1_in, 16)

            def load_expert(e, j):
                sp.dma_start(ew1_s[0:DC, j, :, :], ew1[bass.ds(e, 1)].rearrange("e (c p) n -> p (e c) n", p=DC)
                             ).then_inc(landed[j], 16)
                sp.dma_start(ew1_s[DC:DC + 1, j, 1, :], eb1[bass.ds(e, 1), :]).then_inc(landed[j], 16)
                sp.dma_start(ew2_s[:, j, :, :], ew2[bass.ds(e, 1)].rearrange("e (c p) n -> p (e c) n", p=P)
                             ).then_inc(landed[j], 16)
                sp.dma_start(eb2_s[:, j, :], eb2[bass.ds(e, 1), :].partition_broadcast(P)
                             ).then_inc(landed[j], 16)

            await_drain(sp, ("y", NB - 1, 1))
            for b in range(NB):
                sp.wait_ge(parts_ready, 4 * b + 2)
                sp.dma_start(q_dram[b].rearrange("m s p t -> p (m s) t"),
                             parts[:, b % 2, 0:2, :, :].rearrange("p m s t -> p (m s) t")).then_inc(parts_out, 16)
                for m in range(2):
                    sp.wait_ge(parts_ready, 4 * b + 3 + m)
                    for to, n in ((0, 3), (3, 2)):
                        sp.dma_start(k_dram[b, m, to:to + n].rearrange("s p t -> p s t"),
                                     parts[:, b % 2, 2 + m, 0:n, :]).then_inc(parts_out, 16)
                sp.wait_ge(parts_out, 80 * (b + 1))
                if b >= 2:
                    await_fill(sp, ("far", b - 2, HEADS - 1))
                for slot, qp, kp, n in PRODUCTS:
                    for to, dram, part in ((qs, q_dram, qp), (ks, k_dram, kp)):
                        for m in range(2):
                            sp.dma_start(
                                to[HS * slot:HS * (slot + n), b % 2, 6 * m:6 * m + 6, :],
                                dram[b, m, part:part + n].rearrange("s (d h) t -> (s d) h t", d=HS),
                            ).then_inc(stacks_in[b % 2], 16)
                if b == 0:
                    for j in range(RING):
                        load_expert(j, j)
            with sp.Fori(1, NE // RING) as it:
                for j in range(RING):
                    sp.wait_ge(slot_free[j], it)
                    load_expert(it * RING + j, j)
            for b in range(NB):
                sp.wait_ge(out_ready, NT * (b + 1))
                sp.dma_start(out[b].rearrange("(t p) d -> p t d", p=P), y_out[:, b, :, :]).then_inc(stored, 16)
            sp.wait_ge(stored, 16 * NB)

        @block.gpsimd
        def _(pool):
            chain = [0]

            def link(inst):
                chain[0] += 1
                inst.then_inc(pool_chain, 1)
                pool.wait_ge(pool_chain, chain[0])

            pool.memset(ones[:, :], 1.0).then_inc(cleared, 1)
            pool.memset(mhalf[:, :], -0.5).then_inc(cleared, 1)
            pool.wait_ge(idx_in, 16)
            for j in range(2):
                pool.indirect_dma_start(g2[:, j, :, :].rearrange("p b f -> p (b f)"), None, x2,
                                        bass.IndirectOffsetOnAxis(ap=idx_s[:, 40 + j:41 + j], axis=0)
                                        ).then_inc(gathered[2], 16)
            for j in range(8):
                pool.indirect_dma_start(g1[:, j, :, :].rearrange("p b f -> p (b f)"), None, x1,
                                        bass.IndirectOffsetOnAxis(ap=idx_s[:, 32 + j:33 + j], axis=0)
                                        ).then_inc(gathered[1], 16)
            for j in range(32):
                pool.indirect_dma_start(g0[:, j // GP, j % GP, :, :].rearrange("p b f -> p (b f)"), None, x0,
                                        bass.IndirectOffsetOnAxis(ap=idx_s[:, j:j + 1], axis=0)
                                        ).then_inc(gathered[0], 16)
            pool.memset(vpad[:, :, :, :, :], 0.0).then_inc(cleared, 1)

            stats_seen, l2_seen = [0], [0]

            def do_norm(layer, b):
                stats_seen[0] += 1
                pool.wait_ge(stats_ready, NT * stats_seen[0])
                link(pool.tensor_scalar(veps[:, :], mv[:, b % 2, :, 1], LN_EPS, None, ALU.add))
                pool.tensor_tensor(rstd[:, b % 2, :], veps[:, :], mhalf[:, :], ALU.pow).then_inc(rstd_ready, 1)
                if layer == 1:
                    l2_seen[0] += 1
                    pool.wait_ge(l2_sums, NT * l2_seen[0])
                    link(pool.tensor_scalar(ssq[:, b % 2, :], ssq[:, b % 2, :], L2_EPS * L2_EPS, None, ALU.max))
                    pool.tensor_tensor(rl2[:, b % 2, :], ssq[:, b % 2, :], mhalf[:, :], ALU.pow
                                       ).then_inc(rl2_ready, 1)

            def do_qkv(b):
                for m in range(4):
                    n = 4 * b + m
                    pool.wait_ge(part2_ready, n + 1)
                    pool.tensor_tensor(parts[:, b % 2, m, 2, :], resid[:, m % 2, :], parts[:, b % 2, m, 1, :],
                                       ALU.subtract).then_inc(parts_ready, 1)

            def do_weigh(u):
                if u == 0:
                    pool.wait_ge(rl2_ready, l2_seen[0])
                    pool.memset(slotsT[DC:DC + 1, 1, :, :, :], 1.0).then_inc(ones_row, 1)
                    pool.wait_ge(ones_row, 1)
                pool.wait_ge(rsum_ready, u + 1)
                if u >= 2:
                    await_fill(pool, ("cwT", u - 2, 1))
                pool.tensor_tensor(dw[:, u % 2, :, :], ex[:, u % 2, :, :],
                                   sm[:, u % 2, 3, :].unsqueeze(2).to_broadcast([P, NE, NS]), ALU.mult
                                   ).then_inc(dw_ready, 1)
                pool.wait_ge(share_ready, u + 1)
                pool.tensor_tensor(cw[:, u % 2, :, :], ex[:, u % 2, :, :],
                                   sm[:, u % 2, 5, :].unsqueeze(2).to_broadcast([P, NE, NS]), ALU.mult
                                   ).then_inc(cw_ready, 1)

            for s in before + after:
                f = {"norm": do_norm, "qkv": do_qkv, "weigh": do_weigh}.get(s[0])
                if f:
                    f(*s[1:])

        @block.scalar
        def _(act):
            def do_phi():
                act.wait_ge(phi_in_s, 32)
                act.activation(sq, phi[:, :, :], ACT.Square).then_inc(phi_sq, 1)
                act.wait_ge(phi_ss, 2)
                act.activation(rt, ss, ACT.Sqrt).then_inc(phi_root, 1)

            def do_embed():
                act.wait_ge(tok_in, 16 * 9)
                p = await_fill(act, ("o2",))
                drained(act.activation(o2, p[0:64, 0:64].rearrange("e (b n) -> e b n", b=NB), ACT.Identity,
                                       bias=tokb_c[0:64, 2:3]), ("o2",))
                for v in range(2):
                    p = await_fill(act, ("z2", v))
                    drained(act.copy(z2[:, 2 * v:2 * v + 2, :], p[0:16, 0:2 * D].rearrange("n (b d) -> n b d", b=2)),
                            ("z2", v))
                p = await_fill(act, ("o1",))
                drained(act.activation(o1, p[0:64, 0:256].rearrange("e (b n) -> e b n", b=NB), ACT.Identity,
                                       bias=tokb_c[0:64, 1:2]), ("o1",))
                for v in range(2):
                    p = await_fill(act, ("z1", v))
                    drained(act.copy(z1[:, 2 * v:2 * v + 2, :], p[0:64, 0:2 * D].rearrange("n (b d) -> n b d", b=2)),
                            ("z1", v))
                for v in range(2):
                    p = await_fill(act, ("o0", v))
                    drained(act.activation(o0[:, v, :, :], p[0:64, :].rearrange("e (b n) -> e b n", b=NB),
                                           ACT.Identity, bias=tokb_c[0:64, 0:1]), ("o0", v))

            def do_turn(layer, b):
                job = ("xT", layer, b, 0)
                p = await_fill(act, job)
                drained(act.copy(xT[:, b % 2, 0, :], p[0:DC, 0:T]), job)

            def part2(b, m):
                act.wait_ge(resid_ready, 4 * b + m + 1)
                act.copy(parts[:, b % 2, m, 1, :], resid[:, m % 2, :]).then_inc(part2_ready, 1)

            def do_qkv(b):
                act.wait_ge(attn_in, 64)
                for m in range(4):
                    p = await_fill(act, ("qkv", b, m))
                    if b >= 2 and m == 0:
                        act.wait_ge(parts_out, 80 * (b - 1))
                    act.activation(parts[:, b % 2, m, 0, :], p[0:DC, 0:T], ACT.Identity,
                                   bias=baqk_c[0:DC, m:m + 1]).then_inc(part1_ready, 1)
                    if m:
                        part2(b, m - 1)
                part2(b, 3)

            def do_attend(b):
                for g in range(NG + 1):
                    if g < NG:
                        for hd in range(HG * g, HG * g + HG):
                            p = await_fill(act, ("far", b, hd))
                            drained(act.activation(att[:, hd % (2 * HG), 1, :], p[:, 0:T], ACT.Relu,
                                                   scale=float(HS) ** -0.5), ("far", b, hd))
                    if g:
                        p = await_fill(act, ("mix", b, g - 1))
                        if g == 1 and b:
                            await_fill(act, ("join", b - 1, NT - 1))
                        drained(act.copy(oT[:, g - 1, :], p[:, 0:T]), ("mix", b, g - 1))

            def do_weigh(u):
                act.wait_ge(shifted, u + 1)
                act.activation(sm[:, u % 2, 1, :], sm[:, u % 2, 0, :], ACT.Exp, bias=tot[:, u % 2, 0:1]
                               ).then_inc(exps_ready, 1)
                act.activation(ex[:, u % 2, :, :], ex[:, u % 2, :, :], ACT.Exp).then_inc(exps_ready, 1)

            def do_slots_out(u):
                b, t = divmod(u, NT)
                p = await_fill(act, ("cwT", u, 0))
                drained(act.copy(cwT[:, b, 0:4, P * t:P * t + P], p[:, :].rearrange("p (k n) -> p k n", k=4)),
                        ("cwT", u, 0))
                if t == NT - 1:
                    for v in range(2):
                        job = ("slots", b, 0, v)
                        p = await_fill(act, job)
                        drained(act.copy(slotsT[0:DC, 0, 16 * v:16 * v + 16, b, :],
                                         p[0:DC, :].rearrange("p (e s) -> p e s", s=NS)), job)

            def do_experts():
                def gelu(e, j):
                    act.wait_ge(hid_full, e + 1)
                    act.activation(hT[:, j % 2, 0:T], ps[2 * (j % 2)][:, 0:T], ACT.Gelu)
                    act.activation(hT[:, j % 2, T:2 * T], ps[2 * (j % 2) + 1][:, 0:T], ACT.Gelu).then_inc(hid_done, 1)

                with act.Fori(0, NE // RING) as it:
                    for j in range(RING):
                        gelu(it * RING + j, j)

            def do_qkv3(b):
                act.wait_ge(layer1_in, 96)
                for m in range(4):
                    p = await_fill(act, ("qkv3", b, m))
                    drained(act.activation(qk3[:, b % 2, m, :], p[0:DC, 0:T], ACT.Identity,
                                           bias=bqqk_c[0:DC, m:m + 1]), ("qkv3", b, m))

            def do_ffn(b):
                for m in range(NC):
                    p = await_fill(act, ("hidden", b, m))
                    drained(act.activation(hid[:, b % 2, m, :], p[:, 0:T], ACT.Gelu, bias=fb1_c[:, m:m + 1],
                                           scale=gamma[:, 0:1]), ("hidden", b, m))

            table = {"phi": do_phi, "embed": do_embed, "turn": do_turn, "qkv": do_qkv, "attend": do_attend,
                     "weigh": do_weigh, "slots_out": do_slots_out, "qkv3": do_qkv3, "ffn": do_ffn}
            for s in before:
                if s[0] in table:
                    table[s[0]](*s[1:])
            do_experts()
            for s in after:
                if s[0] in table:
                    table[s[0]](*s[1:])

        @block.vector
        def _(dve):
            chain = [0]

            def link(inst):
                chain[0] += 1
                inst.then_inc(dve_chain, 1)
                return chain[0]

            def settle(n=None):
                dve.wait_ge(dve_chain, n or chain[0])

            def do_phi():
                for v in range(2):
                    p = await_fill(dve, ("phi", v))
                    inst = dve.tensor_scalar(ss[:, 512 * v:512 * v + 512], p[0:DC, :], L2_EPS * L2_EPS, None, ALU.max)
                    drained(inst, ("phi", v))
                for v in range(2):
                    await_drain(dve, ("phi", v))
                dve.nop().then_inc(phi_ss, 2)
                dve.wait_ge(phi_root, 1)
                link(dve.reciprocal(rt, rt))
                settle()
                link(dve.tensor_tensor(nw, rt, rt, ALU.mult))
                settle()
                link(dve.tensor_tensor(nw, nw, ss, ALU.mult))
                settle()
                link(dve.tensor_scalar(nw, nw, -0.5, 1.5, ALU.mult, ALU.add))
                settle()
                link(dve.scalar_tensor_tensor(out=nw, in0=rt, scalar=scale_c[0:DC, :], in1=nw,
                                              op0=ALU.mult, op1=ALU.mult))
                settle()
                for c in range(2):
                    dve.tensor_tensor(phi[:, c, :], phi[:, c, :], nw, ALU.mult).then_inc(phi_ready, 1)

            def do_ternary():
                dve.wait_ge(tern_in, 32)
                dve.tensor_reduce(gsum[0:DC, 0:1], fw1_s, AX.XY, ALU.add, apply_absolute_value=True
                                  ).then_inc(abs_sums, 1)
                dve.tensor_reduce(gsum[:, 1:2], fw2_s, AX.XY, ALU.add, apply_absolute_value=True
                                  ).then_inc(abs_sums, 1)
                p = await_fill(dve, ("gamma",))
                drained(dve.tensor_scalar(gamma[:, :], p[:, 0:2], 1.0 / (D * HID), TQ_EPS, ALU.mult, ALU.add),
                        ("gamma",))
                await_drain(dve, ("gamma",))
                link(dve.tensor_scalar(half[:, :], gamma[:, :], 0.5, None, ALU.mult))
                link(dve.tensor_scalar(nhalf[:, :], gamma[:, :], -0.5, None, ALU.mult))
                settle()
                link(dve.tensor_scalar(neg1, fw1_s, nhalf[0:DC, 0:1], None, ALU.is_lt))
                link(dve.tensor_scalar(neg2, fw2_s, nhalf[:, 1:2], None, ALU.is_lt))
                settle()
                link(dve.scalar_tensor_tensor(out=tern1[:, :, :], in0=fw1_s, scalar=half[0:DC, 0:1], in1=neg1,
                                              op0=ALU.is_gt, op1=ALU.subtract))
                link(dve.scalar_tensor_tensor(out=tern2[:, :, :], in0=fw2_s, scalar=half[:, 1:2], in1=neg2,
                                              op0=ALU.is_gt, op1=ALU.subtract))
                settle()

            def do_embed():
                dve.wait_ge(gathered[2], 32)
                dve.tensor_copy(r2.rearrange("p b j f -> p j b f"), g2).then_inc(regrouped, 1)
                p = await_fill(dve, ("f2",))
                drained(dve.tensor_copy(f2, p[0:DC, :].rearrange("f (b g n) -> f b g n", b=NB, g=8)), ("f2",))
                dve.wait_ge(gathered[1], 128)
                dve.tensor_copy(r1.rearrange("p b j f -> p j b f"), g1).then_inc(regrouped, 1)
                p = await_fill(dve, ("f1",))
                drained(dve.tensor_copy(f1, p[0:DC, :].rearrange("f (b g n) -> f b g n", b=NB, g=2)), ("f1",))
                dve.wait_ge(gathered[0], 512)
                for v in range(2):
                    dve.tensor_copy(r0[:, v, :, :, :].rearrange("p b j f -> p j b f"), g0[:, v, :, :, :]
                                    ).then_inc(regrouped, 1)
                for v in range(2):
                    p = await_fill(dve, ("f0", v))
                    drained(dve.tensor_copy(f0[:, v, :], p[0:48, :]), ("f0", v))
                for b in range(NB):
                    for v in range(2):
                        p = await_fill(dve, ("y", b, v))
                        drained(dve.tensor_tensor(h[:, b, v, :], p[:, 0:D], bias_row[:, 1, :], ALU.add), ("y", b, v))

            stat_calls = [0]

            def do_stats(layer, b):
                if stat_calls[0]:
                    dve.wait_ge(stats_ready, NT * stat_calls[0])
                stat_calls[0] += 1
                if layer == 0:
                    dve.wait_ge(txt_in, 16)
                    for v in range(2):
                        await_drain(dve, ("y", b, v))
                else:
                    kind = {1: "join", 2: "combine", 3: "read"}[layer]
                    for t in range(NT):
                        await_drain(dve, (kind, b, t))
                for t in range(NT):
                    link(dve.bn_stats(st6[:, t, :], h[:, b, t, :]))
                settle()
                for t in range(NT):
                    dve.bn_aggr(mv[:, b % 2, t, :], st6[:, t, :]).then_inc(stats_ready, 1)

            norms, l2s = [0], [0]

            def do_norm(layer, b):
                norms[0] += 1
                dve.wait_ge(rstd_ready, norms[0])
                for t in range(NT):
                    inst = dve.tensor_scalar(xn[:, b % 2, t, :], h[:, b, t, :], mv[:, b % 2, t, 0:1],
                                             rstd[:, b % 2, t:t + 1], ALU.subtract, ALU.mult)
                    if layer != 1:
                        inst.then_inc(xn_ready, 1)
                    else:
                        link(inst)
                if layer == 1:
                    if l2s[0]:
                        dve.wait_ge(l2_sums, NT * l2s[0])
                    l2s[0] += 1
                    settle()
                    for t in range(NT):
                        dve.tensor_tensor_reduce(squares[:, t, :], xn[:, b % 2, t, :], xn[:, b % 2, t, :], 1.0, 0.0,
                                                 ALU.mult, ALU.add, ssq[:, b % 2, t:t + 1]).then_inc(l2_sums, 1)
                    dve.wait_ge(rl2_ready, l2s[0])
                    for t in range(NT):
                        dve.tensor_scalar(xn[:, b % 2, t, :], xn[:, b % 2, t, :], rl2[:, b % 2, t:t + 1], None,
                                          ALU.mult).then_inc(xn_ready, 1)

            def do_turn(layer, b):
                job = ("xT", layer, b, 1)
                p = await_fill(dve, job)
                drained(dve.tensor_copy(xT[:, b % 2, 1, :], p[0:DC, 0:T]), job)

            def do_qkv(b):
                dve.wait_ge(attn_in, 64)
                for m in range(4):
                    n = 4 * b + m
                    job = ("qkv", b, m)
                    p = await_fill(dve, job)
                    dve.wait_ge(part1_ready, n + 1)
                    if n >= 2:
                        dve.wait_ge(parts_ready, n - 1)
                    inst = dve.scalar_tensor_tensor(out=resid[:, m % 2, :], in0=p[0:DC, 0:T],
                                                    scalar=baqk_c[0:DC, m:m + 1], in1=parts[:, b % 2, m, 0, :],
                                                    op0=ALU.add, op1=ALU.subtract)
                    drained(inst, job)
                    await_drain(dve, job)
                    dve.nop().then_inc(resid_ready, 1)
                if b == 0:
                    dve.wait_ge(cleared, 3)
                for t in range(NT):
                    job = ("qkv_v", b, t)
                    p = await_fill(dve, job)
                    drained(dve.tensor_tensor(vpad[:, b % 2, t, :, 0:HS],
                                              p[:, 0:D].rearrange("p (h d) -> p h d", d=HS),
                                              bias_row[:, 0, :].rearrange("p (h d) -> p h d", d=HS), ALU.add), job)

            def do_attend(b):
                for hd in range(HEADS):
                    job = ("near", b, hd)
                    p = await_fill(dve, job)
                    drained(dve.scalar_tensor_tensor(out=att[:, hd % (2 * HG), 0, :], in0=p[:, 0:T], scalar=0.0,
                                                     in1=causal[:, :, :].rearrange("p a q -> p (a q)"),
                                                     op0=ALU.max, op1=ALU.mult), job)

            def do_join(b):
                for t in range(NT):
                    job = ("join", b, t)
                    p = await_fill(dve, job)
                    hv = h[:, b, t, :].rearrange("p (h d) -> p h d", d=HS)
                    drained(dve.tensor_tensor(hv, p[:, 0:T].rearrange("p (h d) -> p h d", d=2 * HS)[:, :, 0:HS],
                                              hv, ALU.add), job)

            def do_peak(u):
                r = u % 2
                p0 = await_fill(dve, ("logits", u, 0))
                link(dve.tensor_reduce(sm[:, r, 0, 0:16], p0[:, :].rearrange("p (e s) -> p e s", s=NS), AX.X, ALU.max))
                p1 = await_fill(dve, ("logits", u, 1))
                link(dve.tensor_reduce(sm[:, r, 0, 16:32], p1[:, :].rearrange("p (e s) -> p e s", s=NS), AX.X,
                                       ALU.max))
                settle()
                link(dve.tensor_reduce(tot[:, r, 0:1], sm[:, r, 0, :], AX.X, ALU.max, negate=True))
                if u >= 2:
                    dve.wait_ge(cw_ready, u - 1)
                for v, p in enumerate((p0, p1)):
                    drained(dve.tensor_tensor(ex[:, r, 16 * v:16 * v + 16, :],
                                              p[:, :].rearrange("p (e s) -> p e s", s=NS),
                                              sm[:, r, 0, 16 * v:16 * v + 16].unsqueeze(2).to_broadcast([P, 16, NS]),
                                              ALU.subtract), ("logits", u, v))
                await_drain(dve, ("logits", u, 0))
                await_drain(dve, ("logits", u, 1))
                settle()
                dve.nop().then_inc(shifted, 1)

            def do_weigh(u):
                r = u % 2
                dve.wait_ge(exps_ready, 2 * (u + 1))
                link(dve.tensor_reduce(sm[:, r, 2, :], ex[:, r, :, :], AX.X, ALU.add))
                settle()
                dve.reciprocal(sm[:, r, 3, :], sm[:, r, 2, :]).then_inc(rsum_ready, 1)
                link(dve.tensor_tensor(sm[:, r, 4, :], sm[:, r, 1, :], sm[:, r, 2, :], ALU.mult))
                settle()
                link(dve.tensor_reduce(tot[:, r, 1:2], sm[:, r, 4, :], AX.X, ALU.add))
                settle()
                link(dve.reciprocal(tot[:, r, 2:3], tot[:, r, 1:2]))
                settle()
                dve.tensor_scalar(sm[:, r, 5, :], sm[:, r, 1, :], tot[:, r, 2:3], None, ALU.mult
                                  ).then_inc(share_ready, 1)

            def do_slots_out(u):
                b, t = divmod(u, NT)
                p = await_fill(dve, ("cwT", u, 1))
                drained(dve.tensor_copy(cwT[:, b, 4:8, P * t:P * t + P], p[:, :].rearrange("p (k n) -> p k n", k=4)),
                        ("cwT", u, 1))
                if t == NT - 1:
                    for v in range(2):
                        job = ("slots", b, 1, v)
                        p = await_fill(dve, job)
                        drained(dve.tensor_copy(slotsT[0:DC, 1, 16 * v:16 * v + 16, b, :],
                                                p[0:DC, :].rearrange("p (e s) -> p e s", s=NS)), job)

            def do_experts():
                dve.nop().then_inc(eo_drained, 2)
                with dve.Fori(0, NE // RING) as it:
                    for j in range(RING):
                        dve.wait_ge(eo_full, it * RING + j + 1)
                        for b in range(NB):
                            inst = dve.tensor_tensor(
                                eok[NS * j:NS * j + NS, bass.ds(it, 1), b, :].rearrange("p k d -> p (k d)"),
                                ps[4 + j % 2][NS * b:NS * b + NS, 0:D], eb2_s[NS * b:NS * b + NS, j, :], ALU.add)
                        inst.then_inc(eo_drained, 1)
                        dve.wait_ge(eo_drained, it * RING + j + 3)
                        dve.nop().then_inc(slot_free[j], 1)

            def add_to_h(job, b, t):
                p = await_fill(dve, job)
                drained(dve.tensor_tensor(h[:, b, t, :], p[:, 0:D], h[:, b, t, :], ALU.add), job)

            def do_combine(b):
                for t in range(NT):
                    add_to_h(("combine", b, t), b, t)

            def do_qkv3(b):
                dve.wait_ge(layer1_in, 96)
                for t in range(NT):
                    job = ("qkv3_v", b, t)
                    p = await_fill(dve, job)
                    drained(dve.tensor_tensor(v3[:, b % 2, t, :], p[:, 0:D], bias_row[:, 2, :], ALU.add), job)

            def do_decay(b):
                job = ("score", b, 0)
                p = await_fill(dve, job)
                drained(dve.tensor_tensor(sc3[:, b % 2, 0, :], p[:, 0:T], decay[:, :], ALU.mult), job)
                job = ("score", b, 1)
                p = await_fill(dve, job)
                link(dve.tensor_tensor(sc3[:, b % 2, 1, 0:2 * P], p[:, 0:2 * P], decay[:, 0:2 * P], ALU.mult))
                drained(dve.tensor_tensor(sc3[:, b % 2, 1, 2 * P:T], p[:, 2 * P:T], decay[:, 0:P], ALU.mult), job)
                for t in range(NT):
                    add_to_h(("read", b, t), b, t)

            def do_ffn(b):
                for t in range(NT):
                    link(dve.tensor_tensor(h[:, b, t, :], h[:, b, t, :], bias_row[:, 3, :], ALU.add))
                for t in range(NT):
                    job = ("down", b, t)
                    p = await_fill(dve, job)
                    settle()
                    drained(dve.scalar_tensor_tensor(out=y_out[:, b, t, :], in0=p[:, 0:D], scalar=gamma[:, 1:2],
                                                     in1=h[:, b, t, :], op0=ALU.mult, op1=ALU.add), job)
                    await_drain(dve, job)
                    dve.nop().then_inc(out_ready, 1)

            table = {"phi": do_phi, "ternary": do_ternary, "embed": do_embed, "stats": do_stats, "norm": do_norm,
                     "turn": do_turn, "qkv": do_qkv, "attend": do_attend, "join": do_join, "peak": do_peak,
                     "weigh": do_weigh, "slots_out": do_slots_out, "combine": do_combine, "qkv3": do_qkv3,
                     "decay": do_decay, "ffn": do_ffn}
            for s in before:
                if s[0] in table:
                    table[s[0]](*s[1:])
            do_experts()
            for s in after:
                if s[0] in table:
                    table[s[0]](*s[1:])

        @block.tensor
        def _(pe):
            def accumulate(o, pairs):
                for n, (lhsT, rhs) in enumerate(pairs):
                    mm = pe.matmul(o, lhsT, rhs, start=(n == 0), stop=(n == len(pairs) - 1))
                return mm

            def do_phi():
                pe.wait_ge(cleared, 2)
                pe.wait_ge(phi_sq, 1)
                for v in range(2):
                    p = refill(pe, ("phi", v))
                    filled(accumulate(p[0:DC, :], [(ones[0:DC, 0:DC], sq[:, c, 512 * v:512 * v + 512])
                                                   for c in range(2)]), ("phi", v))

            def do_ternary():
                pe.wait_ge(abs_sums, 2)
                p = refill(pe, ("gamma",))
                pe.matmul(p[:, 0:1], ones[0:DC, :], gsum[0:DC, 0:1], start=True, stop=True)
                filled(pe.matmul(p[:, 1:2], ones[:, :], gsum[:, 1:2], start=True, stop=True), ("gamma",))

            def do_embed():
                pe.wait_ge(tok_in, 16 * 9)
                pe.wait_ge(regrouped, 1)
                p = refill(pe, ("f2",))
                for b in range(NB):
                    mm = pe.transpose(p[0:DC, P * b:P * b + P], r2[:, b, :, :].rearrange("p j f -> p (j f)"), ident[:, :])
                filled(mm, ("f2",))
                await_drain(pe, ("f2",))
                p = refill(pe, ("o2",))
                filled(accumulate(p[0:64, 0:64], [(w2_s[:, g, :], f2[:, :, g, :]) for g in range(8)]), ("o2",))
                await_drain(pe, ("o2",))
                for v in range(2):
                    p = refill(pe, ("z2", v))
                    for i in range(2):
                        mm = pe.matmul(p[0:16, D * i:D * i + D], o2[:, 2 * v + i, :], wf_s[:, 2, :],
                                       start=True, stop=True)
                    filled(mm, ("z2", v))
                pe.wait_ge(regrouped, 2)
                p = refill(pe, ("f1",))
                for b in range(NB):
                    mm = pe.transpose(p[0:DC, P * b:P * b + P], r1[:, b, :, :].rearrange("p j f -> p (j f)"), ident[:, :])
                filled(mm, ("f1",))
                await_drain(pe, ("f1",))
                p = refill(pe, ("o1",))
                filled(accumulate(p[0:64, 0:256], [(w1_s[:, g, :], f1[:, :, g, :]) for g in range(2)]), ("o1",))
                await_drain(pe, ("o1",))
                for v in range(2):
                    p = refill(pe, ("z1", v))
                    for i in range(2):
                        mm = pe.matmul(p[0:64, D * i:D * i + D], o1[:, 2 * v + i, :], wf_s[:, 1, :],
                                       start=True, stop=True)
                    filled(mm, ("z1", v))
                for v in range(2):
                    pe.wait_ge(regrouped, 3 + v)
                    p = refill(pe, ("f0", v))
                    for b in range(NB):
                        mm = pe.transpose(p[0:48, P * b:P * b + P], r0[:, v, b, :, :].rearrange("p j f -> p (j f)"), ident[:, :])
                    filled(mm, ("f0", v))
                    await_drain(pe, ("f0", v))
                    p = refill(pe, ("o0", v))
                    filled(pe.matmul(p[0:64, :], w0_s, f0[:, v, :], start=True, stop=True), ("o0", v))
                for v in range(2):
                    await_drain(pe, ("z2", v))
                    await_drain(pe, ("z1", v))
                    await_drain(pe, ("o0", v))
                for b in range(NB):
                    for v in range(2):
                        p = refill(pe, ("y", b, v))
                        filled(accumulate(p[:, 0:D], [(o0[:, v, b, :], wf_s[:, 0, :]),
                                                      (i1_s[:, P * v:P * v + P], z1[:, b, :]),
                                                      (i2_s[:, P * v:P * v + P], z2[:, b, :])]), ("y", b, v))

            turns = [0]

            def do_turn(layer, b):
                turns[0] += 1
                pe.wait_ge(xn_ready, NT * turns[0])
                for c in range(2):
                    p = refill(pe, ("xT", layer, b, c))
                    for t in range(NT):
                        mm = pe.transpose(p[0:DC, P * t:P * t + P], xn[:, b % 2, t, DC * c:DC * c + DC], ident[:, :])
                    filled(mm, ("xT", layer, b, c))

            def project(kind, layer, b, w):
                for c in range(2):
                    await_drain(pe, ("xT", layer, b, c))
                for m in range(4):
                    p = refill(pe, (kind, b, m))
                    filled(accumulate(p[0:DC, 0:T], [(w[:, c, DC * m:DC * m + DC], xT[:, b % 2, c, :])
                                                     for c in range(2)]), (kind, b, m))
                for t in range(NT):
                    p = refill(pe, (kind + "_v", b, t))
                    filled(accumulate(p[:, 0:D], [(xT[:, b % 2, c, P * t:P * t + P], w[:, c, 2 * D:3 * D])
                                                  for c in range(2)]), (kind + "_v", b, t))

            def do_qkv(b):
                pe.wait_ge(attn_in, 64)
                project("qkv", 0, b, wa_s)

            def do_attend(b):
                r = b % 2
                pe.wait_ge(stacks_in[r], 16 * 4 * len(PRODUCTS) * (b // 2 + 1))
                for t in range(NT):
                    await_drain(pe, ("qkv_v", b, t))
                for g in range(NG + 1):
                    if g < NG:
                        for hd in range(HG * g, HG * g + HG):
                            p = refill(pe, ("near", b, hd))
                            for t in range(NT):
                                mm = pe.matmul(p[:, P * t:P * t + P], ks[:, r, hd, P * t:P * t + P],
                                               qs[:, r, hd, P * t:P * t + P], start=True, stop=True)
                            filled(mm, ("near", b, hd))
                            p = refill(pe, ("far", b, hd))
                            pe.matmul(p[:, 0:2 * P], ks[:, r, hd, 0:P], qs[:, r, hd, P:T], start=True, stop=True)
                            filled(pe.matmul(p[:, 2 * P:T], ks[:, r, hd, P:2 * P], qs[:, r, hd, 2 * P:T],
                                             start=True, stop=True), ("far", b, hd))
                    if g:
                        job = ("mix", b, g - 1)
                        heads = range(HG * (g - 1), HG * g)
                        for hd in heads:
                            await_drain(pe, ("near", b, hd))
                            await_drain(pe, ("far", b, hd))
                        p = refill(pe, job)
                        spans = [(0, 0, 0, P, 0), (0, 1, 0, 2 * P, P), (1, 0, P, P, P), (1, 1, 2 * P, P, 2 * P),
                                 (2, 0, 2 * P, P, 2 * P)]
                        for n, (kt, far, src, width, dst) in enumerate(spans):
                            for i, hd in enumerate(heads):
                                mm = pe.matmul(p[32 * i:32 * i + 32, dst:dst + width], vpad[:, r, kt, hd, :],
                                               att[:, hd % (2 * HG), far, src:src + width],
                                               start=(n == 0), stop=(n == len(spans) - 1), skip_group_check=True)
                        filled(mm, job)

            def do_join(b):
                for g in range(NG):
                    await_drain(pe, ("mix", b, g))
                for t in range(NT):
                    p = refill(pe, ("join", b, t))
                    for g in range(NG):
                        mm = pe.transpose(p[:, P * g:P * g + P], oT[:, g, P * t:P * t + P], ident[:, :])
                    filled(mm, ("join", b, t))

            def do_logits(u):
                b, t = divmod(u, NT)
                if u == 0:
                    pe.wait_ge(phi_ready, 2)
                if t == 0:
                    for c in range(2):
                        await_drain(pe, ("xT", 1, b, c))
                for v in range(2):
                    p = refill(pe, ("logits", u, v))
                    filled(accumulate(p[:, :], [(xT[:, b % 2, c, P * t:P * t + P], phi[:, c, 512 * v:512 * v + 512])
                                                for c in range(2)]), ("logits", u, v))

            def do_slots(u):
                b, t = divmod(u, NT)
                pe.wait_ge(dw_ready, u + 1)
                for c in range(2):
                    for v in range(2):
                        job = ("slots", b, c, v)
                        p = refill(pe, job) if t == 0 else ps[use[job][0]]
                        mm = pe.matmul(p[0:DC, :], xn[:, b % 2, t, DC * c:DC * c + DC],
                                       dw[:, u % 2, 16 * v:16 * v + 16, :].rearrange("p e s -> p (e s)"),
                                       start=(t == 0), stop=(t == NT - 1))
                        if t == NT - 1:
                            filled(mm, job)
                pe.wait_ge(cw_ready, u + 1)
                for v in range(2):
                    p = refill(pe, ("cwT", u, v))
                    for k in range(4):
                        e = EPC * (4 * v + k)
                        mm = pe.transpose(p[:, P * k:P * k + P],
                                          cw[:, u % 2, e:e + EPC, :].rearrange("p e s -> p (e s)"), ident[:, :])
                    filled(mm, ("cwT", u, v))

            def do_experts():
                for c in range(2):
                    for v in range(2):
                        await_drain(pe, ("slots", NB - 1, c, v))
                for v in range(2):
                    await_drain(pe, ("cwT", NB * NT - 1, v))
                pe.wait_ge(ones_row, 1)

                def up(it, j):
                    pe.wait_ge(landed[j % RING], (it + j // RING) * 64 + 64)
                    e = it * RING + j
                    for m in range(NC):
                        o = ps[2 * (j % 2) + m // 3][:, P * (m % 3):P * (m % 3) + P]
                        for c in range(2):
                            rows = DC + c
                            if isinstance(e, int):
                                rhs = slotsT[0:rows, c, e, :, :].rearrange("p b s -> p (b s)")
                            else:
                                rhs = slotsT[0:rows, c, bass.ds(e, 1), :, :].rearrange("p e b s -> p (e b s)")
                            mm = pe.matmul(o, ew1_s[0:rows, j % RING, c, P * m:P * m + P], rhs,
                                           start=(c == 0), stop=(c == 1))
                    mm.then_inc(hid_full, 1)

                def down(it, j):
                    pe.wait_ge(hid_done, it * RING + j + 1)
                    pe.wait_ge(eo_drained, it * RING + j + 1)
                    for m in range(NC):
                        mm = pe.matmul(ps[4 + j % 2][:, 0:D], hT[:, j % 2, P * m:P * m + P], ew2_s[:, j, m, :],
                                       start=(m == 0), stop=(m == NC - 1))
                    mm.then_inc(eo_full, 1)

                up(0, 0)
                with pe.Fori(0, NE // RING - 1) as it:
                    for j in range(RING):
                        up(it, j + 1)
                        down(it, j)
                last = NE // RING - 1
                for j in range(RING):
                    if j + 1 < RING:
                        up(last, j + 1)
                    down(last, j)
                pe.wait_ge(eo_drained, NE + 2)

            def do_combine(b):
                for t in range(NT):
                    p = refill(pe, ("combine", b, t))
                    filled(accumulate(p[:, 0:D], [(cwT[:, b, k, P * t:P * t + P], eok[:, k, b, :])
                                                  for k in range(KC)]), ("combine", b, t))

            def do_qkv3(b):
                pe.wait_ge(layer1_in, 96)
                project("qkv3", 2, b, wq_s)

            def do_decay(b):
                r = b % 2
                for m in range(4):
                    await_drain(pe, ("qkv3", b, m))
                for t in range(NT):
                    await_drain(pe, ("qkv3_v", b, t))
                q, k = qk3[:, r, 0:2, :], qk3[:, r, 2:4, :]
                p = refill(pe, ("score", b, 0))
                filled(accumulate(p[:, 0:T], [(k[:, c, 0:P], q[:, c, :]) for c in range(2)]), ("score", b, 0))
                p = refill(pe, ("score", b, 1))
                accumulate(p[:, 0:2 * P], [(k[:, c, P:2 * P], q[:, c, P:T]) for c in range(2)])
                filled(accumulate(p[:, 2 * P:T], [(k[:, c, 2 * P:T], q[:, c, 2 * P:T]) for c in range(2)]),
                       ("score", b, 1))
                await_drain(pe, ("score", b, 0))
                await_drain(pe, ("score", b, 1))
                sc = [sc3[:, r, 0, :], sc3[:, r, 1, 0:2 * P], sc3[:, r, 1, 2 * P:T]]
                for t in range(NT):
                    p = refill(pe, ("read", b, t))
                    filled(accumulate(p[:, 0:D], [(sc[k][:, P * (t - k):P * (t - k) + P], v3[:, r, k, :])
                                                  for k in range(t + 1)]), ("read", b, t))

            def do_ffn(b):
                r = b % 2
                for c in range(2):
                    await_drain(pe, ("xT", 3, b, c))
                for m in range(NC):
                    p = refill(pe, ("hidden", b, m))
                    filled(accumulate(p[:, 0:T], [(tern1[:, c, P * m:P * m + P], xT[:, r, c, :])
                                                  for c in range(2)]), ("hidden", b, m))
                for m in range(NC):
                    await_drain(pe, ("hidden", b, m))
                for t in range(NT):
                    p = refill(pe, ("down", b, t))
                    filled(accumulate(p[:, 0:D], [(hid[:, r, m, P * t:P * t + P], tern2[:, m, :])
                                                  for m in range(NC)]), ("down", b, t))

            table = {"phi": do_phi, "ternary": do_ternary, "embed": do_embed, "turn": do_turn, "qkv": do_qkv,
                     "attend": do_attend, "join": do_join, "logits": do_logits, "slots": do_slots,
                     "combine": do_combine, "qkv3": do_qkv3, "decay": do_decay, "ffn": do_ffn}
            for s in before:
                if s[0] in table:
                    table[s[0]](*s[1:])
            do_experts()
            for s in after:
                if s[0] in table:
                    table[s[0]](*s[1:])


def interpolation(n_in, n_out):
    pos = np.clip((np.arange(n_out, dtype=np.float32) + 0.5) * np.float32(n_in / n_out) - 0.5, 0.0, n_in - 1)
    i0 = np.floor(pos).astype(np.int64)
    i1 = np.minimum(i0 + 1, n_in - 1)
    w = (pos - i0).astype(np.float32)
    m = np.zeros((n_in, n_out), np.float32)
    np.add.at(m, (i0, np.arange(n_out)), 1.0 - w)
    np.add.at(m, (i1, np.arange(n_out)), w)
    return m


def causal_tiles():
    k, q = np.arange(P)[:, None], np.arange(P)[None, :]
    m = np.where(q >= k, np.float32(HS) ** -0.5, 0.0).astype(np.float32)
    return np.ascontiguousarray(np.broadcast_to(m[:, None, :], (P, NT, P)))


def decay_tiles():
    diff = (np.arange(T)[None, :] - np.arange(P)[:, None]).astype(np.float32)
    m = np.where(diff >= 0, np.float32(ALPHA) ** diff, 0.0).astype(np.float32)
    return m / np.sqrt(np.float32(D))


def kernel(**inputs):
    import concourse.bacc as bacc
    from concourse.bass_utils import run_bass_kernel_spmd

    a = {k: np.asarray(v) for k, v in inputs.items()}
    x = a["x"]

    def table(p):
        g = 64 // p
        t = x.reshape(NB, 3, g, p, g, p).transpose(2, 4, 0, 3, 5, 1)
        return t.reshape(g * g, NB * p * p * 3)

    idx0 = a["L0_tok_idx0"].reshape(2, P, GP).transpose(1, 0, 2).reshape(P, 32)
    idx1 = a["L0_tok_idx1"].reshape(64, 2, 8).transpose(1, 0, 2).reshape(P, 8)
    idx2 = a["L0_tok_idx2"].reshape(16, 8, 2).transpose(1, 0, 2).reshape(P, 2)
    ba, bq = a["L0_attn_b_attn"], a["L1_attn_b_qkv"]
    order = np.arange(4 * DC).reshape(4, 6, HS).transpose(0, 2, 1).reshape(-1)
    wa = np.concatenate([a["L0_attn_W_attn"][:, order], a["L0_attn_W_attn"][:, 2 * D:]], axis=1)
    arrays = {
        "x0": table(1), "x1": table(2), "x2": table(4),
        "idx": np.concatenate([idx0, idx1, idx2], axis=1),
        "txt": a["txt"],
        "w0": a["L0_tok_W0"].T, "w1t": a["L0_tok_W1"].T, "w2t": a["L0_tok_W2"].T, "wf": a["L0_tok_Wf"].T,
        "tok_b": np.stack([a["L0_tok_b0"], a["L0_tok_b1"], a["L0_tok_b2"]], axis=1),
        "bf": a["L0_tok_bf"],
        "interp1": interpolation(64, 256), "interp2": interpolation(16, 256),
        "ident": np.eye(P, dtype=np.float32), "causal": causal_tiles(), "decay": decay_tiles(),
        "wa": wa, "ba_qk": ba[order].reshape(4, DC).T, "ba_v": ba[2 * D:],
        "phi": a["L0_ffn_phi"].reshape(D, NE * NS), "scale": a["L0_ffn_scale"],
        "ew1": a["L0_ffn_w1"], "eb1": a["L0_ffn_b1"], "ew2": a["L0_ffn_w2"], "eb2": a["L0_ffn_b2"],
        "wq": a["L1_attn_W_qkv"], "bq_qk": bq[:2 * D].reshape(4, DC).T, "bq_v": bq[2 * D:],
        "fw1": a["L1_ffn_w1"].T, "fb1": a["L1_ffn_b1"].reshape(NC, P).T, "fw2": a["L1_ffn_w2"].T,
        "fb2": a["L1_ffn_b2"],
    }
    arrays = {f"in_{k}": np.ascontiguousarray(v) for k, v in arrays.items()}
    nc = bacc.Bacc("TRN2", target_bir_lowering=False, num_devices=1)
    args = [nc.dram_tensor(k, v.shape, mybir.dt.from_np(v.dtype), kind="ExternalInput").ap()
            for k, v in arrays.items()]
    args.append(nc.dram_tensor("out_tokens", (NB, T, D), F32, kind="ExternalOutput").ap())
    build(nc, *args)
    r = run_bass_kernel_spmd(nc, [arrays], core_ids=[0])
    return r.results[0]["out_tokens"]
```

```python
from contextlib import ExitStack

import numpy as np

import concourse.bass as bass
from concourse import mybir

ALU = mybir.AluOpType
ACT = mybir.ActivationFunctionType
AX = mybir.AxisListType
F32 = mybir.dt.float32
BF16 = mybir.dt.bfloat16
I32 = mybir.dt.int32
F32R = mybir.dt.float32r

P = 128
NB = 4
NT = 3
T = NT * P
D = 192
DR = D - P
FC = 96
GP = 16
HEADS, HS = 12, 16
HG = 4
NG = HEADS // HG
NE, NS, HID = 32, 32, 768
NC = HID // P
KC = NE * NS // P
EPC = P // NS
RING = 4
LN_EPS, L2_EPS, TQ_EPS = 1e-5, 1e-12, 1e-5
ALPHA = 0.99
PRODUCTS = ((0, 0, 1, 3), (3, 0, 2, 3), (6, 0, 0, 2))


def steps():
    def normal(layer, b):
        return [("stats", layer, b), ("norm", layer, b)]

    def attend(b, *groups):
        return [("attend", b, g) for g in groups]

    attention = [
        ("phi_norms",), ("coarse",), ("gamma",), ("fine", 0), ("phi",), *(("fuse", b, 0) for b in range(NB)),
        ("split_wa",), ("fine", 1), ("ternary",),
        ("fuse", 0, 1), ("stats", 0, 0), ("fuse", 1, 1), ("norm", 0, 0), ("fuse", 2, 1), ("turn", 0, 0),
        ("stats", 0, 1), ("fuse", 3, 1), ("norm", 0, 1),
        ("qkv", 0), ("turn", 0, 1), *normal(0, 2), ("qkv", 1),
        ("turn", 0, 2), *normal(0, 3), ("qkv", 2), ("turn", 0, 3),
        *attend(0, 0, 1, 2, 3), ("qkv", 3), ("join", 0), *attend(1, 0, 1), *normal(1, 0), *attend(1, 2, 3),
        *attend(2, 0), ("join", 1), *attend(2, 1), *normal(1, 1), *attend(2, 2, 3),
        ("turn", 1, 0, 0), ("turn", 1, 0, 1), *attend(3, 0), ("join", 2), ("logits", 0), ("peak", 0),
        *attend(3, 1, 2, 3), ("weigh", 0), ("join", 3)]
    moe = []
    last = NB * NT - 1
    for u in range(NB * NT):
        b, t = divmod(u, NT)
        if u and t == 0:
            moe += [("slots_out", b - 1)]
        if u < last:
            moe += [("logits", u + 1)]
        if u:
            moe += [("shares", u - 1)]
        if t == 1 and b < NB - 1:
            moe += [("turn", 1, b + 1, 0)]
        moe += [("slots", u)]
        if u < last:
            moe += [("peak", u + 1)]
        if u:
            moe += [("shares_out", u - 1)]
        if t == 1 and b < NB - 1:
            moe += [("turn", 1, b + 1, 1)]
        other = t == 0 and 1 <= b <= NB - 2
        if other:
            moe += [("stats", 1, b + 1)]
        if u < last:
            moe += [("weigh", u + 1)]
        if other:
            moe += [("norm", 1, b + 1)]
    moe += [("slots_out", NB - 1), ("shares", last), ("shares_out", last)]
    layer1 = [
        ("split_wq",),
        ("combine", 0), *normal(2, 0), ("combine", 1), ("turn", 2, 0), *normal(2, 1), ("combine", 2),
        ("turn", 2, 1), ("qkv3", 0), *normal(2, 2), ("combine", 3), ("turn", 2, 2), ("qkv3", 1), ("score", 0),
        *normal(2, 3), ("turn", 2, 3), ("qkv3", 2), ("score", 1), ("read", 0), *normal(3, 0), ("qkv3", 3),
        ("read", 1), *normal(3, 1), ("score", 2), ("turn", 3, 0), ("score", 3), ("read", 2), *normal(3, 2),
        ("hidden", 0), ("turn", 3, 1), ("read", 3), *normal(3, 3), ("hidden", 1), ("down", 0), ("turn", 3, 2),
        ("hidden", 2), ("down", 1), ("turn", 3, 3), ("hidden", 3), ("down", 2), ("down", 3)]
    return attention + moe, layer1


def jobs_of(step):
    kind, *n = step
    n = tuple(n)
    if kind == "phi":
        return [("phi", 1), ("phi", 2)]
    if kind == "phi_norms":
        return [("phi", 0)]
    if kind == "gamma":
        return [("gamma",)]
    if kind == "coarse":
        return [("f2",), ("o2",), ("z2", 0), ("z2", 1), ("f1",), ("o1",), ("z1", 0), ("z1", 1)]
    if kind == "fine":
        return [("f0", *n), ("o0", *n)]
    if kind == "fuse":
        return [("y", *n)]
    if kind == "turn":
        return [("xT", *n, c) for c in range(2)] if len(n) == 2 else [("xT", *n)]
    if kind in ("qkv", "qkv3"):
        return [(kind, *n, m) for m in range(3)] + [(kind + "_v", *n, t) for t in range(NT)]
    if kind == "attend":
        b, g = n
        scores = [(s, b, h) for h in range(HG * g, HG * g + HG) for s in ("near", "far")] if g < NG else []
        return scores + ([("mix", b, g - 1)] if g else [])
    if kind == "join":
        return [("join", *n, t) for t in range(NT)]
    if kind == "logits":
        return [("logits", *n, v) for v in range(2)]
    if kind == "slots":
        u, = n
        return [("slots", u // NT, k) for k in range(3)] if u % NT == 0 else []
    if kind == "shares":
        return [("cwT", *n, v) for v in range(2)]
    if kind == "combine":
        return [("combine", *n, t) for t in range(NT)]
    if kind in ("score", "read", "hidden", "down"):
        return [(kind, *n, m) for m in range({"score": 2, "hidden": NC}.get(kind, NT))]
    return []


def plan_banks(before, after):
    fixed = {"logits": (0, 1), "cwT": (6, 7)}
    use, count, turn = {}, [0] * 8, 0
    for s in before + after:
        for j in jobs_of(s):
            if j[0] in fixed:
                bank = fixed[j[0]][j[-1]]
            elif j[0] == "slots":
                bank = 2 + j[2]
            elif j[0] == "xT" and j[1] == 1:
                bank = 5
            else:
                bank, turn = turn % 8, turn + 1
            count[bank] += 1
            use[j] = (bank, count[bank])
    return use


def build(nc, x0, x1, x2, idx, txt, w0, w1t, w2t, wf, tok_b, bf, interp1, interp2, ident_in, causal_in,
          decay_in, wa, ba_qk, ba_v, phi_in, scale_in, ew1, eb1, ew2, eb2, wq, bq_qk, bq_v, fw1, fb1, fw2,
          fb2, out):
    before, after = steps()
    use = plan_banks(before, after)
    q_dram = nc.dram_tensor("q_parts", [NB, 3, D, T], BF16).ap()
    k_dram = nc.dram_tensor("k_parts", [NB, 5, D, T], BF16).ap()

    with ExitStack() as ctx:
        def sb(name, shape, dt=F32):
            return ctx.enter_context(nc.sbuf_tensor(name, shape, dt))

        def sem(name):
            return ctx.enter_context(nc.semaphore(name))

        h = sb("h", [P, NB, NT, D])
        ident = sb("ident", [P, P])
        causal = sb("causal", [P, NT, P])
        decay = sb("decay", [P, T])
        ones = sb("ones", [P, P])
        bias_row = sb("bias_row", [P, 4, D])
        bias_col = sb("bias_col", [P, 24])
        tokb_c, baqk_c, bqqk_c, fb1_c = (bias_col[:, 0:3], bias_col[:, 3:6], bias_col[:, 7:10],
                                         bias_col[:, 11:17])
        scale_c = bias_col[:, 17:18]
        st6 = sb("st6", [P, NT, 6])
        mv = sb("mv", [P, 2, NT, 2])
        rstd = sb("rstd", [P, 2, NT])
        veps = sb("veps", [P, 2, NT])
        vlen = sb("vlen", [P, NT])
        mhalf = sb("mhalf", [P, NT])
        sm = sb("sm", [P, 2, 6, NE])
        tot = sb("tot", [P, 2, 3])
        tern1 = sb("tern1", [P, 2, HID], F32R)
        tern2 = sb("tern2", [P, NC, D], F32R)
        gsum = sb("gsum", [P, 3])
        gamma = sb("gamma", [P, 2])
        half = sb("half", [P, 2])
        nhalf = sb("nhalf", [P, 2])
        idx_s = sb("idx_s", [P, 42], I32)
        wq_s = sb("wq_s", [P, 2, 3 * D])
        phi_h = sb("phi_h", [P, 2, NE * NS], F32R)

        def region(name, *variants):
            views, most = [], 0
            for n, variant in enumerate(variants):
                with ExitStack() as lot:
                    got, size = [], 0
                    for m, (label, shape, dt) in enumerate(variant):
                        t = lot.enter_context(nc.sbuf_tensor(label or f"{name}_gap{n}_{m}", shape, dt))
                        size += int(np.prod(shape[1:])) * (2 if dt == BF16 else 4)
                        if label:
                            got.append(t[tuple(slice(None) for _ in shape)])
                    views.append(got)
                    most = max(most, size)
            sb(f"{name}_region", [P, most // 4])
            return views

        (xn, xT_h, xT_l, xT_s), (hT,) = region(
            "x",
            [("xn", [P, 2, NT, D], F32), ("xT_h", [P, 2, T], F32R), ("xT_l", [P, 2, T], F32R),
             ("xT_s", [P, 2, T], F32R)],
            [("hT", [P, 2, NC * P], F32)])

        expert = [[(f"ew1_{j}", [P, 2, HID], F32), (f"ew2_{j}", [P, NC, D], F32), (f"eb2_{j}", [P, D], F32)]
                  for j in range(RING)]
        weights, (phi_l, wa_l, wa_s), (q3_h, q3_l, wq_h, wq_l) = region(
            "weights",
            [b for e in expert for b in e],
            [(None, [P, RING // 2 * (2 * HID + NC * D + D)], F32), ("phi_l", [P, 2, NE * NS], F32R),
             ("wa_l", [P, 2, 3 * D], F32R), ("wa_s", [P, 2, 3 * D], F32)],
            [("q3_h", [P, 2, 4, T], F32R), ("q3_l", [P, 2, 3, T], F32R), ("wq_h", [P, 2, 3 * D], F32R),
             ("wq_l", [P, 2, 3 * D], F32R)])
        ew1_s, ew2_s, eb2_s = weights[0::3], weights[1::3], weights[2::3]

        SLOTS, CWT = 2 * NE * NB * NS, NB * KC * T
        prep, (sq, w0_s, w1_s, w2_s, wf_s, i1_s, i2_s), attn, (parts, resid, wa_h), moe, (eok,), (y_out, v3_h, v3_l, v3, act1), (sc, sc_h, sc_l, hid_h, hid_l) = region(
            "main",
            [("diag", [P, KC, P], F32), ("phi_s", [P, 2, NE * NS], F32), ("ss", [P, KC], F32), ("rt", [P, KC], F32),
             ("nw", [P, KC], F32), ("fw1_s", [P, 2, HID], F32), ("fw2_s", [P, NC, D], F32),
             ("neg1", [P, 2, HID], F32), ("neg2", [P, NC, D], F32),
             ("g0", [P, 2, GP, NB, 3], F32), ("g1", [P, 8, NB, 12], F32), ("g2", [P, 2, NB, 48], F32),
             ("r0", [P, 2, NB, GP, 3], F32), ("r1", [P, NB, 8, 12], F32), ("r2", [P, NB, 2, 48], F32),
             ("f0", [48, 2, NB * P], F32), ("f1", [FC, NB, 2, 64], F32), ("f2", [FC, NB, 8, 16], F32),
             ("o0", [64, 2, NB, P], F32), ("o1", [64, NB, 64], F32), ("o2", [64, NB, 16], F32),
             ("z1", [64, NB, D], F32), ("z2", [16, NB, D], F32)],
            [(None, [P, SLOTS + CWT], F32), ("sq", [P, 2, NE * NS], F32),
             ("w0_s", [48, 64], F32), ("w1_s", [FC, 2, 64], F32), ("w2_s", [FC, 8, 64], F32),
             ("wf_s", [64, 3, D], F32), ("i1_s", [64, 256], F32), ("i2_s", [16, 256], F32)],
            [("qs", [P, 2, HEADS, T], BF16), ("ks", [P, 2, HEADS, T], BF16), ("att", [P, 2 * HG, 2, T], F32),
             ("oT", [P, NG, T], F32), ("vpad", [P, 3, NT, HEADS, 2 * HS], F32)],
            [(None, [P, SLOTS + CWT], F32), ("parts", [P, 2, 3, 3, T], BF16), ("resid", [P, 2, T], F32),
             ("wa_h", [P, 2, 3 * D], F32R)],
            [("slotsT", [P, 2, NE, NB, NS], F32), ("cwT", [P, NB, KC, T], F32), ("ex", [P, 2, NE, NS], F32),
             ("dw", [P, 2, NE, NS], F32), ("cw", [P, 2, NE, NS], F32)],
            [(None, [P, SLOTS + CWT], F32), ("eok", [P, KC, NB, D], F32)],
            [("y_out", [P, NB, NT, D], F32), ("v3_h", [P, 3, NT, D], F32R), ("v3_l", [P, 3, NT, D], F32R),
             ("v3", [P, NT, D], F32), ("act1", [P, 2, T], F32)],
            [(None, [P, SLOTS], F32), ("sc", [P, 2, T], F32), ("sc_h", [P, 2, 2, T], F32R),
             ("sc_l", [P, 2, 2, T], F32R), ("hid_h", [P, 2, NC, T], F32R), ("hid_l", [P, 2, NC, T], F32R)])
        (diag, phi_s, ss, rt, nw, fw1_s, fw2_s, neg1, neg2, g0, g1, g2, r0, r1, r2, f0, f1, f2, o0, o1, o2, z1,
         z2) = prep
        qs, ks, att, oT, vpad = attn
        slotsT, cwT, ex, dw, cw = moe

        def raw(ap):
            return ap.bitcast(F32)

        ps = [ctx.enter_context(nc.psum_tensor(f"ps{k}", [P, 512], F32)) for k in range(8)]

        bank_full = [sem(f"bank_full{k}") for k in range(8)]
        bank_drained = [sem(f"bank_drained{k}") for k in range(8)]
        idx_in, tok_in, txt_in, phi_in_s, tern_in, attn_in, layer1_in = (
            sem(n) for n in ("idx_in", "tok_in", "txt_in", "phi_in", "tern_in", "attn_in", "layer1_in"))
        gathered = [[sem(f"gathered0_{v}") for v in range(2)], sem("gathered1"), sem("gathered2")]
        regrouped = sem("regrouped")
        cleared = sem("cleared")
        phi_sq, phi_ss, phi_root, phi_diag, phi_scaled, phi_high, phi_ready = (
            sem(n) for n in ("phi_sq", "phi_ss", "phi_root", "phi_diag", "phi_scaled", "phi_high", "phi_ready"))
        abs_sums = sem("abs_sums")
        wa_ready, wq_ready = sem("wa_ready"), sem("wq_ready")
        xT_h_ready, q3_h_ready, v3_ready, v3_parts, sc_ready, sc_h_ready, sc_parts, act1_ready, hid_h_ready, hid_parts = (
            sem(n) for n in ("xT_h_ready", "q3_h_ready", "v3_ready", "v3_parts", "sc_ready", "sc_h_ready", "sc_parts",
                             "act1_ready", "hid_h_ready", "hid_parts"))
        dve_chain, pool_chain = sem("dve_chain"), sem("pool_chain")
        stats_ready, rstd_ready, xn_ready = (
            sem(n) for n in ("stats_ready", "rstd_ready", "xn_ready"))
        part1_ready, resid_ready, part2_ready, parts_ready = (
            sem(n) for n in ("part1_ready", "resid_ready", "part2_ready", "parts_ready"))
        parts_out = sem("parts_out")
        stacks_in = [sem(f"stacks_in{r}") for r in range(2)]
        shifted, exps_ready, rsum_ready, total_ready, dw_ready, cw_ready = (
            sem(n) for n in ("shifted", "exps_ready", "rsum_ready", "total_ready", "dw_ready", "cw_ready"))
        ones_row = sem("ones_row")
        landed = [sem(f"weights_landed{j}") for j in range(RING)]
        slot_free = [sem(f"weights_free{j}") for j in range(RING)]
        hid_full, hid_done, eo_full, eo_drained = (sem(n) for n in ("hid_full", "hid_done", "eo_full", "eo_drained"))
        out_ready, stored = sem("out_ready"), sem("stored")

        def refill(pe, job):
            bank, n = use[job]
            if n > 1:
                pe.wait_ge(bank_drained[bank], n - 1)
            return ps[bank]

        def filled(inst, job):
            inst.then_inc(bank_full[use[job][0]], 1)

        def await_fill(eng, job):
            bank, n = use[job]
            eng.wait_ge(bank_full[bank], n)
            return ps[bank]

        def drained(inst, job):
            inst.then_inc(bank_drained[use[job][0]], 1)

        def await_drain(eng, job):
            bank, n = use[job]
            eng.wait_ge(bank_drained[bank], n)

        def await_xn_free(eng, layer, b):
            n = NB * layer + b - 2
            if n >= 0:
                layer, b = divmod(n, NB)
                await_fill(eng, ("slots", b, 2) if layer == 1 else ("xT", layer, b, 1))

        def chunked(w, rows=P):
            return w.rearrange("(c p) n -> p c n", p=rows)

        block = ctx.enter_context(nc.Block())

        @block.sync
        def _(sp):
            sp.dma_start(idx_s[:, :], idx).then_inc(idx_in, 16)
            sp.dma_start(phi_s, chunked(phi_in)).then_inc(phi_in_s, 16)
            sp.dma_start(scale_c[:, :], scale_in.partition_broadcast(P)).then_inc(phi_in_s, 16)
            sp.dma_start(fw1_s, chunked(fw1)).then_inc(tern_in, 16)
            sp.dma_start(fw2_s, fw2.rearrange("(c p) n -> p c n", p=P)).then_inc(tern_in, 16)
            sp.dma_start(ident[:, :], ident_in).then_inc(tok_in, 16)
            sp.dma_start(w0_s, w0).then_inc(tok_in, 16)
            sp.dma_start(w1_s, chunked(w1t, FC)).then_inc(tok_in, 16)
            sp.dma_start(w2_s, chunked(w2t, FC)).then_inc(tok_in, 16)
            sp.dma_start(wf_s, chunked(wf, 64)).then_inc(tok_in, 16)
            sp.dma_start(i1_s, interp1).then_inc(tok_in, 16)
            sp.dma_start(i2_s, interp2).then_inc(tok_in, 16)
            sp.dma_start(tokb_c[0:64, :], tok_b).then_inc(tok_in, 16)
            sp.dma_start(bias_row[:, 1, :], bf.partition_broadcast(P)).then_inc(tok_in, 16)
            sp.dma_start(h[:, :, NT - 1, :], txt.rearrange("b t d -> t b d")).then_inc(txt_in, 16)
            sp.dma_start(wa_s, chunked(wa)).then_inc(attn_in, 16)
            sp.dma_start(baqk_c, ba_qk).then_inc(attn_in, 16)
            sp.dma_start(bias_row[:, 0, :], ba_v.partition_broadcast(P)).then_inc(attn_in, 16)
            sp.dma_start(causal[:, :, :], causal_in).then_inc(attn_in, 16)
            sp.dma_start(wq_s[:, :, :], chunked(wq)).then_inc(layer1_in, 16)
            sp.dma_start(bqqk_c, bq_qk).then_inc(layer1_in, 16)
            sp.dma_start(bias_row[:, 2, :], bq_v.partition_broadcast(P)).then_inc(layer1_in, 16)
            sp.dma_start(bias_row[:, 3, :], fb2.partition_broadcast(P)).then_inc(layer1_in, 16)
            sp.dma_start(fb1_c[:, :], fb1).then_inc(layer1_in, 16)
            sp.dma_start(decay[:, :], decay_in).then_inc(layer1_in, 16)

            def load_expert(e, j):
                sp.dma_start(ew1_s[j][:, 0, :], ew1[bass.ds(e, 1), 0:P, :].rearrange("e p n -> p (e n)")
                             ).then_inc(landed[j], 16)
                sp.dma_start(ew1_s[j][0:DR, 1, :], ew1[bass.ds(e, 1), P:D, :].rearrange("e p n -> p (e n)")
                             ).then_inc(landed[j], 16)
                sp.dma_start(ew1_s[j][DR:DR + 1, 1, :], eb1[bass.ds(e, 1), :]).then_inc(landed[j], 16)
                sp.dma_start(ew2_s[j][:, :, :], ew2[bass.ds(e, 1)].rearrange("e (c p) n -> p (e c) n", p=P)
                             ).then_inc(landed[j], 16)
                sp.dma_start(eb2_s[j][:, :], eb2[bass.ds(e, 1), :].partition_broadcast(P)
                             ).then_inc(landed[j], 16)

            for b in range(NB):
                r = b % 2
                sp.wait_ge(parts_ready, 3 * b + 1)
                sp.dma_start(q_dram[b, :, 0:P].rearrange("s p t -> p s t"), parts[:, r, 0, :, :]
                             ).then_inc(parts_out, 16)
                sp.wait_ge(parts_ready, 3 * b + 2)
                sp.dma_start(q_dram[b, :, P:D].rearrange("s p t -> p s t"), parts[0:DR, r, 1, :, :]
                             ).then_inc(parts_out, 16)
                for to, n in ((0, 3), (3, 2)):
                    sp.dma_start(k_dram[b, to:to + n, 0:DR].rearrange("s p t -> p s t"),
                                 parts[DR:P, r, 1, 0:n, :]).then_inc(parts_out, 16)
                sp.wait_ge(parts_ready, 3 * b + 3)
                for to, n in ((0, 3), (3, 2)):
                    sp.dma_start(k_dram[b, to:to + n, DR:D].rearrange("s p t -> p s t"),
                                 parts[:, r, 2, 0:n, :]).then_inc(parts_out, 16)
                sp.wait_ge(parts_out, 96 * (b + 1))
                if b >= 2:
                    await_fill(sp, ("far", b - 2, HEADS - 1))
                for slot, qp, kp, n in PRODUCTS:
                    for to, dram, part in ((qs, q_dram, qp), (ks, k_dram, kp)):
                        sp.dma_start(
                            to[HS * slot:HS * (slot + n), r, :, :],
                            dram[b, part:part + n].rearrange("s (d h) t -> (s d) h t", d=HS),
                        ).then_inc(stacks_in[r], 16)
                if b == 0:
                    for j in range(RING // 2):
                        load_expert(j, j)
            await_fill(sp, ("logits", NB * NT - 1, 1))
            for j in range(RING // 2, RING):
                load_expert(j, j)
            with sp.Fori(1, NE // RING) as it:
                for j in range(RING):
                    sp.wait_ge(slot_free[j], it)
                    load_expert(it * RING + j, j)
            for b in range(NB):
                sp.wait_ge(out_ready, NT * (b + 1))
                sp.dma_start(out[b].rearrange("(t p) d -> p t d", p=P), y_out[:, b, :, :]).then_inc(stored, 16)
            sp.wait_ge(stored, 16 * NB)

        @block.gpsimd
        def _(pool):
            chain = [0]

            def link(inst):
                chain[0] += 1
                inst.then_inc(pool_chain, 1)
                pool.wait_ge(pool_chain, chain[0])

            pool.memset(ones[:, :], 1.0).then_inc(cleared, 1)
            pool.memset(mhalf[:, :], -0.5).then_inc(cleared, 1)
            pool.wait_ge(idx_in, 16)
            for j in range(2):
                pool.indirect_dma_start(g2[:, j, :, :].rearrange("p b f -> p (b f)"), None, x2,
                                        bass.IndirectOffsetOnAxis(ap=idx_s[:, 40 + j:41 + j], axis=0)
                                        ).then_inc(gathered[2], 16)
            for j in range(8):
                pool.indirect_dma_start(g1[:, j, :, :].rearrange("p b f -> p (b f)"), None, x1,
                                        bass.IndirectOffsetOnAxis(ap=idx_s[:, 32 + j:33 + j], axis=0)
                                        ).then_inc(gathered[1], 16)
            for j in range(32):
                pool.indirect_dma_start(g0[:, j // GP, j % GP, :, :].rearrange("p b f -> p (b f)"), None, x0,
                                        bass.IndirectOffsetOnAxis(ap=idx_s[:, j:j + 1], axis=0)
                                        ).then_inc(gathered[0][j // GP], 16)
            pool.memset(vpad, 0.0).then_inc(cleared, 1)

            norms = [0]

            def do_stats(layer, b):
                norms[0] += 1
                pool.wait_ge(stats_ready, norms[0])
                pool.tensor_tensor(rstd[:, b % 2, :], veps[:, b % 2, :], mhalf[:, :], ALU.pow).then_inc(rstd_ready, 1)

            def do_qkv(b):
                for m in range(3):
                    n = 3 * b + m
                    pool.wait_ge(part2_ready, n + 1)
                    pool.tensor_tensor(parts[:, b % 2, m, 2, :], resid[:, n % 2, :], parts[:, b % 2, m, 1, :],
                                       ALU.subtract).then_inc(parts_ready, 1)

            def do_weigh(u):
                if u == 0:
                    pool.wait_ge(rstd_ready, norms[0])
                    await_fill(pool, ("join", NB - 1, NT - 1))
                    pool.memset(slotsT[DR:DR + 1, 1, :, :, :], 1.0).then_inc(ones_row, 1)
                    pool.wait_ge(ones_row, 1)
                r = u % 2
                pool.wait_ge(rsum_ready, u + 1)
                if u >= 2:
                    await_fill(pool, ("cwT", u - 2, 1))
                for v in range(2):
                    some = slice(16 * v, 16 * v + 16)
                    pool.tensor_tensor(dw[:, r, some, :], ex[:, r, some, :],
                                       sm[:, r, 3, some].unsqueeze(2).to_broadcast([P, 16, NS]), ALU.mult
                                       ).then_inc(dw_ready, 1)
                pool.wait_ge(total_ready, u + 1)
                link(pool.tensor_scalar(sm[:, r, 5, :], sm[:, r, 1, :], tot[:, r, 2:3], None, ALU.mult))
                pool.tensor_tensor(cw[:, r, :, :], ex[:, r, :, :],
                                   sm[:, r, 5, :].unsqueeze(2).to_broadcast([P, NE, NS]), ALU.mult
                                   ).then_inc(cw_ready, 1)

            def do_qkv3(b):
                for t in range(NT):
                    pool.wait_ge(v3_ready, NT * b + t + 1)
                    link(pool.tensor_copy(v3_h[:, b % 3, t, :], v3[:, t, :]))
                    pool.tensor_tensor(v3_l[:, b % 3, t, :], v3[:, t, :], raw(v3_h[:, b % 3, t, :]), ALU.subtract
                                       ).then_inc(v3_parts, 1)

            def do_score(b):
                for v in range(2):
                    pool.wait_ge(sc_h_ready, 2 * b + v + 1)
                    pool.tensor_tensor(sc_l[:, b % 2, v, :], sc[:, v, :], raw(sc_h[:, b % 2, v, :]), ALU.subtract
                                       ).then_inc(sc_parts, 1)

            def do_hidden(b):
                for m in range(NC):
                    pool.wait_ge(hid_h_ready, NC * b + m + 1)
                    pool.tensor_tensor(hid_l[:, b % 2, m, :], act1[:, m % 2, :], raw(hid_h[:, b % 2, m, :]), ALU.subtract
                                       ).then_inc(hid_parts, 1)

            for s in before + after:
                f = {"stats": do_stats, "qkv": do_qkv, "weigh": do_weigh, "qkv3": do_qkv3, "score": do_score,
                     "hidden": do_hidden}.get(s[0])
                if f:
                    f(*s[1:])

        @block.scalar
        def _(act):
            def do_phi_norms():
                act.wait_ge(phi_in_s, 32)
                act.activation(sq, phi_s, ACT.Square).then_inc(phi_sq, 1)
                act.wait_ge(phi_ss, 1)
                act.activation(rt, ss, ACT.Sqrt).then_inc(phi_root, 1)

            def do_phi():
                act.wait_ge(phi_scaled, 4)
                act.copy(phi_h[:, :, :], phi_s).then_inc(phi_high, 1)

            def do_coarse():
                act.wait_ge(tok_in, 16 * 9)
                p = await_fill(act, ("o2",))
                drained(act.activation(o2, p[0:64, 0:64].rearrange("e (b n) -> e b n", b=NB), ACT.Identity,
                                       bias=tokb_c[0:64, 2:3]), ("o2",))
                for v in range(2):
                    p = await_fill(act, ("z2", v))
                    drained(act.copy(z2[:, 2 * v:2 * v + 2, :], p[0:16, 0:2 * D].rearrange("n (b d) -> n b d", b=2)),
                            ("z2", v))
                p = await_fill(act, ("o1",))
                drained(act.activation(o1, p[0:64, 0:256].rearrange("e (b n) -> e b n", b=NB), ACT.Identity,
                                       bias=tokb_c[0:64, 1:2]), ("o1",))
                for v in range(2):
                    p = await_fill(act, ("z1", v))
                    drained(act.copy(z1[:, 2 * v:2 * v + 2, :], p[0:64, 0:2 * D].rearrange("n (b d) -> n b d", b=2)),
                            ("z1", v))

            def do_fine(v):
                p = await_fill(act, ("o0", v))
                drained(act.activation(o0[:, v, :, :], p[0:64, :].rearrange("e (b n) -> e b n", b=NB),
                                       ACT.Identity, bias=tokb_c[0:64, 0:1]), ("o0", v))

            def do_turn(layer, b, *chunk):
                for c in chunk or range(2):
                    p = await_fill(act, ("xT", layer, b, c))
                    if c == 0:
                        act.copy(xT_h[:, b % 2, :], p[:, 0:T]).then_inc(xT_h_ready, 1)
                    else:
                        act.copy(xT_s[0:DR, b % 2, :], p[0:DR, 0:T]).then_inc(xT_h_ready, 1)

            def part2(b, m):
                act.wait_ge(resid_ready, 3 * b + m + 1)
                act.copy(parts[:, b % 2, m, 1, :], resid[:, (3 * b + m) % 2, :]).then_inc(part2_ready, 1)

            def do_qkv(b):
                act.wait_ge(attn_in, 64)
                for m in range(3):
                    p = await_fill(act, ("qkv", b, m))
                    if b >= 2 and m == 0:
                        act.wait_ge(parts_out, 96 * (b - 1))
                    act.activation(parts[:, b % 2, m, 0, :], p[:, 0:T], ACT.Identity, bias=baqk_c[:, m:m + 1]
                                   ).then_inc(part1_ready, 1)
                    if m:
                        part2(b, m - 1)
                part2(b, 2)

            def do_attend(b, g):
                if g < NG:
                    for hd in range(HG * g, HG * g + HG):
                        p = await_fill(act, ("far", b, hd))
                        drained(act.activation(att[:, hd % (2 * HG), 1, :], p[:, 0:T], ACT.Relu,
                                               scale=float(HS) ** -0.5), ("far", b, hd))
                if g:
                    p = await_fill(act, ("mix", b, g - 1))
                    if g == 1 and b:
                        await_fill(act, ("join", b - 1, NT - 1))
                    drained(act.copy(oT[:, g - 1, :], p[:, 0:T]), ("mix", b, g - 1))

            def do_peak(u):
                act.wait_ge(shifted, u + 1)
                act.activation(sm[:, u % 2, 1, :], sm[:, u % 2, 0, :], ACT.Exp, bias=tot[:, u % 2, 0:1]
                               ).then_inc(exps_ready, 1)
                act.activation(ex[:, u % 2, :, :], ex[:, u % 2, :, :], ACT.Exp).then_inc(exps_ready, 1)

            def do_shares_out(u):
                b, t = divmod(u, NT)
                p = await_fill(act, ("cwT", u, 0))
                drained(act.copy(cwT[:, b, 0:4, P * t:P * t + P], p[:, :].rearrange("p (k n) -> p k n", k=4)),
                        ("cwT", u, 0))

            def do_slots_out(b):
                for v in range(2):
                    job = ("slots", b, v)
                    p = await_fill(act, job)
                    drained(act.copy(slotsT[:, 0, 16 * v:16 * v + 16, b, :],
                                     p[:, :].rearrange("p (e s) -> p e s", s=NS)), job)
                if b < NB - 1:
                    job = ("slots", b, 2)
                    p = await_fill(act, job)
                    for v in range(2):
                        inst = act.copy(slotsT[0:DR, 1, 16 * v:16 * v + 16, b, :],
                                        p[DR * v:DR * v + DR, :].rearrange("p (e s) -> p e s", s=NS))
                    drained(inst, job)

            def do_experts():
                def gelu(e, j):
                    act.wait_ge(hid_full, e + 1)
                    act.activation(hT[:, j % 2, 0:T], ps[2 * (j % 2)][:, 0:T], ACT.Gelu)
                    act.activation(hT[:, j % 2, T:2 * T], ps[2 * (j % 2) + 1][:, 0:T], ACT.Gelu).then_inc(hid_done, 1)

                with act.Fori(0, NE // RING) as it:
                    for j in range(RING):
                        gelu(it * RING + j, j)

            def do_qkv3(b):
                act.wait_ge(layer1_in, 96)
                for m in range(3):
                    p = await_fill(act, ("qkv3", b, m))
                    for to, rows, at in (((0, slice(0, P), slice(0, P)),), 
                                         ((1, slice(0, DR), slice(0, DR)), (3, slice(0, DR), slice(DR, P)),
                                          (3, slice(DR, P), slice(DR, P))),
                                         ((2, slice(0, P), slice(0, P)),))[m]:
                        inst = act.activation(q3_h[rows, b % 2, to, :], p[at, 0:T], ACT.Identity,
                                              bias=bqqk_c[at, m:m + 1])
                    inst.then_inc(q3_h_ready, 1)

            def do_score(b):
                for v in range(2):
                    act.wait_ge(sc_ready, 2 * b + v + 1)
                    act.copy(sc_h[:, b % 2, v, :], sc[:, v, :]).then_inc(sc_h_ready, 1)

            def do_hidden(b):
                for m in range(NC):
                    p = await_fill(act, ("hidden", b, m))
                    n = NC * b + m
                    if n >= 2:
                        act.wait_ge(hid_parts, n - 1)
                    drained(act.activation(act1[:, m % 2, :], p[:, 0:T], ACT.Gelu, bias=fb1_c[:, m:m + 1],
                                           scale=gamma[:, 0:1]), ("hidden", b, m))

            table = {"phi_norms": do_phi_norms, "phi": do_phi, "coarse": do_coarse, "fine": do_fine, "turn": do_turn, "qkv": do_qkv, "attend": do_attend,
                     "peak": do_peak, "shares_out": do_shares_out, "slots_out": do_slots_out, "qkv3": do_qkv3,
                     "score": do_score, "hidden": do_hidden}
            for s in before:
                if s[0] in table:
                    table[s[0]](*s[1:])
            do_experts()
            for s in after:
                if s[0] in table:
                    table[s[0]](*s[1:])

        @block.vector
        def _(dve):
            chain = [0]

            def link(inst):
                chain[0] += 1
                inst.then_inc(dve_chain, 1)
                return chain[0]

            def settle(n=None):
                dve.wait_ge(dve_chain, n or chain[0])

            def do_phi_norms():
                p = await_fill(dve, ("phi", 0))
                drained(dve.tensor_scalar(ss, p[:, 0:KC], L2_EPS * L2_EPS, None, ALU.max), ("phi", 0))
                await_drain(dve, ("phi", 0))
                dve.nop().then_inc(phi_ss, 1)
                dve.wait_ge(phi_root, 1)
                link(dve.reciprocal(rt, rt))
                settle()
                link(dve.tensor_tensor(nw, rt, rt, ALU.mult))
                settle()
                link(dve.tensor_tensor(nw, nw, ss, ALU.mult))
                settle()
                link(dve.tensor_scalar(nw, nw, -0.5, 1.5, ALU.mult, ALU.add))
                settle()
                link(dve.scalar_tensor_tensor(out=nw, in0=rt, scalar=scale_c, in1=nw, op0=ALU.mult, op1=ALU.mult))
                settle()
                dve.wait_ge(tok_in, 16 * 9)
                dve.tensor_tensor(diag, ident[:, :].unsqueeze(1).to_broadcast([P, KC, P]),
                                  nw.unsqueeze(2).to_broadcast([P, KC, P]), ALU.mult).then_inc(phi_diag, 1)

            def do_phi():
                for v in range(2):
                    p = await_fill(dve, ("phi", 1 + v))
                    for c in range(2):
                        part = phi_s[:, c, 512 * v:512 * v + 512]
                        inst = dve.tensor_tensor(part, part, p[:, :], ALU.mult).then_inc(phi_scaled, 1)
                    dve.wait_ge(phi_scaled, 2 * (v + 1))
                    dve.nop().then_inc(bank_drained[use[("phi", 1 + v)][0]], 1)
                dve.wait_ge(phi_high, 1)
                dve.tensor_tensor(phi_l, phi_s, raw(phi_h[:, :, :]), ALU.subtract).then_inc(phi_ready, 1)

            def do_gamma():
                dve.wait_ge(tern_in, 32)
                dve.tensor_reduce(gsum[:, 0:2], fw1_s, AX.X, ALU.add, apply_absolute_value=True
                                  ).then_inc(abs_sums, 1)
                dve.tensor_reduce(gsum[:, 2:3], fw2_s, AX.XY, ALU.add, apply_absolute_value=True
                                  ).then_inc(abs_sums, 1)
                p = await_fill(dve, ("gamma",))
                drained(dve.tensor_scalar(gamma[:, :], p[:, 0:2], 1.0 / (D * HID), TQ_EPS, ALU.mult, ALU.add),
                        ("gamma",))

            def do_ternary():
                await_drain(dve, ("gamma",))
                link(dve.tensor_scalar(half[:, :], gamma[:, :], 0.5, None, ALU.mult))
                link(dve.tensor_scalar(nhalf[:, :], gamma[:, :], -0.5, None, ALU.mult))
                settle()
                link(dve.tensor_scalar(neg1, fw1_s, nhalf[:, 0:1], None, ALU.is_lt))
                link(dve.tensor_scalar(neg2, fw2_s, nhalf[:, 1:2], None, ALU.is_lt))
                settle()
                link(dve.scalar_tensor_tensor(out=tern1[:, :, :], in0=fw1_s, scalar=half[:, 0:1], in1=neg1,
                                              op0=ALU.is_gt, op1=ALU.subtract))
                link(dve.scalar_tensor_tensor(out=tern2[:, :, :], in0=fw2_s, scalar=half[:, 1:2], in1=neg2,
                                              op0=ALU.is_gt, op1=ALU.subtract))
                settle()

            def do_split_wa():
                dve.wait_ge(attn_in, 64)
                link(dve.tensor_copy(wa_h, wa_s))
                settle()
                dve.tensor_tensor(wa_l, wa_s, raw(wa_h), ALU.subtract).then_inc(wa_ready, 1)

            def do_split_wq():
                dve.wait_ge(layer1_in, 96)
                link(dve.tensor_copy(wq_h, wq_s[:, :, :]))
                settle()
                dve.tensor_tensor(wq_l, wq_s[:, :, :], raw(wq_h), ALU.subtract).then_inc(wq_ready, 1)

            def do_coarse():
                dve.wait_ge(gathered[2], 32)
                dve.tensor_copy(r2.rearrange("p b j f -> p j b f"), g2).then_inc(regrouped, 1)
                p = await_fill(dve, ("f2",))
                drained(dve.tensor_copy(f2, p[0:FC, :].rearrange("f (b g n) -> f b g n", b=NB, g=8)), ("f2",))
                dve.wait_ge(gathered[1], 128)
                dve.tensor_copy(r1.rearrange("p b j f -> p j b f"), g1).then_inc(regrouped, 1)
                p = await_fill(dve, ("f1",))
                drained(dve.tensor_copy(f1, p[0:FC, :].rearrange("f (b g n) -> f b g n", b=NB, g=2)), ("f1",))

            def do_fine(v):
                dve.wait_ge(gathered[0][v], 16 * GP)
                dve.tensor_copy(r0[:, v, :, :, :].rearrange("p b j f -> p j b f"), g0[:, v, :, :, :]
                                ).then_inc(regrouped, 1)
                p = await_fill(dve, ("f0", v))
                drained(dve.tensor_copy(f0[:, v, :], p[0:48, :]), ("f0", v))

            def do_fuse(b, v):
                p = await_fill(dve, ("y", b, v))
                drained(dve.tensor_tensor(h[:, b, v, :], p[:, 0:D], bias_row[:, 1, :], ALU.add), ("y", b, v))

            def do_stats(layer, b):
                n = NB * layer + b
                if n >= 2:
                    dve.wait_ge(xn_ready, NT * (n - 1))
                if layer == 0:
                    dve.wait_ge(txt_in, 16)
                    for v in range(2):
                        await_drain(dve, ("y", b, v))
                else:
                    kind = {1: "join", 2: "combine", 3: "read"}[layer]
                    for t in range(NT):
                        await_drain(dve, (kind, b, t))
                for t in range(NT):
                    link(dve.bn_stats(st6[:, t, :], h[:, b, t, :]))
                settle()
                for t in range(NT):
                    link(dve.bn_aggr(mv[:, b % 2, t, :], st6[:, t, :]))
                settle()
                var = mv[:, b % 2, :, 1]
                if layer == 1:
                    link(dve.tensor_scalar(vlen[:, :], var, LN_EPS, L2_EPS * L2_EPS, ALU.add, ALU.mult))
                    settle()
                    dve.scalar_tensor_tensor(out=veps[:, b % 2, :], in0=var, scalar=float(D), in1=vlen[:, :], op0=ALU.mult,
                                             op1=ALU.max).then_inc(stats_ready, 1)
                else:
                    dve.tensor_scalar(veps[:, b % 2, :], var, LN_EPS, None, ALU.add).then_inc(stats_ready, 1)

            def do_norm(layer, b):
                dve.wait_ge(rstd_ready, NB * layer + b + 1)
                await_xn_free(dve, layer, b)
                for t in range(NT):
                    dve.tensor_scalar(xn[:, b % 2, t, :], h[:, b, t, :], mv[:, b % 2, t, 0:1],
                                      rstd[:, b % 2, t:t + 1], ALU.subtract, ALU.mult).then_inc(xn_ready, 1)

            def do_turn(layer, b, *chunk):
                r = b % 2
                for c in chunk or range(2):
                    job = ("xT", layer, b, c)
                    p = await_fill(dve, job)
                    dve.wait_ge(xT_h_ready, 2 * (NB * layer + b) + c + 1)
                    if c == 0:
                        drained(dve.tensor_tensor(xT_l[:, r, :], p[:, 0:T], raw(xT_h[:, r, :]), ALU.subtract), job)
                    else:
                        drained(dve.tensor_tensor(xT_s[DR:P, r, :], p[0:DR, 0:T], raw(xT_s[0:DR, r, :]),
                                                  ALU.subtract), job)

            def do_qkv(b):
                dve.wait_ge(attn_in, 64)
                for m in range(3):
                    n = 3 * b + m
                    job = ("qkv", b, m)
                    p = await_fill(dve, job)
                    dve.wait_ge(part1_ready, n + 1)
                    if n >= 2:
                        dve.wait_ge(parts_ready, n - 1)
                    inst = dve.scalar_tensor_tensor(out=resid[:, n % 2, :], in0=p[:, 0:T],
                                                    scalar=baqk_c[:, m:m + 1], in1=parts[:, b % 2, m, 0, :],
                                                    op0=ALU.add, op1=ALU.subtract)
                    drained(inst, job)
                    await_drain(dve, job)
                    dve.nop().then_inc(resid_ready, 1)
                if b == 0:
                    dve.wait_ge(cleared, 3)
                for t in range(NT):
                    job = ("qkv_v", b, t)
                    p = await_fill(dve, job)
                    drained(dve.tensor_tensor(vpad[:, b % 3, t, :, 0:HS],
                                              p[:, 0:D].rearrange("p (h d) -> p h d", d=HS),
                                              bias_row[:, 0, :].rearrange("p (h d) -> p h d", d=HS), ALU.add), job)

            def do_attend(b, g):
                for hd in range(HG * g, min(HG * g + HG, HEADS)):
                    job = ("near", b, hd)
                    p = await_fill(dve, job)
                    drained(dve.scalar_tensor_tensor(out=att[:, hd % (2 * HG), 0, :], in0=p[:, 0:T], scalar=0.0,
                                                     in1=causal[:, :, :].rearrange("p a q -> p (a q)"),
                                                     op0=ALU.max, op1=ALU.mult), job)

            def do_join(b):
                for t in range(NT):
                    job = ("join", b, t)
                    p = await_fill(dve, job)
                    hv = h[:, b, t, :].rearrange("p (h d) -> p h d", d=HS)
                    drained(dve.tensor_tensor(hv, p[:, 0:T].rearrange("p (h d) -> p h d", d=2 * HS)[:, :, 0:HS],
                                              hv, ALU.add), job)

            def do_peak(u):
                r = u % 2
                p0 = await_fill(dve, ("logits", u, 0))
                link(dve.tensor_reduce(sm[:, r, 0, 0:16], p0[:, :].rearrange("p (e s) -> p e s", s=NS), AX.X, ALU.max))
                p1 = await_fill(dve, ("logits", u, 1))
                link(dve.tensor_reduce(sm[:, r, 0, 16:32], p1[:, :].rearrange("p (e s) -> p e s", s=NS), AX.X,
                                       ALU.max))
                settle()
                link(dve.tensor_reduce(tot[:, r, 0:1], sm[:, r, 0, :], AX.X, ALU.max, negate=True))
                if u >= 2:
                    dve.wait_ge(cw_ready, u - 1)
                for v, p in enumerate((p0, p1)):
                    drained(dve.tensor_tensor(ex[:, r, 16 * v:16 * v + 16, :],
                                              p[:, :].rearrange("p (e s) -> p e s", s=NS),
                                              sm[:, r, 0, 16 * v:16 * v + 16].unsqueeze(2).to_broadcast([P, 16, NS]),
                                              ALU.subtract), ("logits", u, v))
                await_drain(dve, ("logits", u, 0))
                await_drain(dve, ("logits", u, 1))
                settle()
                dve.nop().then_inc(shifted, 1)

            def do_weigh(u):
                r = u % 2
                dve.wait_ge(exps_ready, 2 * (u + 1))
                link(dve.tensor_reduce(sm[:, r, 2, :], ex[:, r, :, :], AX.X, ALU.add))
                settle()
                dve.reciprocal(sm[:, r, 3, :], sm[:, r, 2, :]).then_inc(rsum_ready, 1)
                link(dve.tensor_tensor_reduce(sm[:, r, 4, :], sm[:, r, 1, :], sm[:, r, 2, :], 1.0, 0.0, ALU.mult,
                                              ALU.add, tot[:, r, 1:2]))
                settle()
                dve.reciprocal(tot[:, r, 2:3], tot[:, r, 1:2]).then_inc(total_ready, 1)

            def do_shares_out(u):
                b, t = divmod(u, NT)
                p = await_fill(dve, ("cwT", u, 1))
                drained(dve.tensor_copy(cwT[:, b, 4:8, P * t:P * t + P], p[:, :].rearrange("p (k n) -> p k n", k=4)),
                        ("cwT", u, 1))

            def do_slots_out(b):
                if b == NB - 1:
                    job = ("slots", b, 2)
                    p = await_fill(dve, job)
                    for v in range(2):
                        inst = dve.tensor_copy(slotsT[0:DR, 1, 16 * v:16 * v + 16, b, :],
                                               p[DR * v:DR * v + DR, :].rearrange("p (e s) -> p e s", s=NS))
                    drained(inst, job)

            def do_experts():
                dve.nop().then_inc(eo_drained, 2)
                with dve.Fori(0, NE // RING) as it:
                    for j in range(RING):
                        dve.wait_ge(eo_full, it * RING + j + 1)
                        for b in range(NB):
                            inst = dve.tensor_tensor(
                                eok[NS * j:NS * j + NS, bass.ds(it, 1), b, :].rearrange("p k d -> p (k d)"),
                                ps[4 + j % 2][NS * b:NS * b + NS, 0:D], eb2_s[j][NS * b:NS * b + NS, :], ALU.add)
                        inst.then_inc(eo_drained, 1)
                        dve.wait_ge(eo_drained, it * RING + j + 3)
                        dve.nop().then_inc(slot_free[j], 1)

            def add_to_h(job, b, t):
                p = await_fill(dve, job)
                drained(dve.tensor_tensor(h[:, b, t, :], p[:, 0:D], h[:, b, t, :], ALU.add), job)

            def do_combine(b):
                for t in range(NT):
                    add_to_h(("combine", b, t), b, t)

            def do_qkv3(b):
                for m in range(3):
                    job = ("qkv3", b, m)
                    p = await_fill(dve, job)
                    dve.wait_ge(q3_h_ready, 3 * b + m + 1)
                    for low, to, high, at in (((q3_l[:, b % 2, 0, :], slice(0, P), 0, slice(0, P)),),
                                              ((q3_h[:, b % 2, 1, :], slice(DR, P), 1, slice(0, DR)),
                                               (q3_l[:, b % 2, 2, :], slice(0, DR), 3, slice(DR, P))),
                                              ((q3_l[:, b % 2, 1, :], slice(0, P), 2, slice(0, P)),))[m]:
                        inst = dve.scalar_tensor_tensor(out=low[to, :], in0=p[at, 0:T], scalar=bqqk_c[at, m:m + 1],
                                                        in1=raw(q3_h[at, b % 2, high, :]), op0=ALU.add,
                                                        op1=ALU.subtract)
                    drained(inst, job)
                for t in range(NT):
                    job = ("qkv3_v", b, t)
                    p = await_fill(dve, job)
                    if b:
                        dve.wait_ge(v3_parts, NT * (b - 1) + t + 1)
                    drained(dve.tensor_tensor(v3[:, t, :], p[:, 0:D], bias_row[:, 2, :], ALU.add), job)
                    await_drain(dve, job)
                    dve.nop().then_inc(v3_ready, 1)

            def do_score(b):
                for v in range(2):
                    job = ("score", b, v)
                    p = await_fill(dve, job)
                    if b:
                        dve.wait_ge(sc_parts, 2 * b + v - 1)
                    if v:
                        link(dve.tensor_tensor(sc[:, 1, 0:2 * P], p[:, 0:2 * P], decay[:, 0:2 * P], ALU.mult))
                        inst = dve.tensor_tensor(sc[:, 1, 2 * P:T], p[:, 2 * P:T], decay[:, 0:P], ALU.mult)
                        settle()
                    else:
                        inst = dve.tensor_tensor(sc[:, 0, :], p[:, 0:T], decay[:, :], ALU.mult)
                    drained(inst, job)
                    await_drain(dve, job)
                    dve.nop().then_inc(sc_ready, 1)

            def do_read(b):
                for t in range(NT):
                    add_to_h(("read", b, t), b, t)

            def do_hidden(b):
                for m in range(NC):
                    await_drain(dve, ("hidden", b, m))
                    dve.tensor_copy(hid_h[:, b % 2, m, :], act1[:, m % 2, :]).then_inc(hid_h_ready, 1)
                for t in range(NT):
                    link(dve.tensor_tensor(h[:, b, t, :], h[:, b, t, :], bias_row[:, 3, :], ALU.add))

            def do_down(b):
                for t in range(NT):
                    job = ("down", b, t)
                    p = await_fill(dve, job)
                    settle()
                    drained(dve.scalar_tensor_tensor(out=y_out[:, b, t, :], in0=p[:, 0:D], scalar=gamma[:, 1:2],
                                                     in1=h[:, b, t, :], op0=ALU.mult, op1=ALU.add), job)
                    await_drain(dve, job)
                    dve.nop().then_inc(out_ready, 1)

            table = {"phi_norms": do_phi_norms, "phi": do_phi, "gamma": do_gamma, "ternary": do_ternary, "coarse": do_coarse,
                     "fine": do_fine, "fuse": do_fuse, "split_wa": do_split_wa,
                     "split_wq": do_split_wq, "stats": do_stats, "norm": do_norm,
                     "turn": do_turn, "qkv": do_qkv, "attend": do_attend, "join": do_join, "peak": do_peak,
                     "weigh": do_weigh, "shares_out": do_shares_out, "slots_out": do_slots_out, "combine": do_combine, "qkv3": do_qkv3,
                     "score": do_score, "read": do_read, "hidden": do_hidden,
                     "down": do_down}
            for s in before:
                if s[0] in table:
                    table[s[0]](*s[1:])
            do_experts()
            for s in after:
                if s[0] in table:
                    table[s[0]](*s[1:])

        @block.tensor
        def _(pe):
            def accumulate(o, pairs):
                for n, (lhsT, rhs) in enumerate(pairs):
                    mm = pe.matmul(o, lhsT, rhs, start=(n == 0), stop=(n == len(pairs) - 1))
                return mm

            def split(one, other):
                (ah, al), (bh, bl) = one, other
                return [(ah, bh), (ah, bl), (al, bh)]

            def five_passes(wh, wl, xh, xl, xs):
                return split((wh[:, 0], wl[:, 0]), (xh, xl)) + [(wh[:, 1], xs), (wl[0:DR, 1], xs[0:DR])]

            def tokens(b, cols):
                return (x[:, b % 2, cols] for x in (xT_h, xT_l, xT_s))

            def flip(pairs):
                return [(x, w) for w, x in pairs]

            def do_phi_norms():
                pe.wait_ge(cleared, 2)
                pe.wait_ge(phi_sq, 1)
                p = refill(pe, ("phi", 0))
                for k in range(KC):
                    mm = accumulate(p[:, k:k + 1], [(sq[0:n, c, P * k:P * k + P], ones[0:n, 0:1])
                                                    for c, n in enumerate((P, DR))])
                filled(mm, ("phi", 0))

            def do_phi():
                pe.wait_ge(phi_diag, 1)
                for v in range(2):
                    p = refill(pe, ("phi", 1 + v))
                    filled(pe.matmul(p[:, :], ones[:, :], diag[:, 4 * v:4 * v + 4, :].rearrange("p k n -> p (k n)"),
                                     start=True, stop=True), ("phi", 1 + v))

            def do_gamma():
                pe.wait_ge(abs_sums, 2)
                p = refill(pe, ("gamma",))
                accumulate(p[:, 0:1], [(ones[:, :], gsum[:, 0:1]), (ones[0:DR, :], gsum[0:DR, 1:2])])
                filled(accumulate(p[:, 1:2], [(ones[:, :], gsum[:, 2:3])]), ("gamma",))

            def do_coarse():
                pe.wait_ge(tok_in, 16 * 9)
                pe.wait_ge(regrouped, 1)
                p = refill(pe, ("f2",))
                for b in range(NB):
                    mm = pe.transpose(p[0:FC, P * b:P * b + P], r2[:, b, :, :].rearrange("p j f -> p (j f)"), ident[:, :])
                filled(mm, ("f2",))
                await_drain(pe, ("f2",))
                p = refill(pe, ("o2",))
                filled(accumulate(p[0:64, 0:64], [(w2_s[:, g, :], f2[:, :, g, :]) for g in range(8)]), ("o2",))
                await_drain(pe, ("o2",))
                for v in range(2):
                    p = refill(pe, ("z2", v))
                    for i in range(2):
                        mm = pe.matmul(p[0:16, D * i:D * i + D], o2[:, 2 * v + i, :], wf_s[:, 2, :],
                                       start=True, stop=True)
                    filled(mm, ("z2", v))
                pe.wait_ge(regrouped, 2)
                p = refill(pe, ("f1",))
                for b in range(NB):
                    mm = pe.transpose(p[0:FC, P * b:P * b + P], r1[:, b, :, :].rearrange("p j f -> p (j f)"), ident[:, :])
                filled(mm, ("f1",))
                await_drain(pe, ("f1",))
                p = refill(pe, ("o1",))
                filled(accumulate(p[0:64, 0:256], [(w1_s[:, g, :], f1[:, :, g, :]) for g in range(2)]), ("o1",))
                await_drain(pe, ("o1",))
                for v in range(2):
                    p = refill(pe, ("z1", v))
                    for i in range(2):
                        mm = pe.matmul(p[0:64, D * i:D * i + D], o1[:, 2 * v + i, :], wf_s[:, 1, :],
                                       start=True, stop=True)
                    filled(mm, ("z1", v))

            def do_fine(v):
                pe.wait_ge(regrouped, 3 + v)
                p = refill(pe, ("f0", v))
                for b in range(NB):
                    mm = pe.transpose(p[0:48, P * b:P * b + P], r0[:, v, b, :, :].rearrange("p j f -> p (j f)"),
                                      ident[:, :])
                filled(mm, ("f0", v))
                await_drain(pe, ("f0", v))
                p = refill(pe, ("o0", v))
                filled(pe.matmul(p[0:64, :], w0_s, f0[:, v, :], start=True, stop=True), ("o0", v))

            def do_fuse(b, v):
                for i in range(2):
                    await_drain(pe, ("z2", i))
                    await_drain(pe, ("z1", i))
                await_drain(pe, ("o0", v))
                p = refill(pe, ("y", b, v))
                filled(accumulate(p[:, 0:D], [(o0[:, v, b, :], wf_s[:, 0, :]),
                                              (i1_s[:, P * v:P * v + P], z1[:, b, :]),
                                              (i2_s[:, P * v:P * v + P], z2[:, b, :])]), ("y", b, v))

            def do_turn(layer, b, *chunk):
                pe.wait_ge(xn_ready, NT * (NB * layer + b + 1))
                for c in chunk or range(2):
                    first, n = ((0, P), (P, DR))[c]
                    p = refill(pe, ("xT", layer, b, c))
                    for t in range(NT):
                        mm = pe.transpose(p[0:n, P * t:P * t + P], xn[:, b % 2, t, first:first + n], ident[:, :])
                    filled(mm, ("xT", layer, b, c))

            def project(kind, layer, b, wh, wl):
                for c in range(2):
                    await_drain(pe, ("xT", layer, b, c))
                for m in range(3):
                    p = refill(pe, (kind, b, m))
                    cols = slice(P * m, P * m + P)
                    filled(accumulate(p[:, 0:T], five_passes(wh[:, :, cols], wl[:, :, cols],
                                                             *tokens(b, slice(0, T)))), (kind, b, m))
                for t in range(NT):
                    p = refill(pe, (kind + "_v", b, t))
                    filled(accumulate(p[:, 0:D], flip(five_passes(wh[:, :, 2 * D:3 * D], wl[:, :, 2 * D:3 * D],
                                                                  *tokens(b, slice(P * t, P * t + P))))),
                           (kind + "_v", b, t))

            def do_qkv(b):
                pe.wait_ge(wa_ready, 1)
                project("qkv", 0, b, wa_h, wa_l)

            def do_attend(b, g):
                r = b % 2
                if g == 0:
                    for t in range(NT):
                        await_drain(pe, ("qkv_v", b, t))
                    pe.wait_ge(stacks_in[r], 16 * 2 * len(PRODUCTS) * (b // 2 + 1))
                if g < NG:
                    for hd in range(HG * g, HG * g + HG):
                        p = refill(pe, ("near", b, hd))
                        for t in range(NT):
                            mm = pe.matmul(p[:, P * t:P * t + P], ks[:, r, hd, P * t:P * t + P],
                                           qs[:, r, hd, P * t:P * t + P], start=True, stop=True)
                        filled(mm, ("near", b, hd))
                        p = refill(pe, ("far", b, hd))
                        pe.matmul(p[:, 0:2 * P], ks[:, r, hd, 0:P], qs[:, r, hd, P:T], start=True, stop=True)
                        filled(pe.matmul(p[:, 2 * P:T], ks[:, r, hd, P:2 * P], qs[:, r, hd, 2 * P:T],
                                         start=True, stop=True), ("far", b, hd))
                if g:
                    job = ("mix", b, g - 1)
                    heads = range(HG * (g - 1), HG * g)
                    for hd in heads:
                        await_drain(pe, ("near", b, hd))
                        await_drain(pe, ("far", b, hd))
                    p = refill(pe, job)
                    spans = [(0, 0, 0, P, 0), (0, 1, 0, 2 * P, P), (1, 0, P, P, P), (1, 1, 2 * P, P, 2 * P),
                             (2, 0, 2 * P, P, 2 * P)]
                    for n, (kt, far, src, width, dst) in enumerate(spans):
                        for i, hd in enumerate(heads):
                            mm = pe.matmul(p[32 * i:32 * i + 32, dst:dst + width], vpad[:, b % 3, kt, hd, :],
                                           att[:, hd % (2 * HG), far, src:src + width],
                                           start=(n == 0), stop=(n == len(spans) - 1), skip_group_check=True)
                    filled(mm, job)

            def do_join(b):
                for g in range(NG):
                    await_drain(pe, ("mix", b, g))
                for t in range(NT):
                    p = refill(pe, ("join", b, t))
                    for g in range(NG):
                        mm = pe.transpose(p[:, P * g:P * g + P], oT[:, g, P * t:P * t + P], ident[:, :])
                    filled(mm, ("join", b, t))

            def do_logits(u):
                b, t = divmod(u, NT)
                if u == 0:
                    pe.wait_ge(phi_ready, 1)
                if t == 0:
                    for c in range(2):
                        await_drain(pe, ("xT", 1, b, c))
                for v in range(2):
                    p = refill(pe, ("logits", u, v))
                    cols = slice(512 * v, 512 * v + 512)
                    filled(accumulate(p[:, :], flip(five_passes(phi_h[:, :, cols], phi_l[:, :, cols],
                                                                *tokens(b, slice(P * t, P * t + P))))),
                           ("logits", u, v))

            def do_slots(u):
                b, t = divmod(u, NT)
                pe.wait_ge(dw_ready, 2 * u + 1)
                weights = [dw[:, u % 2, 16 * v:16 * v + 16, :].rearrange("p e s -> p (e s)") for v in range(2)]
                start, stop = t == 0, t == NT - 1
                for v in range(2):
                    if v:
                        pe.wait_ge(dw_ready, 2 * u + 2)
                    p = refill(pe, ("slots", b, v)) if start else ps[use[("slots", b, v)][0]]
                    mm = pe.matmul(p[:, :], xn[:, b % 2, t, 0:P], weights[v], start=start, stop=stop)
                    if stop:
                        filled(mm, ("slots", b, v))
                p = refill(pe, ("slots", b, 2)) if start else ps[use[("slots", b, 2)][0]]
                for v in range(2):
                    mm = pe.matmul(p[DR * v:DR * v + DR, :], xn[:, b % 2, t, P:D], weights[v],
                                   start=start, stop=stop, skip_group_check=True)
                if stop:
                    filled(mm, ("slots", b, 2))

            def do_shares(u):
                pe.wait_ge(cw_ready, u + 1)
                for v in range(2):
                    p = refill(pe, ("cwT", u, v))
                    for k in range(4):
                        e = EPC * (4 * v + k)
                        mm = pe.transpose(p[:, P * k:P * k + P],
                                          cw[:, u % 2, e:e + EPC, :].rearrange("p e s -> p (e s)"), ident[:, :])
                    filled(mm, ("cwT", u, v))

            def do_experts():
                for k in range(3):
                    await_drain(pe, ("slots", NB - 1, k))
                for v in range(2):
                    await_drain(pe, ("cwT", NB * NT - 1, v))
                pe.wait_ge(ones_row, 1)

                def up(it, j):
                    pe.wait_ge(landed[j % RING], (it + j // RING) * 80 + 80)
                    e = it * RING + j
                    for m in range(NC):
                        o = ps[2 * (j % 2) + m // 3][:, P * (m % 3):P * (m % 3) + P]
                        for c in range(2):
                            rows = P if c == 0 else DR + 1
                            if isinstance(e, int):
                                rhs = slotsT[0:rows, c, e, :, :].rearrange("p b s -> p (b s)")
                            else:
                                rhs = slotsT[0:rows, c, bass.ds(e, 1), :, :].rearrange("p e b s -> p (e b s)")
                            mm = pe.matmul(o, ew1_s[j % RING][0:rows, c, P * m:P * m + P], rhs,
                                           start=(c == 0), stop=(c == 1))
                    mm.then_inc(hid_full, 1)

                def down(it, j):
                    pe.wait_ge(hid_done, it * RING + j + 1)
                    pe.wait_ge(eo_drained, it * RING + j + 1)
                    for m in range(NC):
                        mm = pe.matmul(ps[4 + j % 2][:, 0:D], hT[:, j % 2, P * m:P * m + P], ew2_s[j][:, m, :],
                                       start=(m == 0), stop=(m == NC - 1))
                    mm.then_inc(eo_full, 1)

                up(0, 0)
                with pe.Fori(0, NE // RING - 1) as it:
                    for j in range(RING):
                        up(it, j + 1)
                        down(it, j)
                last = NE // RING - 1
                for j in range(RING):
                    if j + 1 < RING:
                        up(last, j + 1)
                    down(last, j)
                pe.wait_ge(eo_drained, NE + 2)

            def do_combine(b):
                for t in range(NT):
                    p = refill(pe, ("combine", b, t))
                    filled(accumulate(p[:, 0:D], [(cwT[:, b, k, P * t:P * t + P], eok[:, k, b, :])
                                                  for k in range(KC)]), ("combine", b, t))

            def do_qkv3(b):
                pe.wait_ge(wq_ready, 1)
                project("qkv3", 2, b, wq_h, wq_l)

            def do_score(b):
                r = b % 2
                for m in range(3):
                    await_drain(pe, ("qkv3", b, m))

                def products(kt, first):
                    keys, queries = slice(P * kt, P * kt + P), slice(first, T)
                    return split((q3_h[:, r, 2, keys], q3_l[:, r, 1, keys]),
                                 (q3_h[:, r, 0, queries], q3_l[:, r, 0, queries])) + [
                        (q3_h[:, r, 3, keys], q3_h[:, r, 1, queries]),
                        (q3_l[0:DR, r, 2, keys], q3_h[0:DR, r, 1, queries])]

                p = refill(pe, ("score", b, 0))
                filled(accumulate(p[:, 0:T], products(0, 0)), ("score", b, 0))
                p = refill(pe, ("score", b, 1))
                accumulate(p[:, 0:2 * P], products(1, P))
                filled(accumulate(p[:, 2 * P:T], products(2, 2 * P)), ("score", b, 1))

            def do_read(b):
                r = b % 2
                pe.wait_ge(sc_parts, 2 * (b + 1))
                pe.wait_ge(v3_parts, NT * (b + 1))
                at = [(0, 0), (1, 0), (1, 2 * P)]
                for t in range(NT):
                    p = refill(pe, ("read", b, t))
                    pairs = []
                    for k in range(t + 1):
                        half_, col = at[k][0], at[k][1] + P * (t - k)
                        pairs += split((sc_h[:, r, half_, col:col + P], sc_l[:, r, half_, col:col + P]),
                                       (v3_h[:, b % 3, k, :], v3_l[:, b % 3, k, :]))
                    filled(accumulate(p[:, 0:D], pairs), ("read", b, t))

            def do_hidden(b):
                r = b % 2
                for c in range(2):
                    await_drain(pe, ("xT", 3, b, c))
                for m in range(NC):
                    p = refill(pe, ("hidden", b, m))
                    filled(accumulate(p[:, 0:T], [(tern1[:, c, P * m:P * m + P], x[:, r, :])
                                                  for c, x in ((0, xT_h), (0, xT_l), (1, xT_s))]), ("hidden", b, m))

            def do_down(b):
                pe.wait_ge(hid_parts, NC * (b + 1))
                for t in range(NT):
                    p = refill(pe, ("down", b, t))
                    filled(accumulate(p[:, 0:D], [(x[:, b % 2, m, P * t:P * t + P], tern2[:, m, :])
                                                  for m in range(NC) for x in (hid_h, hid_l)]), ("down", b, t))

            table = {"phi_norms": do_phi_norms, "phi": do_phi, "gamma": do_gamma, "coarse": do_coarse, "fine": do_fine,
                     "fuse": do_fuse, "turn": do_turn, "qkv": do_qkv,
                     "attend": do_attend, "join": do_join, "logits": do_logits, "slots": do_slots,
                     "shares": do_shares,
                     "combine": do_combine, "qkv3": do_qkv3, "score": do_score, "read": do_read, "hidden": do_hidden,
                     "down": do_down}
            for s in before:
                if s[0] in table:
                    table[s[0]](*s[1:])
            do_experts()
            for s in after:
                if s[0] in table:
                    table[s[0]](*s[1:])


def interpolation(n_in, n_out):
    pos = np.clip((np.arange(n_out, dtype=np.float32) + 0.5) * np.float32(n_in / n_out) - 0.5, 0.0, n_in - 1)
    i0 = np.floor(pos).astype(np.int64)
    i1 = np.minimum(i0 + 1, n_in - 1)
    w = (pos - i0).astype(np.float32)
    m = np.zeros((n_in, n_out), np.float32)
    np.add.at(m, (i0, np.arange(n_out)), 1.0 - w)
    np.add.at(m, (i1, np.arange(n_out)), w)
    return m


def causal_tiles():
    k, q = np.arange(P)[:, None], np.arange(P)[None, :]
    m = np.where(q >= k, np.float32(HS) ** -0.5, 0.0).astype(np.float32)
    return np.ascontiguousarray(np.broadcast_to(m[:, None, :], (P, NT, P)))


def decay_tiles():
    diff = (np.arange(T)[None, :] - np.arange(P)[:, None]).astype(np.float32)
    m = np.where(diff >= 0, np.float32(ALPHA) ** diff, 0.0).astype(np.float32)
    return m / np.sqrt(np.float32(D))


def kernel(**inputs):
    import concourse.bacc as bacc
    from concourse.bass_utils import run_bass_kernel_spmd

    a = {k: np.asarray(v) for k, v in inputs.items()}
    x = a["x"]

    def table(p):
        g = 64 // p
        t = x.reshape(NB, 3, g, p, g, p).transpose(2, 4, 0, 3, 5, 1)
        return t.reshape(g * g, NB * p * p * 3)

    idx0 = a["L0_tok_idx0"].reshape(2, P, GP).transpose(1, 0, 2).reshape(P, 32)
    idx1 = a["L0_tok_idx1"].reshape(64, 2, 8).transpose(1, 0, 2).reshape(P, 8)
    idx2 = a["L0_tok_idx2"].reshape(16, 8, 2).transpose(1, 0, 2).reshape(P, 2)
    ba, bq = a["L0_attn_b_attn"], a["L1_attn_b_qkv"]
    order = np.arange(2 * D).reshape(2, HEADS, HS).transpose(0, 2, 1).reshape(-1)
    wa = np.concatenate([a["L0_attn_W_attn"][:, order], a["L0_attn_W_attn"][:, 2 * D:]], axis=1)
    order3 = np.concatenate([np.arange(D), np.arange(D + P, 2 * D), np.arange(D, D + P)])
    wq = np.concatenate([a["L1_attn_W_qkv"][:, order3], a["L1_attn_W_qkv"][:, 2 * D:]], axis=1)

    def doubled(w):
        return np.concatenate([w, w[P:]], axis=0)

    arrays = {
        "x0": table(1), "x1": table(2), "x2": table(4),
        "idx": np.concatenate([idx0, idx1, idx2], axis=1),
        "txt": a["txt"],
        "w0": a["L0_tok_W0"].T, "w1t": a["L0_tok_W1"].T, "w2t": a["L0_tok_W2"].T, "wf": a["L0_tok_Wf"].T,
        "tok_b": np.stack([a["L0_tok_b0"], a["L0_tok_b1"], a["L0_tok_b2"]], axis=1),
        "bf": a["L0_tok_bf"],
        "interp1": interpolation(64, 256), "interp2": interpolation(16, 256),
        "ident": np.eye(P, dtype=np.float32), "causal": causal_tiles(), "decay": decay_tiles(),
        "wa": doubled(wa), "ba_qk": ba[order].reshape(3, P).T, "ba_v": ba[2 * D:],
        "phi": doubled(a["L0_ffn_phi"].reshape(D, NE * NS)), "scale": a["L0_ffn_scale"],
        "ew1": a["L0_ffn_w1"], "eb1": a["L0_ffn_b1"], "ew2": a["L0_ffn_w2"], "eb2": a["L0_ffn_b2"],
        "wq": doubled(wq), "bq_qk": bq[order3].reshape(3, P).T, "bq_v": bq[2 * D:],
        "fw1": doubled(a["L1_ffn_w1"].T), "fb1": a["L1_ffn_b1"].reshape(NC, P).T, "fw2": a["L1_ffn_w2"].T,
        "fb2": a["L1_ffn_b2"],
    }
    arrays = {f"in_{k}": np.ascontiguousarray(v) for k, v in arrays.items()}
    nc = bacc.Bacc("TRN2", target_bir_lowering=False, num_devices=1)
    args = [nc.dram_tensor(k, v.shape, mybir.dt.from_np(v.dtype), kind="ExternalInput").ap()
            for k, v in arrays.items()]
    args.append(nc.dram_tensor("out_tokens", (NB, T, D), F32, kind="ExternalOutput").ap())
    build(nc, *args)
    r = run_bass_kernel_spmd(nc, [arrays], core_ids=[0])
    return r.results[0]["out_tokens"]
```

```python
from contextlib import ExitStack

import numpy as np

import concourse.bass as bass
from concourse import mybir

ALU = mybir.AluOpType
ACT = mybir.ActivationFunctionType
AX = mybir.AxisListType
F32 = mybir.dt.float32
BF16 = mybir.dt.bfloat16
I32 = mybir.dt.int32
F32R = mybir.dt.float32r

P = 128
NB = 4
NT = 3
T = NT * P
D = 192
DR = D - P
FC = 96
GP = 16
HEADS, HS = 12, 16
HG = 4
NG = HEADS // HG
NE, NS, HID = 32, 32, 768
NC = HID // P
KC = NE * NS // P
EPC = P // NS
RING = 4
LN_EPS, L2_EPS, TQ_EPS = 1e-5, 1e-12, 1e-5
ALPHA = 0.99
PRODUCTS = ((0, 0, 1, 3), (3, 0, 2, 3), (6, 0, 0, 2))


def steps():
    def normal(layer, b):
        return [("stats", layer, b), ("norm", layer, b)]

    def turn(layer, b, *chunk):
        return [(kind, layer, b, *chunk) for kind in ("turn", "turn_h", "turn_l")]

    def attend(b, *groups):
        return [("attend", b, g) for g in groups]

    attention = [
        ("abs_sums",), ("phi_norms",), ("gamma",), ("coarse",), ("ternary",), ("fine", 0), ("own", 0), ("phi",),
        *((kind, b, 0) for b in range(NB) for kind in ("blend", "fuse")),
        *(("blend", b, 1) for b in range(NB)), *(("early_stats", b) for b in range(NB)), ("fine", 1), ("own", 1),
        ("split_wa",),
        ("fuse", 0, 1), ("stats", 0, 0), ("fuse", 1, 1), ("norm", 0, 0), ("stats", 0, 1), ("fuse", 2, 1),
        ("turn_h", 0, 0), ("turn_l", 0, 0), ("turn", 0, 0), ("norm", 0, 1), ("fuse", 3, 1), ("stats", 0, 3),
        ("qkv", 0), ("turn", 0, 1), ("stats", 0, 2), ("turn_h", 0, 1), ("turn_l", 0, 1), ("v", 0),
        ("norm", 0, 2), ("qkv", 1), *turn(0, 2), ("v", 1), ("norm", 0, 3), ("qkv", 2), ("turn", 0, 3),
        ("turn_h", 0, 3), ("v", 2), ("turn_l", 0, 3), *attend(0, 0, 1, 2), ("qkv", 3), *attend(0, 3), ("v", 3),
        ("join", 0), *attend(1, 0, 1), ("stats", 1, 0), *attend(1, 2), ("norm", 1, 0), *attend(1, 3),
        *attend(2, 0), ("join", 1), *attend(2, 1, 2), ("turn_h", 1, 0, 0), ("stats", 1, 1),
        ("turn_l", 1, 0, 0), ("turn", 1, 0, 0), *turn(1, 0, 1), *attend(2, 3), *attend(3, 0), ("norm", 1, 1),
        ("join", 2), ("logits", 0), ("peak", 0), *attend(3, 1, 2), ("weigh", 0), *attend(3, 3),
        ("stats", 1, 2), ("join", 3)]
    moe = []
    last = NB * NT - 1
    for u in range(NB * NT):
        b, t = divmod(u, NT)
        turns = t == 1 and b < NB - 1
        if u and t == 0:
            moe += [("slots_out", b - 1)]
        if u < last:
            moe += [("logits", u + 1)]
        if turns:
            moe += turn(1, b + 1, 0)
        if u:
            moe += [("shares", u - 1)]
        if turns:
            moe += [("turn", 1, b + 1, 1), ("turn_h", 1, b + 1, 1)]
        moe += [("slots", u)]
        if u < last:
            moe += [("peak", u + 1)]
        if turns:
            moe += [("turn_l", 1, b + 1, 1)]
        if u:
            moe += [("shares_out", u - 1)]
        if t == 0 and 1 <= b < NB - 1:
            moe += [("norm", 1, b + 1)]
        if t == 2 and 2 < b + 2 < NB:
            moe += [("stats", 1, b + 2)]
        if u < last:
            moe += [("weigh", u + 1)]
    moe += [("slots_out", NB - 1), ("shares", last), ("shares_out", last)]
    layer1 = [
        ("split_wq",), ("combine", 0, 1), ("combine", 0, 0), ("combine", 0, 2), ("stats", 2, 0),
        ("combine", 1, 0), ("norm", 2, 0), ("combine", 1, 1), *turn(2, 0), ("combine", 1, 2), *normal(2, 1),
        ("qkv3", 0), ("v3", 0), *turn(2, 1), ("combine", 2, 0), ("score", 0), ("combine", 2, 2),
        ("combine", 2, 1), *normal(2, 2), ("qkv3", 1), ("v3", 1), ("combine", 3, 0), ("combine", 3, 1),
        ("score", 1), ("turn_h", 2, 2), ("turn", 2, 2), ("turn_l", 2, 2), ("combine", 3, 2), ("stats", 2, 3),
        ("read", 0), ("norm", 2, 3), ("qkv3", 2), ("turn", 2, 3), ("turn_l", 2, 3), ("turn_h", 2, 3),
        ("v3", 2), ("read", 1), ("stats", 3, 0), ("score", 2), ("norm", 3, 0), ("qkv3", 3), ("turn", 3, 0),
        ("turn_l", 3, 0), ("turn_h", 3, 0), ("v3", 3), ("hidden", 0), ("stats", 3, 1), ("score", 3),
        ("norm", 3, 1), ("read", 2), ("stats", 3, 2), *turn(3, 1), ("read", 3), ("norm", 3, 2), ("hidden", 1),
        ("turn", 3, 2), ("turn_h", 3, 2), ("stats", 3, 3), ("turn_l", 3, 2), ("norm", 3, 3), ("down", 0),
        ("hidden", 2), ("turn", 3, 3), ("turn_l", 3, 3), ("turn_h", 3, 3), ("down", 1), ("hidden", 3),
        ("down", 2), ("down", 3)]
    return attention + moe, layer1


def jobs_of(step):
    kind, *n = step
    n = tuple(n)
    if kind == "phi":
        return [("phi", 1), ("phi", 2)]
    if kind == "phi_norms":
        return [("phi", 0)]
    if kind == "gamma":
        return [("gamma",)]
    if kind == "coarse":
        return [("f2",), ("f1",), ("o2",), ("o1",), ("z2", 0), ("z2", 1), ("z1", 0), ("z1", 1)]
    if kind == "fine":
        return [("f0", *n)]
    if kind == "own":
        return [("o0", *n)]
    if kind == "blend":
        return [("y", *n)]
    if kind == "turn":
        return [("xT", *n, c) for c in range(2)] if len(n) == 2 else [("xT", *n)]
    if kind in ("qkv", "qkv3"):
        return [(kind, *n, m) for m in range(3)]
    if kind in ("v", "v3"):
        return [(kind, *n, t) for t in range(NT)]
    if kind == "attend":
        b, g = n
        scores = [(s, b, h) for h in range(HG * g, HG * g + HG) for s in ("near", "far")] if g < NG else []
        return scores + ([("mix", b, g - 1)] if g else [])
    if kind == "join":
        return [("join", *n, t) for t in range(NT)]
    if kind == "logits":
        return [("logits", *n, v) for v in range(2)]
    if kind == "slots":
        u, = n
        return [("slots", u // NT, k) for k in range(3)] if u % NT == 0 else []
    if kind == "shares":
        return [("cwT", *n, v) for v in range(2)]
    if kind == "combine":
        return [step]
    if kind in ("score", "read", "hidden", "down"):
        return [(kind, *n, m) for m in range({"score": 2, "hidden": NC}.get(kind, NT))]
    return []


def plan_banks(before, after):
    fixed = {"logits": (0, 1), "cwT": (6, 7)}
    use, count, turn = {}, [0] * 8, 0
    for s in before + after:
        for j in jobs_of(s):
            if j[0] in fixed:
                bank = fixed[j[0]][j[-1]]
            elif j[0] == "slots":
                bank = 2 + j[2]
            elif j[0] == "xT" and j[1] == 1 and j[2]:
                bank = 5
            else:
                bank, turn = turn % 8, turn + 1
            count[bank] += 1
            use[j] = (bank, count[bank])
    return use


def build(nc, x0, x1, x2, idx, txt, w0, w1t, w2t, wf, tok_b, bf, interp1, interp2, ident_in, causal_in,
          decay_in, wa, ba_qk, ba_v, phi_in, scale_in, ew1, eb1, ew2, eb2, wq, bq_qk, bq_v, fw1, fb1, fw2,
          fb2, out):
    before, after = steps()
    use = plan_banks(before, after)
    q_dram = nc.dram_tensor("q_parts", [NB, 3, D, T], BF16).ap()
    k_dram = nc.dram_tensor("k_parts", [NB, 5, D, T], BF16).ap()

    with ExitStack() as ctx:
        def sb(name, shape, dt=F32):
            return ctx.enter_context(nc.sbuf_tensor(name, shape, dt))

        def sem(name):
            return ctx.enter_context(nc.semaphore(name))

        h = sb("h", [P, NB, NT, D])
        ident = sb("ident", [P, P])
        causal = sb("causal", [P, NT, P])
        decay = sb("decay", [P, T])
        ones = sb("ones", [P, P])
        bias_row = sb("bias_row", [P, 4, D])
        bias_col = sb("bias_col", [P, 24])
        tokb_c, baqk_c, bqqk_c, fb1_c = (bias_col[:, 0:3], bias_col[:, 3:6], bias_col[:, 7:10],
                                         bias_col[:, 11:17])
        scale_c = bias_col[:, 17:18]
        st6 = sb("st6", [P, NB, NT, 6])
        mv = sb("mv", [P, NB, NT, 2])
        rstd = sb("rstd", [P, NB, NT])
        veps = sb("veps", [P, NB, NT])
        vlen = sb("vlen", [P, NT])
        mhalf = sb("mhalf", [P, NT])
        sm = sb("sm", [P, 2, 6, NE])
        tot = sb("tot", [P, 2, 3])
        tern1 = sb("tern1", [P, 2, HID], F32R)
        tern2 = sb("tern2", [P, NC, D], F32R)
        gsum = sb("gsum", [P, 3])
        gamma = sb("gamma", [P, 2])
        half = sb("half", [P, 2])
        nhalf = sb("nhalf", [P, 2])
        idx_s = sb("idx_s", [P, 42], I32)
        wq_s = sb("wq_s", [P, 2, 3 * D])
        phi_h = sb("phi_h", [P, 2, NE * NS], F32R)

        def region(name, *variants):
            views, most = [], 0
            for n, variant in enumerate(variants):
                with ExitStack() as lot:
                    got, size = [], 0
                    for m, (label, shape, dt) in enumerate(variant):
                        t = lot.enter_context(nc.sbuf_tensor(label or f"{name}_gap{n}_{m}", shape, dt))
                        size += int(np.prod(shape[1:])) * (2 if dt == BF16 else 4)
                        if label:
                            got.append(t[tuple(slice(None) for _ in shape)])
                    views.append(got)
                    most = max(most, size)
            sb(f"{name}_region", [P, most // 4])
            return views

        (xn, xT_h, xT_l, xT_s), (hT,) = region(
            "x",
            [("xn", [P, 2, NT, D], F32), ("xT_h", [P, 2, T], F32R), ("xT_l", [P, 2, T], F32R),
             ("xT_s", [P, 2, T], F32R)],
            [("hT", [P, 2, NC * P], F32)])

        expert = [[(f"ew1_{j}", [P, 2, HID], F32), (f"ew2_{j}", [P, NC, D], F32), (f"eb2_{j}", [P, D], F32)]
                  for j in range(RING)]
        weights, (phi_l, wa_l, wa_s), (q3_h, q3_l, wq_h, wq_l) = region(
            "weights",
            [b for e in expert for b in e],
            [(None, [P, RING // 2 * (2 * HID + NC * D + D)], F32), ("phi_l", [P, 2, NE * NS], F32R),
             ("wa_l", [P, 2, 3 * D], F32R), ("wa_s", [P, 2, 3 * D], F32)],
            [("q3_h", [P, 2, 4, T], F32R), ("q3_l", [P, 2, 3, T], F32R), ("wq_h", [P, 2, 3 * D], F32R),
             ("wq_l", [P, 2, 3 * D], F32R)])
        ew1_s, ew2_s, eb2_s = weights[0::3], weights[1::3], weights[2::3]

        SLOTS, CWT = 2 * NE * NB * NS, NB * KC * T
        (prep, (sq, w0_s, w1_s, w2_s, wf_s, i1_s, i2_s), attn, (parts, resid, wa_h), moe, (eok,),
         (y_out, v3_h, v3_l, v3, act1), (sc, sc_h, sc_l, hid_h, hid_l)) = region(
            "main",
            [("diag", [P, KC, P], F32), ("phi_s", [P, 2, NE * NS], F32), ("ss", [P, KC], F32), ("rt", [P, KC], F32),
             ("nw", [P, KC], F32), ("fw1_s", [P, 2, HID], F32), ("fw2_s", [P, NC, D], F32),
             ("neg1", [P, 2, HID], F32), ("neg2", [P, NC, D], F32),
             ("g0", [P, 2, GP, NB, 3], F32), ("g1", [P, 8, NB, 12], F32), ("g2", [P, 2, NB, 48], F32),
             ("r0", [P, 2, NB, GP, 3], F32), ("r1", [P, NB, 8, 12], F32), ("r2", [P, NB, 2, 48], F32),
             ("f0", [48, 2, NB * P], F32), ("f1", [FC, NB, 2, 64], F32), ("f2", [FC, NB, 8, 16], F32),
             ("o0", [64, 2, NB, P], F32), ("o1", [64, NB, 64], F32), ("o2", [64, NB, 16], F32),
             ("z1", [64, NB, D], F32), ("z2", [16, NB, D], F32)],
            [(None, [P, SLOTS + CWT], F32), ("sq", [P, 2, NE * NS], F32),
             ("w0_s", [48, 64], F32), ("w1_s", [FC, 2, 64], F32), ("w2_s", [FC, 8, 64], F32),
             ("wf_s", [64, 3, D], F32), ("i1_s", [64, 256], F32), ("i2_s", [16, 256], F32)],
            [("qs", [P, 2, HEADS, T], BF16), ("ks", [P, 2, HEADS, T], BF16), ("att", [P, 2 * HG, 2, T], F32),
             ("oT", [P, NG, T], F32), ("vpad", [P, 3, NT, HEADS, 2 * HS], F32)],
            [(None, [P, SLOTS + CWT], F32), ("parts", [P, 2, 3, 3, T], BF16), ("resid", [P, 2, T], F32),
             ("wa_h", [P, 2, 3 * D], F32R)],
            [("slotsT", [P, 2, NE, NB, NS], F32), ("cwT", [P, NB, KC, T], F32), ("ex", [P, 2, NE, NS], F32),
             ("dw", [P, 2, NE, NS], F32), ("cw", [P, 2, NE, NS], F32)],
            [(None, [P, SLOTS + CWT], F32), ("eok", [P, KC, NB, D], F32)],
            [("y_out", [P, NB, NT, D], F32), ("v3_h", [P, 3, NT, D], F32R), ("v3_l", [P, 3, NT, D], F32R),
             ("v3", [P, NT, D], F32), ("act1", [P, 4, T], F32)],
            [(None, [P, SLOTS], F32), ("sc", [P, 2, T], F32), ("sc_h", [P, 2, 2, T], F32R),
             ("sc_l", [P, 2, 2, T], F32R), ("hid_h", [P, 2, NC, T], F32R), ("hid_l", [P, 2, NC, T], F32R)])
        (diag, phi_s, ss, rt, nw, fw1_s, fw2_s, neg1, neg2, g0, g1, g2, r0, r1, r2, f0, f1, f2, o0, o1, o2, z1,
         z2) = prep
        qs, ks, att, oT, vpad = attn
        slotsT, cwT, ex, dw, cw = moe

        def raw(ap):
            return ap.bitcast(F32)

        ps = [ctx.enter_context(nc.psum_tensor(f"ps{k}", [P, 512], F32)) for k in range(8)]

        bank_full = [sem(f"bank_full{k}") for k in range(8)]
        bank_drained = [sem(f"bank_drained{k}") for k in range(8)]
        idx_in, tok_in, txt_in, phi_in_s, tern_in, attn_in, layer1_in = (
            sem(n) for n in ("idx_in", "tok_in", "txt_in", "phi_in", "tern_in", "attn_in", "layer1_in"))
        gathered = [[sem(f"gathered0_{v}") for v in range(2)], sem("gathered1"), sem("gathered2")]
        regrouped = sem("regrouped")
        cleared = sem("cleared")
        phi_sq, phi_ss, phi_root, phi_diag, phi_scaled, phi_high, phi_ready = (
            sem(n) for n in ("phi_sq", "phi_ss", "phi_root", "phi_diag", "phi_scaled", "phi_high", "phi_ready"))
        abs_sums = sem("abs_sums")
        wa_ready, wq_ready = sem("wa_ready"), sem("wq_ready")
        q3_h_ready, v3_ready, v3_h_ready, v3_parts, sc_ready, sc_h_ready, sc_parts, hid_h_ready = (
            sem(n) for n in ("q3_h_ready", "v3_ready", "v3_h_ready", "v3_parts", "sc_ready", "sc_h_ready", "sc_parts",
                             "hid_h_ready"))
        hid_parts = [sem(f"hid_parts{k}") for k in range(2)]
        dve_chain, pool_chain = sem("dve_chain"), sem("pool_chain")
        stats_ready, rstd_ready = ([sem(f"{n}{b}") for b in range(NB)] for n in ("stats_ready", "rstd_ready"))
        xn_ready, xT_h_ready = ([sem(f"{n}{r}") for r in range(2)] for n in ("xn_ready", "xT_h_ready"))
        part1_ready, resid_ready, part2_ready, parts_ready = (
            sem(n) for n in ("part1_ready", "resid_ready", "part2_ready", "parts_ready"))
        parts_out = sem("parts_out")
        stacks_in = [sem(f"stacks_in{r}") for r in range(2)]
        shifted, exps_ready, rsum_ready, total_ready, dw_ready, cw_ready = (
            sem(n) for n in ("shifted", "exps_ready", "rsum_ready", "total_ready", "dw_ready", "cw_ready"))
        ones_row = sem("ones_row")
        landed = [sem(f"weights_landed{j}") for j in range(RING)]
        slot_free = [sem(f"weights_free{j}") for j in range(RING)]
        hid_full, hid_done, eo_full, eo_drained = (sem(n) for n in ("hid_full", "hid_done", "eo_full", "eo_drained"))
        h_biased = sem("h_biased")
        out_ready, stored = sem("out_ready"), sem("stored")

        def refill(pe, job):
            bank, n = use[job]
            if n > 1:
                pe.wait_ge(bank_drained[bank], n - 1)
            return ps[bank]

        def filled(inst, job):
            inst.then_inc(bank_full[use[job][0]], 1)

        def await_fill(eng, job):
            bank, n = use[job]
            eng.wait_ge(bank_full[bank], n)
            return ps[bank]

        def drained(inst, job):
            inst.then_inc(bank_drained[use[job][0]], 1)

        def await_drain(eng, job):
            bank, n = use[job]
            eng.wait_ge(bank_drained[bank], n)

        def turn_number(layer, b):
            return (NB * layer + b) // 2 + 1

        def await_xn_free(eng, layer, b):
            n = NB * layer + b - 2
            if n >= 0:
                layer, b = divmod(n, NB)
                await_fill(eng, ("slots", b, 2) if layer == 1 else ("xT", layer, b, 1))

        def chunked(w, rows=P):
            return w.rearrange("(c p) n -> p c n", p=rows)

        block = ctx.enter_context(nc.Block())

        @block.sync
        def _(sp):
            sp.dma_start(idx_s[:, :], idx).then_inc(idx_in, 16)
            sp.dma_start(phi_s, chunked(phi_in)).then_inc(phi_in_s, 16)
            sp.dma_start(scale_c[:, :], scale_in.partition_broadcast(P)).then_inc(phi_in_s, 16)
            sp.dma_start(fw1_s, chunked(fw1)).then_inc(tern_in, 16)
            sp.dma_start(fw2_s, fw2.rearrange("(c p) n -> p c n", p=P)).then_inc(tern_in, 16)
            sp.dma_start(ident[:, :], ident_in).then_inc(tok_in, 16)
            sp.dma_start(w0_s, w0).then_inc(tok_in, 16)
            sp.dma_start(w1_s, chunked(w1t, FC)).then_inc(tok_in, 16)
            sp.dma_start(w2_s, chunked(w2t, FC)).then_inc(tok_in, 16)
            sp.dma_start(wf_s, chunked(wf, 64)).then_inc(tok_in, 16)
            sp.dma_start(i1_s, interp1).then_inc(tok_in, 16)
            sp.dma_start(i2_s, interp2).then_inc(tok_in, 16)
            sp.dma_start(tokb_c[0:64, :], tok_b).then_inc(tok_in, 16)
            sp.dma_start(bias_row[:, 1, :], bf.partition_broadcast(P)).then_inc(tok_in, 16)
            sp.dma_start(h[:, :, NT - 1, :], txt.rearrange("b t d -> t b d")).then_inc(txt_in, 16)
            sp.dma_start(wa_s, chunked(wa)).then_inc(attn_in, 16)
            sp.dma_start(baqk_c, ba_qk).then_inc(attn_in, 16)
            sp.dma_start(bias_row[:, 0, :], ba_v.partition_broadcast(P)).then_inc(attn_in, 16)
            sp.dma_start(causal[:, :, :], causal_in).then_inc(attn_in, 16)
            sp.dma_start(wq_s[:, :, :], chunked(wq)).then_inc(layer1_in, 16)
            sp.dma_start(bqqk_c, bq_qk).then_inc(layer1_in, 16)
            sp.dma_start(bias_row[:, 2, :], bq_v.partition_broadcast(P)).then_inc(layer1_in, 16)
            sp.dma_start(bias_row[:, 3, :], fb2.partition_broadcast(P)).then_inc(layer1_in, 16)
            sp.dma_start(fb1_c[:, :], fb1).then_inc(layer1_in, 16)
            sp.dma_start(decay[:, :], decay_in).then_inc(layer1_in, 16)

            def load_expert(e, j):
                sp.dma_start(ew1_s[j][:, 0, :], ew1[bass.ds(e, 1), 0:P, :].rearrange("e p n -> p (e n)")
                             ).then_inc(landed[j], 16)
                sp.dma_start(ew1_s[j][0:DR, 1, :], ew1[bass.ds(e, 1), P:D, :].rearrange("e p n -> p (e n)")
                             ).then_inc(landed[j], 16)
                sp.dma_start(ew1_s[j][DR:DR + 1, 1, :], eb1[bass.ds(e, 1), :]).then_inc(landed[j], 16)
                sp.dma_start(ew2_s[j][:, :, :], ew2[bass.ds(e, 1)].rearrange("e (c p) n -> p (e c) n", p=P)
                             ).then_inc(landed[j], 16)
                sp.dma_start(eb2_s[j][:, :], eb2[bass.ds(e, 1), :].partition_broadcast(P)
                             ).then_inc(landed[j], 16)

            for b in range(NB):
                r = b % 2
                sp.wait_ge(parts_ready, 3 * b + 1)
                sp.dma_start(q_dram[b, :, 0:P].rearrange("s p t -> p s t"), parts[:, r, 0, :, :]
                             ).then_inc(parts_out, 16)
                sp.wait_ge(parts_ready, 3 * b + 2)
                sp.dma_start(q_dram[b, :, P:D].rearrange("s p t -> p s t"), parts[0:DR, r, 1, :, :]
                             ).then_inc(parts_out, 16)
                for to, n in ((0, 3), (3, 2)):
                    sp.dma_start(k_dram[b, to:to + n, 0:DR].rearrange("s p t -> p s t"),
                                 parts[DR:P, r, 1, 0:n, :]).then_inc(parts_out, 16)
                sp.wait_ge(parts_ready, 3 * b + 3)
                for to, n in ((0, 3), (3, 2)):
                    sp.dma_start(k_dram[b, to:to + n, DR:D].rearrange("s p t -> p s t"),
                                 parts[:, r, 2, 0:n, :]).then_inc(parts_out, 16)
                sp.wait_ge(parts_out, 96 * (b + 1))
                if b >= 2:
                    await_fill(sp, ("far", b - 2, HEADS - 1))
                for slot, qp, kp, n in PRODUCTS:
                    for to, dram, part in ((qs, q_dram, qp), (ks, k_dram, kp)):
                        sp.dma_start(
                            to[HS * slot:HS * (slot + n), r, :, :],
                            dram[b, part:part + n].rearrange("s (d h) t -> (s d) h t", d=HS),
                        ).then_inc(stacks_in[r], 16)
            for j in range(RING // 2):
                load_expert(j, j)
            await_fill(sp, ("logits", NB * NT - 1, 1))
            for j in range(RING // 2, RING):
                load_expert(j, j)
            with sp.Fori(1, NE // RING) as it:
                for j in range(RING):
                    sp.wait_ge(slot_free[j], it)
                    load_expert(it * RING + j, j)
            for b in range(NB):
                for first, n in ((0, NT),) if b < NB - 1 else ((0, 2), (2, 1)):
                    sp.wait_ge(out_ready, NT * b + first + n)
                    sp.dma_start(out[b, P * first:P * (first + n)].rearrange("(t p) d -> p t d", p=P),
                                 y_out[:, b, first:first + n, :]).then_inc(stored, 16)
            sp.wait_ge(stored, 16 * (NB + 1))

        @block.gpsimd
        def _(pool):
            chain = [0]

            def link(inst):
                chain[0] += 1
                inst.then_inc(pool_chain, 1)
                pool.wait_ge(pool_chain, chain[0])

            pool.memset(ones[:, :], 1.0).then_inc(cleared, 1)
            pool.memset(mhalf[:, :], -0.5).then_inc(cleared, 1)
            pool.wait_ge(idx_in, 16)
            for j in range(2):
                pool.indirect_dma_start(g2[:, j, :, :].rearrange("p b f -> p (b f)"), None, x2,
                                        bass.IndirectOffsetOnAxis(ap=idx_s[:, 40 + j:41 + j], axis=0)
                                        ).then_inc(gathered[2], 16)
            for j in range(8):
                pool.indirect_dma_start(g1[:, j, :, :].rearrange("p b f -> p (b f)"), None, x1,
                                        bass.IndirectOffsetOnAxis(ap=idx_s[:, 32 + j:33 + j], axis=0)
                                        ).then_inc(gathered[1], 16)
            for j in range(32):
                pool.indirect_dma_start(g0[:, j // GP, j % GP, :, :].rearrange("p b f -> p (b f)"), None, x0,
                                        bass.IndirectOffsetOnAxis(ap=idx_s[:, j:j + 1], axis=0)
                                        ).then_inc(gathered[0][j // GP], 16)
            pool.memset(vpad, 0.0).then_inc(cleared, 1)

            def do_stats(layer, b):
                pool.wait_ge(stats_ready[b], layer + 1)
                pool.tensor_tensor(rstd[:, b, :], veps[:, b, :], mhalf[:, :], ALU.pow).then_inc(rstd_ready[b], 1)

            def do_qkv(b):
                for m in range(3):
                    n = 3 * b + m
                    pool.wait_ge(part2_ready, n + 1)
                    pool.tensor_tensor(parts[:, b % 2, m, 2, :], resid[:, n % 2, :], parts[:, b % 2, m, 1, :],
                                       ALU.subtract).then_inc(parts_ready, 1)

            def do_weigh(u):
                r = u % 2
                pool.wait_ge(rsum_ready, u + 1)
                if u >= 2:
                    await_fill(pool, ("cwT", u - 2, 1))
                for v in range(2):
                    some = slice(16 * v, 16 * v + 16)
                    pool.tensor_tensor(dw[:, r, some, :], ex[:, r, some, :],
                                       sm[:, r, 3, some].unsqueeze(2).to_broadcast([P, 16, NS]), ALU.mult
                                       ).then_inc(dw_ready, 1)
                pool.wait_ge(total_ready, u + 1)
                link(pool.tensor_scalar(sm[:, r, 5, :], sm[:, r, 1, :], tot[:, r, 2:3], None, ALU.mult))
                pool.tensor_tensor(cw[:, r, :, :], ex[:, r, :, :],
                                   sm[:, r, 5, :].unsqueeze(2).to_broadcast([P, NE, NS]), ALU.mult
                                   ).then_inc(cw_ready, 1)
                if u == 1:
                    pool.wait_ge(cw_ready, u + 1)
                    await_fill(pool, ("join", NB - 1, NT - 1))
                    pool.memset(slotsT[DR:DR + 1, 1, :, :, :], 1.0).then_inc(ones_row, 1)
                    pool.wait_ge(ones_row, 1)

            def do_v3(b):
                for t in range(NT):
                    pool.wait_ge(v3_h_ready, NT * b + t + 1)
                    pool.tensor_tensor(v3_l[:, b % 3, t, :], v3[:, t, :], raw(v3_h[:, b % 3, t, :]), ALU.subtract
                                       ).then_inc(v3_parts, 1)

            def do_score(b):
                for v in range(2):
                    pool.wait_ge(sc_h_ready, 2 * b + v + 1)
                    pool.tensor_tensor(sc_l[:, b % 2, v, :], sc[:, v, :], raw(sc_h[:, b % 2, v, :]), ALU.subtract
                                       ).then_inc(sc_parts, 1)

            def do_hidden(b):
                pool.wait_ge(xn_ready[b % 2], NT * turn_number(3, b))
                for t in range(NT):
                    pool.tensor_tensor(h[:, b, t, :], h[:, b, t, :], bias_row[:, 3, :], ALU.add).then_inc(h_biased, 1)
                for m in range(0, NC, 2):
                    pool.wait_ge(hid_h_ready, NC * b + m + 1)
                    pool.tensor_tensor(hid_l[:, b % 2, m, :], act1[:, (NC * b + m) % 4, :],
                                       raw(hid_h[:, b % 2, m, :]), ALU.subtract).then_inc(hid_parts[0], 1)

            for s in before + after:
                f = {"stats": do_stats, "qkv": do_qkv, "weigh": do_weigh, "v3": do_v3, "score": do_score,
                     "hidden": do_hidden}.get(s[0])
                if f:
                    f(*s[1:])

        @block.scalar
        def _(act):
            def do_phi_norms():
                act.wait_ge(phi_in_s, 32)
                act.activation(sq, phi_s, ACT.Square).then_inc(phi_sq, 1)
                act.wait_ge(phi_ss, 1)
                act.activation(rt, ss, ACT.Sqrt).then_inc(phi_root, 1)

            def do_phi():
                act.wait_ge(phi_scaled, 4)
                act.copy(phi_h[:, :, :], phi_s).then_inc(phi_high, 1)

            def do_coarse():
                act.wait_ge(tok_in, 16 * 9)
                p = await_fill(act, ("o2",))
                drained(act.activation(o2, p[0:64, 0:64].rearrange("e (b n) -> e b n", b=NB), ACT.Identity,
                                       bias=tokb_c[0:64, 2:3]), ("o2",))
                p = await_fill(act, ("o1",))
                drained(act.activation(o1, p[0:64, 0:256].rearrange("e (b n) -> e b n", b=NB), ACT.Identity,
                                       bias=tokb_c[0:64, 1:2]), ("o1",))
                for v in range(2):
                    p = await_fill(act, ("z2", v))
                    drained(act.copy(z2[:, 2 * v:2 * v + 2, :], p[0:16, 0:2 * D].rearrange("n (b d) -> n b d", b=2)),
                            ("z2", v))
                for v in range(2):
                    p = await_fill(act, ("z1", v))
                    drained(act.copy(z1[:, 2 * v:2 * v + 2, :], p[0:64, 0:2 * D].rearrange("n (b d) -> n b d", b=2)),
                            ("z1", v))

            def do_own(v):
                p = await_fill(act, ("o0", v))
                drained(act.activation(o0[:, v, :, :], p[0:64, :].rearrange("e (b n) -> e b n", b=NB),
                                       ACT.Identity, bias=tokb_c[0:64, 0:1]), ("o0", v))

            def do_turn(layer, b, *chunk):
                for c in chunk or range(2):
                    p = await_fill(act, ("xT", layer, b, c))
                    if c == 0:
                        act.copy(xT_h[:, b % 2, :], p[:, 0:T]).then_inc(xT_h_ready[b % 2], 1)
                    else:
                        act.copy(xT_s[0:DR, b % 2, :], p[0:DR, 0:T]).then_inc(xT_h_ready[b % 2], 1)

            def part2(b, m):
                act.wait_ge(resid_ready, 3 * b + m + 1)
                act.copy(parts[:, b % 2, m, 1, :], resid[:, (3 * b + m) % 2, :]).then_inc(part2_ready, 1)

            def do_qkv(b):
                act.wait_ge(attn_in, 64)
                for m in range(3):
                    p = await_fill(act, ("qkv", b, m))
                    if b >= 2 and m == 0:
                        act.wait_ge(parts_out, 96 * (b - 1))
                    act.activation(parts[:, b % 2, m, 0, :], p[:, 0:T], ACT.Identity, bias=baqk_c[:, m:m + 1]
                                   ).then_inc(part1_ready, 1)
                    if m:
                        part2(b, m - 1)

            def do_v(b):
                part2(b, 2)

            def do_attend(b, g):
                if g < NG:
                    for hd in range(HG * g, HG * g + HG):
                        p = await_fill(act, ("far", b, hd))
                        drained(act.activation(att[:, hd % (2 * HG), 1, :], p[:, 0:T], ACT.Relu,
                                               scale=float(HS) ** -0.5), ("far", b, hd))
                if g:
                    p = await_fill(act, ("mix", b, g - 1))
                    if g == 1 and b:
                        await_fill(act, ("join", b - 1, NT - 1))
                    drained(act.copy(oT[:, g - 1, :], p[:, 0:T]), ("mix", b, g - 1))

            def do_peak(u):
                act.wait_ge(shifted, u + 1)
                act.activation(sm[:, u % 2, 1, :], sm[:, u % 2, 0, :], ACT.Exp, bias=tot[:, u % 2, 0:1]
                               ).then_inc(exps_ready, 1)
                act.activation(ex[:, u % 2, :, :], ex[:, u % 2, :, :], ACT.Exp).then_inc(exps_ready, 1)

            def do_shares_out(u):
                b, t = divmod(u, NT)
                p = await_fill(act, ("cwT", u, 0))
                drained(act.copy(cwT[:, b, 0:4, P * t:P * t + P], p[:, :].rearrange("p (k n) -> p k n", k=4)),
                        ("cwT", u, 0))

            def do_slots_out(b):
                for v in range(2):
                    job = ("slots", b, v)
                    p = await_fill(act, job)
                    drained(act.copy(slotsT[:, 0, 16 * v:16 * v + 16, b, :],
                                     p[:, :].rearrange("p (e s) -> p e s", s=NS)), job)
                if b < NB - 1:
                    job = ("slots", b, 2)
                    p = await_fill(act, job)
                    for v in range(2):
                        inst = act.copy(slotsT[0:DR, 1, 16 * v:16 * v + 16, b, :],
                                        p[DR * v:DR * v + DR, :].rearrange("p (e s) -> p e s", s=NS))
                    drained(inst, job)

            def do_experts():
                def gelu(e, j):
                    act.wait_ge(hid_full, e + 1)
                    act.activation(hT[:, j % 2, 0:T], ps[2 * (j % 2)][:, 0:T], ACT.Gelu)
                    act.activation(hT[:, j % 2, T:2 * T], ps[2 * (j % 2) + 1][:, 0:T], ACT.Gelu).then_inc(hid_done, 1)

                with act.Fori(0, NE // RING) as it:
                    for j in range(RING):
                        gelu(it * RING + j, j)

            def do_qkv3(b):
                act.wait_ge(layer1_in, 96)
                for m in range(3):
                    p = await_fill(act, ("qkv3", b, m))
                    for to, rows, at in (((0, slice(0, P), slice(0, P)),), 
                                         ((1, slice(0, DR), slice(0, DR)), (3, slice(0, DR), slice(DR, P)),
                                          (3, slice(DR, P), slice(DR, P))),
                                         ((2, slice(0, P), slice(0, P)),))[m]:
                        inst = act.activation(q3_h[rows, b % 2, to, :], p[at, 0:T], ACT.Identity,
                                              bias=bqqk_c[at, m:m + 1])
                    inst.then_inc(q3_h_ready, 1)

            def do_v3(b):
                for t in range(NT):
                    act.wait_ge(v3_ready, NT * b + t + 1)
                    act.copy(v3_h[:, b % 3, t, :], v3[:, t, :]).then_inc(v3_h_ready, 1)

            def do_score(b):
                for v in range(2):
                    act.wait_ge(sc_ready, 2 * b + v + 1)
                    act.copy(sc_h[:, b % 2, v, :], sc[:, v, :]).then_inc(sc_h_ready, 1)

            def do_hidden(b):
                for m in range(NC):
                    p = await_fill(act, ("hidden", b, m))
                    n = NC * b + m
                    if n >= 4:
                        act.wait_ge(hid_parts[m % 2], n // 2 - 1)
                    drained(act.activation(act1[:, (NC * b + m) % 4, :], p[:, 0:T], ACT.Gelu, bias=fb1_c[:, m:m + 1],
                                           scale=gamma[:, 0:1]), ("hidden", b, m))

            table = {"phi_norms": do_phi_norms, "phi": do_phi, "coarse": do_coarse, "own": do_own,
                     "turn_h": do_turn, "qkv": do_qkv, "attend": do_attend, "peak": do_peak,
                     "shares_out": do_shares_out, "slots_out": do_slots_out, "v": do_v, "v3": do_v3,
                     "qkv3": do_qkv3, "score": do_score, "hidden": do_hidden}
            for s in before:
                if s[0] in table:
                    table[s[0]](*s[1:])
            do_experts()
            for s in after:
                if s[0] in table:
                    table[s[0]](*s[1:])

        @block.vector
        def _(dve):
            chain = [0]

            def link(inst):
                chain[0] += 1
                inst.then_inc(dve_chain, 1)
                return chain[0]

            def settle(n=None):
                dve.wait_ge(dve_chain, n or chain[0])

            def do_phi_norms():
                p = await_fill(dve, ("phi", 0))
                drained(dve.tensor_scalar(ss, p[:, 0:KC], L2_EPS * L2_EPS, None, ALU.max), ("phi", 0))
                await_drain(dve, ("phi", 0))
                dve.nop().then_inc(phi_ss, 1)
                dve.wait_ge(phi_root, 1)
                link(dve.reciprocal(rt, rt))
                settle()
                link(dve.tensor_tensor(nw, rt, rt, ALU.mult))
                settle()
                link(dve.tensor_tensor(nw, nw, ss, ALU.mult))
                settle()
                link(dve.tensor_scalar(nw, nw, -0.5, 1.5, ALU.mult, ALU.add))
                settle()
                link(dve.scalar_tensor_tensor(out=nw, in0=rt, scalar=scale_c, in1=nw, op0=ALU.mult, op1=ALU.mult))
                settle()
                dve.wait_ge(tok_in, 16 * 9)
                dve.tensor_tensor(diag, ident[:, :].unsqueeze(1).to_broadcast([P, KC, P]),
                                  nw.unsqueeze(2).to_broadcast([P, KC, P]), ALU.mult).then_inc(phi_diag, 1)

            def do_phi():
                for v in range(2):
                    p = await_fill(dve, ("phi", 1 + v))
                    for c in range(2):
                        part = phi_s[:, c, 512 * v:512 * v + 512]
                        inst = dve.tensor_tensor(part, part, p[:, :], ALU.mult).then_inc(phi_scaled, 1)
                    dve.wait_ge(phi_scaled, 2 * (v + 1))
                    dve.nop().then_inc(bank_drained[use[("phi", 1 + v)][0]], 1)
                dve.wait_ge(phi_high, 1)
                dve.tensor_tensor(phi_l, phi_s, raw(phi_h[:, :, :]), ALU.subtract).then_inc(phi_ready, 1)

            def do_abs_sums():
                dve.wait_ge(tern_in, 32)
                dve.tensor_reduce(gsum[:, 0:2], fw1_s, AX.X, ALU.add, apply_absolute_value=True
                                  ).then_inc(abs_sums, 1)
                dve.tensor_reduce(gsum[:, 2:3], fw2_s, AX.XY, ALU.add, apply_absolute_value=True
                                  ).then_inc(abs_sums, 1)

            def do_ternary():
                p = await_fill(dve, ("gamma",))
                drained(dve.tensor_scalar(gamma[:, :], p[:, 0:2], 1.0 / (D * HID), TQ_EPS, ALU.mult, ALU.add),
                        ("gamma",))
                await_drain(dve, ("gamma",))
                link(dve.tensor_scalar(half[:, :], gamma[:, :], 0.5, None, ALU.mult))
                link(dve.tensor_scalar(nhalf[:, :], gamma[:, :], -0.5, None, ALU.mult))
                settle()
                link(dve.tensor_scalar(neg1, fw1_s, nhalf[:, 0:1], None, ALU.is_lt))
                link(dve.tensor_scalar(neg2, fw2_s, nhalf[:, 1:2], None, ALU.is_lt))
                settle()
                link(dve.scalar_tensor_tensor(out=tern1[:, :, :], in0=fw1_s, scalar=half[:, 0:1], in1=neg1,
                                              op0=ALU.is_gt, op1=ALU.subtract))
                link(dve.scalar_tensor_tensor(out=tern2[:, :, :], in0=fw2_s, scalar=half[:, 1:2], in1=neg2,
                                              op0=ALU.is_gt, op1=ALU.subtract))
                settle()

            def do_split_wa():
                dve.wait_ge(attn_in, 64)
                link(dve.tensor_copy(wa_h, wa_s))
                settle()
                dve.tensor_tensor(wa_l, wa_s, raw(wa_h), ALU.subtract).then_inc(wa_ready, 1)

            def do_split_wq():
                dve.wait_ge(layer1_in, 96)
                link(dve.tensor_copy(wq_h, wq_s[:, :, :]))
                settle()
                dve.tensor_tensor(wq_l, wq_s[:, :, :], raw(wq_h), ALU.subtract).then_inc(wq_ready, 1)

            def do_coarse():
                dve.wait_ge(gathered[2], 32)
                dve.tensor_copy(r2.rearrange("p b j f -> p j b f"), g2).then_inc(regrouped, 1)
                dve.wait_ge(gathered[1], 128)
                dve.tensor_copy(r1.rearrange("p b j f -> p j b f"), g1).then_inc(regrouped, 1)
                p = await_fill(dve, ("f2",))
                drained(dve.tensor_copy(f2, p[0:FC, :].rearrange("f (b g n) -> f b g n", b=NB, g=8)), ("f2",))
                p = await_fill(dve, ("f1",))
                drained(dve.tensor_copy(f1, p[0:FC, :].rearrange("f (b g n) -> f b g n", b=NB, g=2)), ("f1",))

            def do_fine(v):
                dve.wait_ge(gathered[0][v], 16 * GP)
                dve.tensor_copy(r0[:, v, :, :, :].rearrange("p b j f -> p j b f"), g0[:, v, :, :, :]
                                ).then_inc(regrouped, 1)
                p = await_fill(dve, ("f0", v))
                drained(dve.tensor_copy(f0[:, v, :], p[0:48, :]), ("f0", v))

            def do_fuse(b, v):
                p = await_fill(dve, ("y", b, v))
                drained(dve.tensor_tensor(h[:, b, v, :], p[:, 0:D], bias_row[:, 1, :], ALU.add), ("y", b, v))

            def do_early_stats(b):
                dve.wait_ge(txt_in, 16)
                await_drain(dve, ("y", b, 0))
                for t in (0, 2):
                    link(dve.bn_stats(st6[:, b, t, :], h[:, b, t, :]))

            def do_stats(layer, b):
                if layer:
                    dve.wait_ge(xn_ready[b % 2], turn_number(layer - 1, b) * NT)
                if layer == 0:
                    await_drain(dve, ("y", b, 1))
                else:
                    kind = {1: "join", 2: "combine", 3: "read"}[layer]
                    for t in range(NT):
                        await_drain(dve, (kind, b, t))
                for t in range(NT) if layer else (1,):
                    link(dve.bn_stats(st6[:, b, t, :], h[:, b, t, :]))
                settle()
                for t in range(NT):
                    link(dve.bn_aggr(mv[:, b, t, :], st6[:, b, t, :]))
                settle()
                var = mv[:, b, :, 1]
                if layer == 1:
                    link(dve.tensor_scalar(vlen[:, :], var, LN_EPS, L2_EPS * L2_EPS, ALU.add, ALU.mult))
                    settle()
                    dve.scalar_tensor_tensor(out=veps[:, b, :], in0=var, scalar=float(D), in1=vlen[:, :], op0=ALU.mult,
                                             op1=ALU.max).then_inc(stats_ready[b], 1)
                else:
                    dve.tensor_scalar(veps[:, b, :], var, LN_EPS, None, ALU.add).then_inc(stats_ready[b], 1)

            def do_norm(layer, b):
                dve.wait_ge(rstd_ready[b], layer + 1)
                await_xn_free(dve, layer, b)
                for t in range(NT):
                    dve.tensor_scalar(xn[:, b % 2, t, :], h[:, b, t, :], mv[:, b, t, 0:1],
                                      rstd[:, b, t:t + 1], ALU.subtract, ALU.mult).then_inc(xn_ready[b % 2], 1)

            def do_turn(layer, b, *chunk):
                r = b % 2
                for c in chunk or range(2):
                    job = ("xT", layer, b, c)
                    p = await_fill(dve, job)
                    dve.wait_ge(xT_h_ready[b % 2], 2 * turn_number(layer, b) + c - 1)
                    if c == 0:
                        drained(dve.tensor_tensor(xT_l[:, r, :], p[:, 0:T], raw(xT_h[:, r, :]), ALU.subtract), job)
                    else:
                        drained(dve.tensor_tensor(xT_s[DR:P, r, :], p[0:DR, 0:T], raw(xT_s[0:DR, r, :]),
                                                  ALU.subtract), job)

            def do_qkv(b):
                dve.wait_ge(attn_in, 64)
                for m in range(3):
                    n = 3 * b + m
                    job = ("qkv", b, m)
                    p = await_fill(dve, job)
                    dve.wait_ge(part1_ready, n + 1)
                    if n >= 2:
                        dve.wait_ge(parts_ready, n - 1)
                    inst = dve.scalar_tensor_tensor(out=resid[:, n % 2, :], in0=p[:, 0:T],
                                                    scalar=baqk_c[:, m:m + 1], in1=parts[:, b % 2, m, 0, :],
                                                    op0=ALU.add, op1=ALU.subtract)
                    drained(inst, job)
                    await_drain(dve, job)
                    dve.nop().then_inc(resid_ready, 1)

            def do_v(b):
                if b == 0:
                    dve.wait_ge(cleared, 3)
                for t in range(NT):
                    job = ("v", b, t)
                    p = await_fill(dve, job)
                    drained(dve.tensor_tensor(vpad[:, b % 3, t, :, 0:HS],
                                              p[:, 0:D].rearrange("p (h d) -> p h d", d=HS),
                                              bias_row[:, 0, :].rearrange("p (h d) -> p h d", d=HS), ALU.add), job)

            def do_attend(b, g):
                for hd in range(HG * g, min(HG * g + HG, HEADS)):
                    job = ("near", b, hd)
                    p = await_fill(dve, job)
                    drained(dve.scalar_tensor_tensor(out=att[:, hd % (2 * HG), 0, :], in0=p[:, 0:T], scalar=0.0,
                                                     in1=causal[:, :, :].rearrange("p a q -> p (a q)"),
                                                     op0=ALU.max, op1=ALU.mult), job)

            def do_join(b):
                for t in range(NT):
                    job = ("join", b, t)
                    p = await_fill(dve, job)
                    hv = h[:, b, t, :].rearrange("p (h d) -> p h d", d=HS)
                    drained(dve.tensor_tensor(hv, p[:, 0:T].rearrange("p (h d) -> p h d", d=2 * HS)[:, :, 0:HS],
                                              hv, ALU.add), job)

            def do_peak(u):
                r = u % 2
                p0 = await_fill(dve, ("logits", u, 0))
                link(dve.tensor_reduce(sm[:, r, 0, 0:16], p0[:, :].rearrange("p (e s) -> p e s", s=NS), AX.X, ALU.max))
                p1 = await_fill(dve, ("logits", u, 1))
                link(dve.tensor_reduce(sm[:, r, 0, 16:32], p1[:, :].rearrange("p (e s) -> p e s", s=NS), AX.X,
                                       ALU.max))
                settle()
                link(dve.tensor_reduce(tot[:, r, 0:1], sm[:, r, 0, :], AX.X, ALU.max, negate=True))
                if u >= 2:
                    dve.wait_ge(cw_ready, u - 1)
                for v, p in enumerate((p0, p1)):
                    drained(dve.tensor_tensor(ex[:, r, 16 * v:16 * v + 16, :],
                                              p[:, :].rearrange("p (e s) -> p e s", s=NS),
                                              sm[:, r, 0, 16 * v:16 * v + 16].unsqueeze(2).to_broadcast([P, 16, NS]),
                                              ALU.subtract), ("logits", u, v))
                await_drain(dve, ("logits", u, 0))
                await_drain(dve, ("logits", u, 1))
                settle()
                dve.nop().then_inc(shifted, 1)

            def do_weigh(u):
                r = u % 2
                dve.wait_ge(exps_ready, 2 * (u + 1))
                link(dve.tensor_reduce(sm[:, r, 2, :], ex[:, r, :, :], AX.X, ALU.add))
                settle()
                dve.reciprocal(sm[:, r, 3, :], sm[:, r, 2, :]).then_inc(rsum_ready, 1)
                link(dve.tensor_tensor_reduce(sm[:, r, 4, :], sm[:, r, 1, :], sm[:, r, 2, :], 1.0, 0.0, ALU.mult,
                                              ALU.add, tot[:, r, 1:2]))
                settle()
                dve.reciprocal(tot[:, r, 2:3], tot[:, r, 1:2]).then_inc(total_ready, 1)

            def do_shares_out(u):
                b, t = divmod(u, NT)
                p = await_fill(dve, ("cwT", u, 1))
                drained(dve.tensor_copy(cwT[:, b, 4:8, P * t:P * t + P], p[:, :].rearrange("p (k n) -> p k n", k=4)),
                        ("cwT", u, 1))

            def do_slots_out(b):
                if b == NB - 1:
                    job = ("slots", b, 2)
                    p = await_fill(dve, job)
                    for v in range(2):
                        inst = dve.tensor_copy(slotsT[0:DR, 1, 16 * v:16 * v + 16, b, :],
                                               p[DR * v:DR * v + DR, :].rearrange("p (e s) -> p e s", s=NS))
                    drained(inst, job)

            def do_experts():
                dve.nop().then_inc(eo_drained, 2)
                with dve.Fori(0, NE // RING) as it:
                    for j in range(RING):
                        dve.wait_ge(eo_full, it * RING + j + 1)
                        for b in range(NB):
                            inst = dve.tensor_tensor(
                                eok[NS * j:NS * j + NS, bass.ds(it, 1), b, :].rearrange("p k d -> p (k d)"),
                                ps[4 + j % 2][NS * b:NS * b + NS, 0:D], eb2_s[j][NS * b:NS * b + NS, :], ALU.add)
                        inst.then_inc(eo_drained, 1)
                        dve.wait_ge(eo_drained, it * RING + j + 3)
                        dve.nop().then_inc(slot_free[j], 1)

            def add_to_h(job, b, t):
                p = await_fill(dve, job)
                drained(dve.tensor_tensor(h[:, b, t, :], p[:, 0:D], h[:, b, t, :], ALU.add), job)

            def do_combine(b, t):
                add_to_h(("combine", b, t), b, t)

            def do_qkv3(b):
                for m in range(3):
                    job = ("qkv3", b, m)
                    p = await_fill(dve, job)
                    dve.wait_ge(q3_h_ready, 3 * b + m + 1)
                    for low, to, high, at in (((q3_l[:, b % 2, 0, :], slice(0, P), 0, slice(0, P)),),
                                              ((q3_h[:, b % 2, 1, :], slice(DR, P), 1, slice(0, DR)),
                                               (q3_l[:, b % 2, 2, :], slice(0, DR), 3, slice(DR, P))),
                                              ((q3_l[:, b % 2, 1, :], slice(0, P), 2, slice(0, P)),))[m]:
                        inst = dve.scalar_tensor_tensor(out=low[to, :], in0=p[at, 0:T], scalar=bqqk_c[at, m:m + 1],
                                                        in1=raw(q3_h[at, b % 2, high, :]), op0=ALU.add,
                                                        op1=ALU.subtract)
                    drained(inst, job)

            def do_v3(b):
                for t in range(NT):
                    job = ("v3", b, t)
                    p = await_fill(dve, job)
                    if b:
                        dve.wait_ge(v3_parts, NT * (b - 1) + t + 1)
                    drained(dve.tensor_tensor(v3[:, t, :], p[:, 0:D], bias_row[:, 2, :], ALU.add), job)
                    await_drain(dve, job)
                    dve.nop().then_inc(v3_ready, 1)

            def do_score(b):
                for v in range(2):
                    job = ("score", b, v)
                    p = await_fill(dve, job)
                    if b:
                        dve.wait_ge(sc_parts, 2 * b + v - 1)
                    if v:
                        link(dve.tensor_tensor(sc[:, 1, 0:2 * P], p[:, 0:2 * P], decay[:, 0:2 * P], ALU.mult))
                        inst = dve.tensor_tensor(sc[:, 1, 2 * P:T], p[:, 2 * P:T], decay[:, 0:P], ALU.mult)
                        settle()
                    else:
                        inst = dve.tensor_tensor(sc[:, 0, :], p[:, 0:T], decay[:, :], ALU.mult)
                    drained(inst, job)
                    await_drain(dve, job)
                    dve.nop().then_inc(sc_ready, 1)

            def do_read(b):
                for t in range(NT):
                    add_to_h(("read", b, t), b, t)

            def do_hidden(b):
                for m in range(NC):
                    await_drain(dve, ("hidden", b, m))
                    dve.tensor_copy(hid_h[:, b % 2, m, :], act1[:, (NC * b + m) % 4, :]).then_inc(hid_h_ready, 1)
                    if m % 2:
                        dve.wait_ge(hid_h_ready, NC * b + m + 1)
                        dve.tensor_tensor(hid_l[:, b % 2, m, :], act1[:, (NC * b + m) % 4, :],
                                          raw(hid_h[:, b % 2, m, :]), ALU.subtract).then_inc(hid_parts[1], 1)

            def do_down(b):
                for t in range(NT):
                    job = ("down", b, t)
                    p = await_fill(dve, job)
                    dve.wait_ge(h_biased, NT * b + t + 1)
                    drained(dve.scalar_tensor_tensor(out=y_out[:, b, t, :], in0=p[:, 0:D], scalar=gamma[:, 1:2],
                                                     in1=h[:, b, t, :], op0=ALU.mult, op1=ALU.add), job)
                    await_drain(dve, job)
                    dve.nop().then_inc(out_ready, 1)

            table = {"phi_norms": do_phi_norms, "phi": do_phi, "abs_sums": do_abs_sums, "ternary": do_ternary,
                     "coarse": do_coarse, "fine": do_fine, "fuse": do_fuse, "split_wa": do_split_wa,
                     "split_wq": do_split_wq, "early_stats": do_early_stats, "stats": do_stats,
                     "norm": do_norm, "turn_l": do_turn, "qkv": do_qkv, "attend": do_attend, "join": do_join,
                     "peak": do_peak, "weigh": do_weigh, "shares_out": do_shares_out,
                     "slots_out": do_slots_out, "v": do_v, "v3": do_v3, "combine": do_combine, "qkv3": do_qkv3,
                     "score": do_score, "read": do_read, "hidden": do_hidden, "down": do_down}
            for s in before:
                if s[0] in table:
                    table[s[0]](*s[1:])
            do_experts()
            for s in after:
                if s[0] in table:
                    table[s[0]](*s[1:])

        @block.tensor
        def _(pe):
            def accumulate(o, pairs):
                for n, (lhsT, rhs) in enumerate(pairs):
                    mm = pe.matmul(o, lhsT, rhs, start=(n == 0), stop=(n == len(pairs) - 1))
                return mm

            def split(one, other):
                (ah, al), (bh, bl) = one, other
                return [(ah, bh), (ah, bl), (al, bh)]

            def five_passes(wh, wl, xh, xl, xs):
                return split((wh[:, 0], wl[:, 0]), (xh, xl)) + [(wh[:, 1], xs), (wl[0:DR, 1], xs[0:DR])]

            def tokens(b, cols):
                return (x[:, b % 2, cols] for x in (xT_h, xT_l, xT_s))

            def flip(pairs):
                return [(x, w) for w, x in pairs]

            def do_phi_norms():
                pe.wait_ge(cleared, 2)
                pe.wait_ge(phi_sq, 1)
                p = refill(pe, ("phi", 0))
                for k in range(KC):
                    mm = accumulate(p[:, k:k + 1], [(sq[0:n, c, P * k:P * k + P], ones[0:n, 0:1])
                                                    for c, n in enumerate((P, DR))])
                filled(mm, ("phi", 0))

            def do_phi():
                pe.wait_ge(phi_diag, 1)
                for v in range(2):
                    p = refill(pe, ("phi", 1 + v))
                    filled(pe.matmul(p[:, :], ones[:, :], diag[:, 4 * v:4 * v + 4, :].rearrange("p k n -> p (k n)"),
                                     start=True, stop=True), ("phi", 1 + v))

            def do_gamma():
                pe.wait_ge(abs_sums, 2)
                p = refill(pe, ("gamma",))
                accumulate(p[:, 0:1], [(ones[:, :], gsum[:, 0:1]), (ones[0:DR, :], gsum[0:DR, 1:2])])
                filled(accumulate(p[:, 1:2], [(ones[:, :], gsum[:, 2:3])]), ("gamma",))

            def do_coarse():
                pe.wait_ge(tok_in, 16 * 9)
                for n, (job, rows) in enumerate(((("f2",), r2), (("f1",), r1))):
                    pe.wait_ge(regrouped, n + 1)
                    p = refill(pe, job)
                    for b in range(NB):
                        mm = pe.transpose(p[0:FC, P * b:P * b + P], rows[:, b, :, :].rearrange("p j f -> p (j f)"),
                                          ident[:, :])
                    filled(mm, job)
                await_drain(pe, ("f2",))
                p = refill(pe, ("o2",))
                filled(accumulate(p[0:64, 0:64], [(w2_s[:, g, :], f2[:, :, g, :]) for g in range(8)]), ("o2",))
                await_drain(pe, ("f1",))
                p = refill(pe, ("o1",))
                filled(accumulate(p[0:64, 0:256], [(w1_s[:, g, :], f1[:, :, g, :]) for g in range(2)]), ("o1",))
                for n, o, level, name in ((16, o2, 2, "2"), (64, o1, 1, "1")):
                    await_drain(pe, ("o" + name,))
                    for v in range(2):
                        p = refill(pe, ("z" + name, v))
                        for i in range(2):
                            mm = pe.matmul(p[0:n, D * i:D * i + D], o[:, 2 * v + i, :], wf_s[:, level, :],
                                           start=True, stop=True)
                        filled(mm, ("z" + name, v))

            def do_fine(v):
                pe.wait_ge(regrouped, 3 + v)
                p = refill(pe, ("f0", v))
                for b in range(NB):
                    mm = pe.transpose(p[0:48, P * b:P * b + P], r0[:, v, b, :, :].rearrange("p j f -> p (j f)"),
                                      ident[:, :])
                filled(mm, ("f0", v))

            def do_own(v):
                await_drain(pe, ("f0", v))
                p = refill(pe, ("o0", v))
                filled(pe.matmul(p[0:64, :], w0_s, f0[:, v, :], start=True, stop=True), ("o0", v))

            def do_blend(b, v):
                for i in range(2):
                    await_drain(pe, ("z2", i))
                    await_drain(pe, ("z1", i))
                p = refill(pe, ("y", b, v))
                pe.matmul(p[:, 0:D], i1_s[:, P * v:P * v + P], z1[:, b, :], start=True, stop=False)
                pe.matmul(p[:, 0:D], i2_s[:, P * v:P * v + P], z2[:, b, :], start=False, stop=False)

            def do_fuse(b, v):
                await_drain(pe, ("o0", v))
                p = ps[use[("y", b, v)][0]]
                filled(pe.matmul(p[:, 0:D], o0[:, v, b, :], wf_s[:, 0, :], start=False, stop=True), ("y", b, v))

            def do_turn(layer, b, *chunk):
                pe.wait_ge(xn_ready[b % 2], NT * turn_number(layer, b))
                for c in chunk or range(2):
                    first, n = ((0, P), (P, DR))[c]
                    p = refill(pe, ("xT", layer, b, c))
                    for t in range(NT):
                        mm = pe.transpose(p[0:n, P * t:P * t + P], xn[:, b % 2, t, first:first + n], ident[:, :])
                    filled(mm, ("xT", layer, b, c))

            def project(kind, layer, b, wh, wl):
                for c in range(2):
                    await_drain(pe, ("xT", layer, b, c))
                for m in range(3):
                    p = refill(pe, (kind, b, m))
                    cols = slice(P * m, P * m + P)
                    filled(accumulate(p[:, 0:T], five_passes(wh[:, :, cols], wl[:, :, cols],
                                                             *tokens(b, slice(0, T)))), (kind, b, m))

            def project_v(kind, b, wh, wl):
                for t in range(NT):
                    p = refill(pe, (kind, b, t))
                    filled(accumulate(p[:, 0:D], flip(five_passes(wh[:, :, 2 * D:3 * D], wl[:, :, 2 * D:3 * D],
                                                                  *tokens(b, slice(P * t, P * t + P))))),
                           (kind, b, t))

            def do_qkv(b):
                pe.wait_ge(wa_ready, 1)
                project("qkv", 0, b, wa_h, wa_l)

            def do_v(b):
                project_v("v", b, wa_h, wa_l)

            def do_v3(b):
                project_v("v3", b, wq_h, wq_l)

            def do_attend(b, g):
                r = b % 2
                if g == 0:
                    for t in range(NT):
                        await_drain(pe, ("v", b, t))
                    pe.wait_ge(stacks_in[r], 16 * 2 * len(PRODUCTS) * (b // 2 + 1))
                if g < NG:
                    for hd in range(HG * g, HG * g + HG):
                        p = refill(pe, ("near", b, hd))
                        for t in range(NT):
                            mm = pe.matmul(p[:, P * t:P * t + P], ks[:, r, hd, P * t:P * t + P],
                                           qs[:, r, hd, P * t:P * t + P], start=True, stop=True)
                        filled(mm, ("near", b, hd))
                        p = refill(pe, ("far", b, hd))
                        pe.matmul(p[:, 0:2 * P], ks[:, r, hd, 0:P], qs[:, r, hd, P:T], start=True, stop=True)
                        filled(pe.matmul(p[:, 2 * P:T], ks[:, r, hd, P:2 * P], qs[:, r, hd, 2 * P:T],
                                         start=True, stop=True), ("far", b, hd))
                if g:
                    job = ("mix", b, g - 1)
                    heads = range(HG * (g - 1), HG * g)
                    for hd in heads:
                        await_drain(pe, ("near", b, hd))
                        await_drain(pe, ("far", b, hd))
                    p = refill(pe, job)
                    spans = [(0, 0, 0, P, 0), (0, 1, 0, 2 * P, P), (1, 0, P, P, P), (1, 1, 2 * P, P, 2 * P),
                             (2, 0, 2 * P, P, 2 * P)]
                    for n, (kt, far, src, width, dst) in enumerate(spans):
                        for i, hd in enumerate(heads):
                            mm = pe.matmul(p[32 * i:32 * i + 32, dst:dst + width], vpad[:, b % 3, kt, hd, :],
                                           att[:, hd % (2 * HG), far, src:src + width],
                                           start=(n == 0), stop=(n == len(spans) - 1), skip_group_check=True)
                    filled(mm, job)

            def do_join(b):
                for g in range(NG):
                    await_drain(pe, ("mix", b, g))
                for t in range(NT):
                    p = refill(pe, ("join", b, t))
                    for g in range(NG):
                        mm = pe.transpose(p[:, P * g:P * g + P], oT[:, g, P * t:P * t + P], ident[:, :])
                    filled(mm, ("join", b, t))

            def do_logits(u):
                b, t = divmod(u, NT)
                if u == 0:
                    pe.wait_ge(phi_ready, 1)
                if t == 0:
                    for c in range(2):
                        await_drain(pe, ("xT", 1, b, c))
                for v in range(2):
                    p = refill(pe, ("logits", u, v))
                    cols = slice(512 * v, 512 * v + 512)
                    filled(accumulate(p[:, :], flip(five_passes(phi_h[:, :, cols], phi_l[:, :, cols],
                                                                *tokens(b, slice(P * t, P * t + P))))),
                           ("logits", u, v))

            def do_slots(u):
                b, t = divmod(u, NT)
                pe.wait_ge(dw_ready, 2 * u + 1)
                weights = [dw[:, u % 2, 16 * v:16 * v + 16, :].rearrange("p e s -> p (e s)") for v in range(2)]
                start, stop = t == 0, t == NT - 1
                for v in range(2):
                    if v:
                        pe.wait_ge(dw_ready, 2 * u + 2)
                    p = refill(pe, ("slots", b, v)) if start else ps[use[("slots", b, v)][0]]
                    mm = pe.matmul(p[:, :], xn[:, b % 2, t, 0:P], weights[v], start=start, stop=stop)
                    if stop:
                        filled(mm, ("slots", b, v))
                p = refill(pe, ("slots", b, 2)) if start else ps[use[("slots", b, 2)][0]]
                for v in range(2):
                    mm = pe.matmul(p[DR * v:DR * v + DR, :], xn[:, b % 2, t, P:D], weights[v],
                                   start=start, stop=stop, skip_group_check=True)
                if stop:
                    filled(mm, ("slots", b, 2))

            def do_shares(u):
                pe.wait_ge(cw_ready, u + 1)
                for v in range(2):
                    p = refill(pe, ("cwT", u, v))
                    for k in range(4):
                        e = EPC * (4 * v + k)
                        mm = pe.transpose(p[:, P * k:P * k + P],
                                          cw[:, u % 2, e:e + EPC, :].rearrange("p e s -> p (e s)"), ident[:, :])
                    filled(mm, ("cwT", u, v))

            def do_experts():
                for k in range(3):
                    await_drain(pe, ("slots", NB - 1, k))
                for v in range(2):
                    await_drain(pe, ("cwT", NB * NT - 1, v))
                pe.wait_ge(ones_row, 1)

                def up(it, j):
                    pe.wait_ge(landed[j % RING], (it + j // RING) * 80 + 80)
                    e = it * RING + j
                    for m in range(NC):
                        o = ps[2 * (j % 2) + m // 3][:, P * (m % 3):P * (m % 3) + P]
                        for c in range(2):
                            rows = P if c == 0 else DR + 1
                            if isinstance(e, int):
                                rhs = slotsT[0:rows, c, e, :, :].rearrange("p b s -> p (b s)")
                            else:
                                rhs = slotsT[0:rows, c, bass.ds(e, 1), :, :].rearrange("p e b s -> p (e b s)")
                            mm = pe.matmul(o, ew1_s[j % RING][0:rows, c, P * m:P * m + P], rhs,
                                           start=(c == 0), stop=(c == 1))
                    mm.then_inc(hid_full, 1)

                def down(it, j):
                    pe.wait_ge(hid_done, it * RING + j + 1)
                    pe.wait_ge(eo_drained, it * RING + j + 1)
                    for m in range(NC):
                        mm = pe.matmul(ps[4 + j % 2][:, 0:D], hT[:, j % 2, P * m:P * m + P], ew2_s[j][:, m, :],
                                       start=(m == 0), stop=(m == NC - 1))
                    mm.then_inc(eo_full, 1)

                up(0, 0)
                with pe.Fori(0, NE // RING - 1) as it:
                    for j in range(RING):
                        up(it, j + 1)
                        down(it, j)
                last = NE // RING - 1
                for j in range(RING):
                    if j + 1 < RING:
                        up(last, j + 1)
                    down(last, j)
                pe.wait_ge(eo_drained, NE + 2)

            def do_combine(b, t):
                p = refill(pe, ("combine", b, t))
                filled(accumulate(p[:, 0:D], [(cwT[:, b, k, P * t:P * t + P], eok[:, k, b, :])
                                              for k in range(KC)]), ("combine", b, t))

            def do_qkv3(b):
                pe.wait_ge(wq_ready, 1)
                project("qkv3", 2, b, wq_h, wq_l)

            def do_score(b):
                r = b % 2
                for m in range(3):
                    await_drain(pe, ("qkv3", b, m))

                def products(kt, first):
                    keys, queries = slice(P * kt, P * kt + P), slice(first, T)
                    return split((q3_h[:, r, 2, keys], q3_l[:, r, 1, keys]),
                                 (q3_h[:, r, 0, queries], q3_l[:, r, 0, queries])) + [
                        (q3_h[:, r, 3, keys], q3_h[:, r, 1, queries]),
                        (q3_l[0:DR, r, 2, keys], q3_h[0:DR, r, 1, queries])]

                p = refill(pe, ("score", b, 0))
                filled(accumulate(p[:, 0:T], products(0, 0)), ("score", b, 0))
                p = refill(pe, ("score", b, 1))
                accumulate(p[:, 0:2 * P], products(1, P))
                filled(accumulate(p[:, 2 * P:T], products(2, 2 * P)), ("score", b, 1))

            def do_read(b):
                r = b % 2
                pe.wait_ge(sc_parts, 2 * (b + 1))
                pe.wait_ge(v3_parts, NT * (b + 1))
                at = [(0, 0), (1, 0), (1, 2 * P)]
                for t in range(NT):
                    p = refill(pe, ("read", b, t))
                    pairs = []
                    for k in range(t + 1):
                        half_, col = at[k][0], at[k][1] + P * (t - k)
                        pairs += split((sc_h[:, r, half_, col:col + P], sc_l[:, r, half_, col:col + P]),
                                       (v3_h[:, b % 3, k, :], v3_l[:, b % 3, k, :]))
                    filled(accumulate(p[:, 0:D], pairs), ("read", b, t))

            def do_hidden(b):
                r = b % 2
                for c in range(2):
                    await_drain(pe, ("xT", 3, b, c))
                for m in range(NC):
                    p = refill(pe, ("hidden", b, m))
                    filled(accumulate(p[:, 0:T], [(tern1[:, c, P * m:P * m + P], x[:, r, :])
                                                  for c, x in ((0, xT_h), (0, xT_l), (1, xT_s))]), ("hidden", b, m))

            def do_down(b):
                for k in range(2):
                    pe.wait_ge(hid_parts[k], NC // 2 * (b + 1))
                for t in range(NT):
                    p = refill(pe, ("down", b, t))
                    filled(accumulate(p[:, 0:D], [(x[:, b % 2, m, P * t:P * t + P], tern2[:, m, :])
                                                  for m in range(NC) for x in (hid_h, hid_l)]), ("down", b, t))

            table = {"phi_norms": do_phi_norms, "phi": do_phi, "gamma": do_gamma, "coarse": do_coarse,
                     "fine": do_fine, "own": do_own, "blend": do_blend, "fuse": do_fuse, "turn": do_turn,
                     "qkv": do_qkv, "attend": do_attend, "join": do_join, "logits": do_logits,
                     "slots": do_slots, "shares": do_shares, "v": do_v, "v3": do_v3, "combine": do_combine,
                     "qkv3": do_qkv3, "score": do_score, "read": do_read, "hidden": do_hidden, "down": do_down}
            for s in before:
                if s[0] in table:
                    table[s[0]](*s[1:])
            do_experts()
            for s in after:
                if s[0] in table:
                    table[s[0]](*s[1:])


def interpolation(n_in, n_out):
    pos = np.clip((np.arange(n_out, dtype=np.float32) + 0.5) * np.float32(n_in / n_out) - 0.5, 0.0, n_in - 1)
    i0 = np.floor(pos).astype(np.int64)
    i1 = np.minimum(i0 + 1, n_in - 1)
    w = (pos - i0).astype(np.float32)
    m = np.zeros((n_in, n_out), np.float32)
    np.add.at(m, (i0, np.arange(n_out)), 1.0 - w)
    np.add.at(m, (i1, np.arange(n_out)), w)
    return m


def causal_tiles():
    k, q = np.arange(P)[:, None], np.arange(P)[None, :]
    m = np.where(q >= k, np.float32(HS) ** -0.5, 0.0).astype(np.float32)
    return np.ascontiguousarray(np.broadcast_to(m[:, None, :], (P, NT, P)))


def decay_tiles():
    diff = (np.arange(T)[None, :] - np.arange(P)[:, None]).astype(np.float32)
    m = np.where(diff >= 0, np.float32(ALPHA) ** diff, 0.0).astype(np.float32)
    return m / np.sqrt(np.float32(D))


def kernel(**inputs):
    import concourse.bacc as bacc
    from concourse.bass_utils import run_bass_kernel_spmd

    a = {k: np.asarray(v) for k, v in inputs.items()}
    x = a["x"]

    def table(p):
        g = 64 // p
        t = x.reshape(NB, 3, g, p, g, p).transpose(2, 4, 0, 3, 5, 1)
        return t.reshape(g * g, NB * p * p * 3)

    idx0 = a["L0_tok_idx0"].reshape(2, P, GP).transpose(1, 0, 2).reshape(P, 32)
    idx1 = a["L0_tok_idx1"].reshape(64, 2, 8).transpose(1, 0, 2).reshape(P, 8)
    idx2 = a["L0_tok_idx2"].reshape(16, 8, 2).transpose(1, 0, 2).reshape(P, 2)
    ba, bq = a["L0_attn_b_attn"], a["L1_attn_b_qkv"]
    order = np.arange(2 * D).reshape(2, HEADS, HS).transpose(0, 2, 1).reshape(-1)
    wa = np.concatenate([a["L0_attn_W_attn"][:, order], a["L0_attn_W_attn"][:, 2 * D:]], axis=1)
    order3 = np.concatenate([np.arange(D), np.arange(D + P, 2 * D), np.arange(D, D + P)])
    wq = np.concatenate([a["L1_attn_W_qkv"][:, order3], a["L1_attn_W_qkv"][:, 2 * D:]], axis=1)

    def doubled(w):
        return np.concatenate([w, w[P:]], axis=0)

    arrays = {
        "x0": table(1), "x1": table(2), "x2": table(4),
        "idx": np.concatenate([idx0, idx1, idx2], axis=1),
        "txt": a["txt"],
        "w0": a["L0_tok_W0"].T, "w1t": a["L0_tok_W1"].T, "w2t": a["L0_tok_W2"].T, "wf": a["L0_tok_Wf"].T,
        "tok_b": np.stack([a["L0_tok_b0"], a["L0_tok_b1"], a["L0_tok_b2"]], axis=1),
        "bf": a["L0_tok_bf"],
        "interp1": interpolation(64, 256), "interp2": interpolation(16, 256),
        "ident": np.eye(P, dtype=np.float32), "causal": causal_tiles(), "decay": decay_tiles(),
        "wa": doubled(wa), "ba_qk": ba[order].reshape(3, P).T, "ba_v": ba[2 * D:],
        "phi": doubled(a["L0_ffn_phi"].reshape(D, NE * NS)), "scale": a["L0_ffn_scale"],
        "ew1": a["L0_ffn_w1"], "eb1": a["L0_ffn_b1"], "ew2": a["L0_ffn_w2"], "eb2": a["L0_ffn_b2"],
        "wq": doubled(wq), "bq_qk": bq[order3].reshape(3, P).T, "bq_v": bq[2 * D:],
        "fw1": doubled(a["L1_ffn_w1"].T), "fb1": a["L1_ffn_b1"].reshape(NC, P).T, "fw2": a["L1_ffn_w2"].T,
        "fb2": a["L1_ffn_b2"],
    }
    arrays = {f"in_{k}": np.ascontiguousarray(v) for k, v in arrays.items()}
    nc = bacc.Bacc("TRN2", target_bir_lowering=False, num_devices=1)
    args = [nc.dram_tensor(k, v.shape, mybir.dt.from_np(v.dtype), kind="ExternalInput").ap()
            for k, v in arrays.items()]
    args.append(nc.dram_tensor("out_tokens", (NB, T, D), F32, kind="ExternalOutput").ap())
    build(nc, *args)
    r = run_bass_kernel_spmd(nc, [arrays], core_ids=[0])
    return r.results[0]["out_tokens"]
```
